# Optimizing a Trainium2 kernel written in Bass

```python
import numpy as np
import jax
import jax.numpy as jnp

def _softmax(x, axis=-1):
    return jax.nn.softmax(x, axis=axis)

def _gelu(x):
    return jax.nn.gelu(x, approximate=True)

def _silu(x):
    return jax.nn.silu(x)

def _sigmoid(x):
    return jax.nn.sigmoid(x)

def _layernorm(x, axis=-1, eps=1e-05):
    m = jnp.mean(x, axis=axis, keepdims=True)
    v = jnp.var(x, axis=axis, keepdims=True)
    return (x - m) / jnp.sqrt(v + eps)

def _scatter_add(tgt, idx, src, axis=0):
    return tgt.at[idx].add(src)

def _segment_sum(src, seg, n):
    return jax.ops.segment_sum(src, seg, n)
kernel_name = 'mk_sandwich_d1_jaxref_r4_8330de'

def setup_inputs(seed: int=0):
    np.random.seed(seed)
    _w = jnp.asarray

    def _L0_attn_setup():
        import jax, jax.numpy as jnp
        import numpy as np
        D_MODEL = 256
        D_STATE = 64
        D_CONV = 4
        EXPAND = 2
        HEADDIM = 64
        D_INNER = EXPAND * D_MODEL
        NHEADS = D_INNER // HEADDIM
        CONV_DIM = D_INNER + 2 * D_STATE
        D_IN_PROJ = 2 * D_INNER + 2 * D_STATE + NHEADS
        BATCH, SEQLEN = (4, 512)
        DT_MIN, DT_MAX = (0.05, 1.0)
        EPS = 1e-05

        def _make_params(key, prefix):
            ks = jax.random.split(key, 5)
            p = {}
            p[prefix + 'in_w'] = jax.random.normal(ks[0], (D_IN_PROJ, D_MODEL), jnp.float32) * D_MODEL ** (-0.5)
            p[prefix + 'conv_w'] = jax.random.normal(ks[1], (CONV_DIM, D_CONV), jnp.float32) * D_CONV ** (-0.5)
            p[prefix + 'conv_b'] = jnp.zeros((CONV_DIM,), jnp.float32)
            u = jax.random.uniform(ks[2], (NHEADS,), jnp.float32)
            dt = jnp.exp(u * (np.log(DT_MAX) - np.log(DT_MIN)) + np.log(DT_MIN))
            p[prefix + 'dt_bias'] = dt + jnp.log(-jnp.expm1(-dt)) + 1.0
            p[prefix + 'A_log'] = jnp.log(jax.random.uniform(ks[3], (NHEADS,), jnp.float32, minval=1.0, maxval=16.0))
            p[prefix + 'Dp'] = jnp.ones((NHEADS,), jnp.float32)
            p[prefix + 'norm_w'] = jnp.ones((D_INNER,), jnp.float32)
            p[prefix + 'out_w'] = jax.random.normal(ks[4], (D_MODEL, D_INNER), jnp.float32) * D_INNER ** (-0.5)
            return p

        def _dconv(x, w, b):
            xt = x.transpose(0, 2, 1)
            out = jax.lax.conv_general_dilated(xt, w[:, None, :], (1,), [(D_CONV - 1, 0)], feature_group_count=CONV_DIM)
            return (out + b[:, None]).transpose(0, 2, 1)

        def _ssd(dt, A, xh, Bm, Cm):
            dA = jnp.exp(dt * A)

            def step(S, inp):
                dA_t, dt_t, x_t, B_t, C_t = inp
                S = S * dA_t[:, :, None, None] + (dt_t[:, :, None] * x_t)[..., None] * B_t[:, None, None, :]
                y = jnp.einsum('bhpn,bn->bhp', S, C_t)
                return (S, y)
            S0 = jnp.zeros((dt.shape[0], NHEADS, HEADDIM, D_STATE), dt.dtype)
            xs = (dA.swapaxes(0, 1), dt.swapaxes(0, 1), xh.swapaxes(0, 1), Bm.swapaxes(0, 1), Cm.swapaxes(0, 1))
            _, ys = jax.lax.scan(step, S0, xs)
            return ys.swapaxes(0, 1)

        def _mamba2(x, in_w, conv_w, conv_b, dt_bias, A_log, Dp, norm_w, out_w):
            Bsz, L, _ = x.shape
            zxbcdt = x @ in_w.T
            z = zxbcdt[..., :D_INNER]
            xBC = zxbcdt[..., D_INNER:D_INNER + CONV_DIM]
            dt = jax.nn.softplus(zxbcdt[..., D_INNER + CONV_DIM:] + dt_bias)
            xBC = jax.nn.silu(_dconv(xBC, conv_w, conv_b))
            xh = xBC[..., :D_INNER].reshape(Bsz, L, NHEADS, HEADDIM)
            Bm = xBC[..., D_INNER:D_INNER + D_STATE]
            Cm = xBC[..., D_INNER + D_STATE:]
            A = -jnp.exp(A_log)
            y = _ssd(dt, A, xh, Bm, Cm) + Dp[None, None, :, None] * xh
            y = y.reshape(Bsz, L, D_INNER) * jax.nn.silu(z)
            y = y * jax.lax.rsqrt(jnp.mean(y * y, -1, keepdims=True) + EPS) * norm_w
            return y @ out_w.T
        key = jax.random.key(seed)
        k1, k2, k3 = jax.random.split(key, 3)
        inp = {'x': jax.random.normal(k1, (BATCH, SEQLEN, D_MODEL), jnp.float32)}
        inp.update(_make_params(k2, 'f_'))
        inp.update(_make_params(k3, 'b_'))
        return inp
    _L0_attn_in = _L0_attn_setup()

    def _L0_ffn_setup():
        import jax, jax.numpy as jnp
        import numpy as np
        B, S, D, H, F, E = (2, 256, 256, 16, 512, 8)
        HD = D // H

        def _ln(x, g, b, eps=1e-05):
            m = x.mean(-1, keepdims=True)
            v = ((x - m) ** 2).mean(-1, keepdims=True)
            return (x - m) / jnp.sqrt(v + eps) * g + b
        key = jax.random.key(seed)
        ks = jax.random.split(key, 12)
        rn = lambda k, shp, s=0.02: jax.random.normal(k, shp, jnp.float32) * s
        return {'src': jax.random.normal(ks[0], (B, S, D), jnp.float32), 'q_w': rn(ks[1], (D, D)), 'k_w': rn(ks[2], (D, D)), 'v_w': rn(ks[3], (D, D)), 'out_w': rn(ks[4], (D, D)), 'gate_w': rn(ks[5], (D, D)), 'gate_b': rn(ks[6], (D,)), 'scale_w': rn(ks[7], (H, HD)), 'n1_g': jnp.ones((D,), jnp.float32), 'n1_b': jnp.zeros((D,), jnp.float32), 'n2_g': jnp.ones((D,), jnp.float32), 'n2_b': jnp.zeros((D,), jnp.float32), 'moe_gate_w': rn(ks[8], (D, E)), 'moe_gate_b': jnp.zeros((E,), jnp.float32), 'w1': rn(ks[9], (E, D, F)), 'b1': jnp.zeros((E, F), jnp.float32), 'ln_g': jnp.ones((E, F), jnp.float32), 'ln_b': jnp.zeros((E, F), jnp.float32), 'w2': rn(ks[10], (E, F, D)), 'b2': jnp.zeros((E, D), jnp.float32), 'res_scale': jnp.ones((E,), jnp.float32)}
    _L0_ffn_in = _L0_ffn_setup()
    _d = {'L0_attn_x': _L0_attn_in['x'], 'L0_attn_f_in_w': _L0_attn_in['f_in_w'], 'L0_attn_f_conv_w': _L0_attn_in['f_conv_w'], 'L0_attn_f_conv_b': _L0_attn_in['f_conv_b'], 'L0_attn_f_dt_bias': _L0_attn_in['f_dt_bias'], 'L0_attn_f_A_log': _L0_attn_in['f_A_log'], 'L0_attn_f_Dp': _L0_attn_in['f_Dp'], 'L0_attn_f_norm_w': _L0_attn_in['f_norm_w'], 'L0_attn_f_out_w': _L0_attn_in['f_out_w'], 'L0_attn_b_in_w': _L0_attn_in['b_in_w'], 'L0_attn_b_conv_w': _L0_attn_in['b_conv_w'], 'L0_attn_b_conv_b': _L0_attn_in['b_conv_b'], 'L0_attn_b_dt_bias': _L0_attn_in['b_dt_bias'], 'L0_attn_b_A_log': _L0_attn_in['b_A_log'], 'L0_attn_b_Dp': _L0_attn_in['b_Dp'], 'L0_attn_b_norm_w': _L0_attn_in['b_norm_w'], 'L0_attn_b_out_w': _L0_attn_in['b_out_w'], 'L0_ffn_q_w': _L0_ffn_in['q_w'], 'L0_ffn_k_w': _L0_ffn_in['k_w'], 'L0_ffn_v_w': _L0_ffn_in['v_w'], 'L0_ffn_out_w': _L0_ffn_in['out_w'], 'L0_ffn_gate_w': _L0_ffn_in['gate_w'], 'L0_ffn_gate_b': _L0_ffn_in['gate_b'], 'L0_ffn_scale_w': _L0_ffn_in['scale_w'], 'L0_ffn_n1_g': _L0_ffn_in['n1_g'], 'L0_ffn_n1_b': _L0_ffn_in['n1_b'], 'L0_ffn_n2_g': _L0_ffn_in['n2_g'], 'L0_ffn_n2_b': _L0_ffn_in['n2_b'], 'L0_ffn_moe_gate_w': _L0_ffn_in['moe_gate_w'], 'L0_ffn_moe_gate_b': _L0_ffn_in['moe_gate_b'], 'L0_ffn_w1': _L0_ffn_in['w1'], 'L0_ffn_b1': _L0_ffn_in['b1'], 'L0_ffn_ln_g': _L0_ffn_in['ln_g'], 'L0_ffn_ln_b': _L0_ffn_in['ln_b'], 'L0_ffn_w2': _L0_ffn_in['w2'], 'L0_ffn_b2': _L0_ffn_in['b2'], 'L0_ffn_res_scale': _L0_ffn_in['res_scale']}
    _x0 = _d['L0_attn_x']
    _d['L0_attn_x'] = jax.random.normal(jax.random.fold_in(jax.random.key(seed), 1), (2, 2048, 256), dtype=_x0.dtype)
    del _x0
    return _d

def reference(L0_attn_x, L0_attn_f_in_w, L0_attn_f_conv_w, L0_attn_f_conv_b, L0_attn_f_dt_bias, L0_attn_f_A_log, L0_attn_f_Dp, L0_attn_f_norm_w, L0_attn_f_out_w, L0_attn_b_in_w, L0_attn_b_conv_w, L0_attn_b_conv_b, L0_attn_b_dt_bias, L0_attn_b_A_log, L0_attn_b_Dp, L0_attn_b_norm_w, L0_attn_b_out_w, L0_ffn_q_w, L0_ffn_k_w, L0_ffn_v_w, L0_ffn_out_w, L0_ffn_gate_w, L0_ffn_gate_b, L0_ffn_scale_w, L0_ffn_n1_g, L0_ffn_n1_b, L0_ffn_n2_g, L0_ffn_n2_b, L0_ffn_moe_gate_w, L0_ffn_moe_gate_b, L0_ffn_w1, L0_ffn_b1, L0_ffn_ln_g, L0_ffn_ln_b, L0_ffn_w2, L0_ffn_b2, L0_ffn_res_scale):

    def _L0_attn_ref(x, f_in_w, f_conv_w, f_conv_b, f_dt_bias, f_A_log, f_Dp, f_norm_w, f_out_w, b_in_w, b_conv_w, b_conv_b, b_dt_bias, b_A_log, b_Dp, b_norm_w, b_out_w):
        import jax, jax.numpy as jnp
        import numpy as np
        D_MODEL = 256
        D_STATE = 64
        D_CONV = 4
        EXPAND = 2
        HEADDIM = 64
        D_INNER = EXPAND * D_MODEL
        NHEADS = D_INNER // HEADDIM
        CONV_DIM = D_INNER + 2 * D_STATE
        D_IN_PROJ = 2 * D_INNER + 2 * D_STATE + NHEADS
        BATCH, SEQLEN = (4, 512)
        DT_MIN, DT_MAX = (0.05, 1.0)
        EPS = 1e-05

        def _make_params(key, prefix):
            ks = jax.random.split(key, 5)
            p = {}
            p[prefix + 'in_w'] = jax.random.normal(ks[0], (D_IN_PROJ, D_MODEL), jnp.float32) * D_MODEL ** (-0.5)
            p[prefix + 'conv_w'] = jax.random.normal(ks[1], (CONV_DIM, D_CONV), jnp.float32) * D_CONV ** (-0.5)
            p[prefix + 'conv_b'] = jnp.zeros((CONV_DIM,), jnp.float32)
            u = jax.random.uniform(ks[2], (NHEADS,), jnp.float32)
            dt = jnp.exp(u * (np.log(DT_MAX) - np.log(DT_MIN)) + np.log(DT_MIN))
            p[prefix + 'dt_bias'] = dt + jnp.log(-jnp.expm1(-dt)) + 1.0
            p[prefix + 'A_log'] = jnp.log(jax.random.uniform(ks[3], (NHEADS,), jnp.float32, minval=1.0, maxval=16.0))
            p[prefix + 'Dp'] = jnp.ones((NHEADS,), jnp.float32)
            p[prefix + 'norm_w'] = jnp.ones((D_INNER,), jnp.float32)
            p[prefix + 'out_w'] = jax.random.normal(ks[4], (D_MODEL, D_INNER), jnp.float32) * D_INNER ** (-0.5)
            return p

        def _dconv(x, w, b):
            xt = x.transpose(0, 2, 1)
            out = jax.lax.conv_general_dilated(xt, w[:, None, :], (1,), [(D_CONV - 1, 0)], feature_group_count=CONV_DIM)
            return (out + b[:, None]).transpose(0, 2, 1)

        def _ssd(dt, A, xh, Bm, Cm):
            dA = jnp.exp(dt * A)

            def step(S, inp):
                dA_t, dt_t, x_t, B_t, C_t = inp
                S = S * dA_t[:, :, None, None] + (dt_t[:, :, None] * x_t)[..., None] * B_t[:, None, None, :]
                y = jnp.einsum('bhpn,bn->bhp', S, C_t)
                return (S, y)
            S0 = jnp.zeros((dt.shape[0], NHEADS, HEADDIM, D_STATE), dt.dtype)
            xs = (dA.swapaxes(0, 1), dt.swapaxes(0, 1), xh.swapaxes(0, 1), Bm.swapaxes(0, 1), Cm.swapaxes(0, 1))
            _, ys = jax.lax.scan(step, S0, xs)
            return ys.swapaxes(0, 1)

        def _mamba2(x, in_w, conv_w, conv_b, dt_bias, A_log, Dp, norm_w, out_w):
            Bsz, L, _ = x.shape
            zxbcdt = x @ in_w.T
            z = zxbcdt[..., :D_INNER]
            xBC = zxbcdt[..., D_INNER:D_INNER + CONV_DIM]
            dt = jax.nn.softplus(zxbcdt[..., D_INNER + CONV_DIM:] + dt_bias)
            xBC = jax.nn.silu(_dconv(xBC, conv_w, conv_b))
            xh = xBC[..., :D_INNER].reshape(Bsz, L, NHEADS, HEADDIM)
            Bm = xBC[..., D_INNER:D_INNER + D_STATE]
            Cm = xBC[..., D_INNER + D_STATE:]
            A = -jnp.exp(A_log)
            y = _ssd(dt, A, xh, Bm, Cm) + Dp[None, None, :, None] * xh
            y = y.reshape(Bsz, L, D_INNER) * jax.nn.silu(z)
            y = y * jax.lax.rsqrt(jnp.mean(y * y, -1, keepdims=True) + EPS) * norm_w
            return y @ out_w.T
        out_fwd = _mamba2(x, f_in_w, f_conv_w, f_conv_b, f_dt_bias, f_A_log, f_Dp, f_norm_w, f_out_w)
        x_rev = jnp.flip(x, 1)
        out_bwd = _mamba2(x_rev, b_in_w, b_conv_w, b_conv_b, b_dt_bias, b_A_log, b_Dp, b_norm_w, b_out_w)
        return out_fwd + jnp.flip(out_bwd, 1)

    def _L0_ffn_ref(src, q_w, k_w, v_w, out_w, gate_w, gate_b, scale_w, n1_g, n1_b, n2_g, n2_b, moe_gate_w, moe_gate_b, w1, b1, ln_g, ln_b, w2, b2, res_scale):
        import jax, jax.numpy as jnp
        import numpy as np
        B, S, D, H, F, E = (2, 256, 256, 16, 512, 8)
        HD = D // H

        def _ln(x, g, b, eps=1e-05):
            m = x.mean(-1, keepdims=True)
            v = ((x - m) ** 2).mean(-1, keepdims=True)
            return (x - m) / jnp.sqrt(v + eps) * g + b
        b, s, d = src.shape
        h = scale_w.shape[0]
        hd = d // h
        q = (src @ q_w).reshape(b, s, h, hd).transpose(0, 2, 1, 3)
        k = (src @ k_w).reshape(b, s, h, hd).transpose(0, 2, 1, 3)
        v = (src @ v_w).reshape(b, s, h, hd).transpose(0, 2, 1, 3)
        scores = jnp.einsum('bhqd,bhkd->bhqk', q, k) / np.float32(np.sqrt(hd))
        scale = jax.nn.sigmoid(jnp.einsum('bhsd,hd->bhs', q, scale_w)) * 2.0
        scores = scores * scale[..., None]
        aw = jax.nn.softmax(scores, axis=-1)
        out = jnp.einsum('bhqk,bhkd->bhqd', aw, v).transpose(0, 2, 1, 3).reshape(b, s, d)
        gate = jax.nn.sigmoid(out @ gate_w + gate_b)
        attn = out * gate @ out_w
        x = _ln(src + attn, n1_g, n1_b)
        xr = x.reshape(-1, d)
        n = xr.shape[0]
        logits = xr @ moe_gate_w + moe_gate_b
        top_v, top_i = jax.lax.top_k(logits, 2)
        wts = jax.nn.softmax(top_v, axis=-1)
        chosen = jnp.max(top_i, axis=-1)

        def expert(W1, B1, G, Bt, W2, B2, rsc):
            hh = xr @ W1 + B1
            hh = jax.nn.gelu(_ln(hh, G, Bt), approximate=False)
            return (hh @ W2 + B2) * rsc + xr
        outs = jax.vmap(expert)(w1, b1, ln_g, ln_b, w2, b2, res_scale)
        sel = jnp.take_along_axis(outs.transpose(1, 0, 2), chosen[:, None, None], axis=1)[:, 0]
        moe = sel * jnp.sum(wts, axis=-1, keepdims=True)
        return _ln(x + moe.reshape(b, s, d), n2_g, n2_b)
    x = L0_attn_x
    x = x + _layernorm(_L0_attn_ref(_layernorm(x, axis=-1), L0_attn_f_in_w, L0_attn_f_conv_w, L0_attn_f_conv_b, L0_attn_f_dt_bias, L0_attn_f_A_log, L0_attn_f_Dp, L0_attn_f_norm_w, L0_attn_f_out_w, L0_attn_b_in_w, L0_attn_b_conv_w, L0_attn_b_conv_b, L0_attn_b_dt_bias, L0_attn_b_A_log, L0_attn_b_Dp, L0_attn_b_norm_w, L0_attn_b_out_w), axis=-1)
    x = x + _layernorm(_L0_ffn_ref(_layernorm(x, axis=-1), L0_ffn_q_w, L0_ffn_k_w, L0_ffn_v_w, L0_ffn_out_w, L0_ffn_gate_w, L0_ffn_gate_b, L0_ffn_scale_w, L0_ffn_n1_g, L0_ffn_n1_b, L0_ffn_n2_g, L0_ffn_n2_b, L0_ffn_moe_gate_w, L0_ffn_moe_gate_b, L0_ffn_w1, L0_ffn_b1, L0_ffn_ln_g, L0_ffn_ln_b, L0_ffn_w2, L0_ffn_b2, L0_ffn_res_scale), axis=-1)
    return x

_drawn_inputs = setup_inputs


def setup_inputs(seed=0):
    import zlib

    import numpy as np

    out = dict(_drawn_inputs(seed))
    spreads = {'L0_attn_f_conv_b': (0.0, 0.1),
     'L0_attn_f_Dp': (1.0, 0.2),
     'L0_attn_f_norm_w': (1.0, 0.2),
     'L0_attn_b_conv_b': (0.0, 0.1),
     'L0_attn_b_Dp': (1.0, 0.2),
     'L0_attn_b_norm_w': (1.0, 0.2),
     'L0_ffn_n1_g': (1.0, 0.2),
     'L0_ffn_n1_b': (0.0, 0.1),
     'L0_ffn_n2_g': (1.0, 0.2),
     'L0_ffn_n2_b': (0.0, 0.1),
     'L0_ffn_moe_gate_b': (0.0, 0.1),
     'L0_ffn_b1': (0.0, 0.38),
     'L0_ffn_ln_g': (1.0, 0.6),
     'L0_ffn_ln_b': (0.0, 0.8),
     'L0_ffn_b2': (0.0, 0.34),
     'L0_ffn_res_scale': (1.0, 0.6)}
    factors = {'L0_ffn_q_w': 8.0,
     'L0_ffn_k_w': 8.0,
     'L0_ffn_v_w': 8.0,
     'L0_ffn_out_w': 8.0,
     'L0_ffn_gate_w': 8.0,
     'L0_ffn_gate_b': 8.0,
     'L0_ffn_scale_w': 8.0}
    for name, (base, spread) in spreads.items():
        noise = np.random.default_rng([zlib.crc32(name.encode()), seed]).standard_normal(out[name].shape)
        drawn = base * np.exp(spread * noise) if base else spread * noise
        out[name] = jnp.asarray(drawn.astype(out[name].dtype))
    for name, factor in factors.items():
        out[name] = (out[name] * factor).astype(out[name].dtype)
    return out
```

```python
from contextlib import ExitStack

import concourse.bass as bass
from concourse import mybir
from concourse.alu_op_type import AluOpType as ALU

F32 = mybir.dt.float32
BF16 = mybir.dt.bfloat16
U32 = mybir.dt.uint32
ACT = mybir.ActivationFunctionType
AX_X = mybir.AxisListType.X

P = 128
BATCH, SEQ, D = 2, 2048, 256
TOK = BATCH * SEQ
NCH = TOK // P
KD = D // P
BLK = 512
CPB = BLK // P
NBLK = TOK // BLK
BPS = SEQ // BLK
DI, NST, NH, HP = 512, 64, 8, 64
CI = DI // P
CX = (DI + 2 * NST) // P
TAPS = 4
EPS = 1e-5
AH, HD = 16, 16
NE, FF = 8, 512
FT = FF // P


class Step:

    def __init__(self, lane, emit, after):
        self.lane, self.emit, self.after = lane, emit, after
        self.signals = False
        self.sem = self.value = None
        for s in after:
            s.signals = True


class Lane:

    def __init__(self, engine, sem):
        self.engine, self.sem, self.count = engine, sem, 0
        self.queue, self.seen = [], {}

    def do(self, instruction, *operands, after=(), **options):
        s = Step(self, lambda: instruction(*operands, **options), [a for a in after if a is not None])
        self.queue.append(s)
        return s

    def number(self):
        for s in self.queue:
            if s.sem is None and s.signals:
                self.count += 1
                s.sem, s.value = self.sem, self.count

    def emit(self):
        for s in self.queue:
            for a in s.after:
                if self.seen.get(a.sem.name, 0) < a.value:
                    self.engine.wait_ge(a.sem, a.value)
                    self.seen[a.sem.name] = a.value
            made = s.emit()
            if s.sem is self.sem:
                made.then_inc(self.sem, 1)
            elif s.sem is not None:
                made.then_inc(s.sem, 16)
        self.queue = []


class Lanes:

    def __init__(self, nc, ctx):
        self.nc, self.ctx = nc, ctx
        self.pe = Lane(nc.tensor, ctx.enter_context(nc.semaphore("pe_done")))
        self.act = Lane(nc.scalar, ctx.enter_context(nc.semaphore("act_done")))
        self.dve = Lane(nc.vector, ctx.enter_context(nc.semaphore("dve_done")))
        self.pool = Lane(nc.gpsimd, ctx.enter_context(nc.semaphore("pool_done")))
        self.sp = Lane(nc.sync, ctx.enter_context(nc.semaphore("sp_done")))
        self.arrivals = {}

    def dma(self, lane, name, out, in_, after=(), start=None, **options):
        if name not in self.arrivals:
            self.arrivals[name] = [self.ctx.enter_context(self.nc.semaphore(name)), 0]
        entry = self.arrivals[name]
        entry[1] += 16
        third = (options.pop("third"),) if "third" in options else ()
        s = lane.do(start or lane.engine.dma_start, out, in_, *third, after=after, **options)
        s.sem, s.value = entry[0], entry[1]
        return s

    def run(self):
        lanes = (self.pe, self.act, self.dve, self.pool, self.sp)
        for lane in lanes:
            lane.number()
        with self.nc.Block() as block:
            @block.tensor
            def _(_e):
                self.pe.emit()

            @block.scalar
            def _(_e):
                self.act.emit()

            @block.vector
            def _(_e):
                self.dve.emit()

            @block.gpsimd
            def _(_e):
                self.pool.emit()

            @block.sync
            def _(_e):
                self.sp.emit()


def heads(ap, n, w):
    return ap.rearrange("p (h q) -> p h q", h=n, q=w)


def over_last(ap, w):
    return ap.unsqueeze(2).to_broadcast([ap.shape[0], ap.shape[1], w])


def over_mid(ap, n):
    return ap.unsqueeze(1).to_broadcast([ap.shape[0], n, ap.shape[1]])


def stats_of(L, src, stat, mv, std, rstd, n, after):
    made = []
    for i in range(n):
        st = L.dve.do(L.nc.vector.bn_stats, stat[:, i, :], src(i), after=after(i))
        made.append(st)
    for i in range(n):
        last = L.dve.do(L.nc.vector.bn_aggr, mv[:, i, :], stat[:, i, :], after=[made[i]])
    biased = L.dve.do(L.nc.vector.tensor_scalar_add, std[:, 0:n], mv[:, 0:n, 1], EPS, after=[last])
    root = L.act.do(L.nc.scalar.activation, std[:, 0:n], std[:, 0:n], ACT.Sqrt, after=[biased])
    return L.dve.do(L.nc.vector.reciprocal, rstd[:, 0:n], std[:, 0:n], after=[root])


def norm_and_steps(nc, L, K, io, xnT, sp):
    with ExitStack() as ctx:
        def sb(name, shape, dt=F32):
            return ctx.enter_context(nc.sbuf_tensor(name, shape, dt))

        def ps(name, shape, dt=F32):
            return ctx.enter_context(nc.psum_tensor(name, shape, dt))

        x = sb("x_in", [P, NCH, D])
        xn = sb("x_normed", [P, 2, CPB, D])
        stat = sb("ln_stat", [P, NCH, 6])
        mv = sb("ln_mv", [P, NCH, 2])
        std = sb("ln_std", [P, NCH])
        rstd = sb("ln_rstd", [P, NCH])
        wdt = sb("w_dt", [P, KD, 2 * NH])
        dt_bias = sb("dt_bias", [P, 2 * NH])
        a_log = sb("a_log", [P, 2 * NH])
        neg_a = sb("neg_a", [P, 2 * NH])
        raw = sb("dt_raw", [P, 2, NCH * NH])
        tmp = sb("dt_tmp", [P, 2, NCH * NH])
        lg = sb("dt_log", [P, 2, NCH * NH])
        da = sb("dt_a", [P, 2, NCH * NH])
        cum = sb("cum", [P, 2, NCH * NH])
        rest = sb("cum_rest", [P, 2, NCH * NH])
        parts = sb("cum_parts", [P, 2 * NCH, 3, NH], BF16)
        tbank = [ps(f"x_t{i}", [P, BLK]) for i in range(3)]
        dtp = ps("dt_psum", [P, NCH, 2, NH])
        flip = ps("flip_psum", [P, NCH * NH])
        cump = ps("cum_psum", [P, 2, NCH * NH])
        totp = ps("tot_psum", [P, 2, NCH * NH])
        ctp = ps("cum_t_psum", [3 * NH, 8, P], BF16)

        xv = io["x"].rearrange("b (c p) d -> p (b c) d", p=P)
        loads = [L.dma(L.sp, f"x_load{b}", x[:, b * CPB:(b + 1) * CPB, :], xv[:, b * CPB:(b + 1) * CPB, :])
                 for b in range(NBLK)]
        small = [L.dma(L.act, "dt_load", wdt[:, :, :], io["w_dt"]),
                 L.dma(L.act, "dt_load", dt_bias[:, :], io["dt_bias"]),
                 L.dma(L.act, "dt_load", a_log[:, :], io["a_log"])][-1]

        evac = [None] * 3
        normed_read = [None, None]
        dt_last = None
        n = 0
        for b in range(NBLK):
            c0 = b * CPB
            r = stats_of(L, lambda i: x[:, c0 + i, :], stat[:, c0:c0 + CPB, :], mv[:, c0:c0 + CPB, :],
                         std[:, c0:c0 + CPB], rstd[:, c0:c0 + CPB], CPB, lambda i: [loads[b]])
            for i in range(CPB):
                nx = L.dve.do(nc.vector.tensor_scalar, xn[:, b % 2, i, :], x[:, c0 + i, :],
                              mv[:, c0 + i, 0:1], rstd[:, c0 + i:c0 + i + 1], ALU.subtract, ALU.mult,
                              after=[r, normed_read[b % 2]])
            for k in range(KD):
                bank = n % 3
                for i in range(CPB):
                    t = L.pe.do(nc.tensor.transpose, tbank[bank][:, i * P:(i + 1) * P],
                                xn[:, b % 2, i, k * P:(k + 1) * P], K["ident"], after=[nx, evac[bank]])
                normed_read[b % 2] = t
                if n % 2:
                    e = L.act.do(nc.scalar.copy, xnT[:, k, b * BLK:(b + 1) * BLK], tbank[bank][:, :], after=[t])
                else:
                    e = L.dve.do(nc.vector.tensor_copy, xnT[:, k, b * BLK:(b + 1) * BLK], tbank[bank][:, :],
                                 after=[t])
                evac[bank] = e
                if k == 0:
                    first = e
                n += 1
            for i in range(CPB):
                g = c0 + i
                for k in range(KD):
                    dt_last = L.pe.do(nc.tensor.matmul, dtp[:, g, :, :].rearrange("p a h -> p (a h)"),
                                      xnT[:, k, g * P:(g + 1) * P], wdt[:, k, :], start=(k == 0),
                                      stop=(k == KD - 1), after=[first, e, small])
        bias = [dt_bias[:, d * NH:(d + 1) * NH].unsqueeze(1).to_broadcast([P, NCH, NH]) for d in range(2)]
        g3 = lambda t, d: t[:, d, :].rearrange("p (g h) -> p g h", h=NH)
        f0 = L.dve.do(nc.vector.tensor_tensor, g3(raw, 0), dtp[:, :, 0, :], bias[0], ALU.add, after=[dt_last, small])
        f1 = L.dve.do(nc.vector.tensor_tensor, g3(tmp, 1), dtp[:, :, 1, :], bias[1], ALU.add, after=[dt_last])
        fl = L.pe.do(nc.tensor.matmul, flip[:, :], K["flip"], tmp[:, 1, :], start=True, stop=True, after=[f1])
        f2 = L.dve.do(nc.vector.tensor_copy, raw[:, 1, :], flip[:, :], after=[fl])
        a0 = L.dve.do(nc.vector.tensor_scalar_mul, tmp[:, :, :], raw[:, :, :], -1.0, after=[f0, f2])
        a1 = L.dve.do(nc.vector.tensor_tensor, tmp[:, :, :], tmp[:, :, :], raw[:, :, :], ALU.min, after=[a0])
        a2 = L.act.do(nc.scalar.activation, tmp[:, :, :], tmp[:, :, :], ACT.Exp, after=[a1])
        a3 = L.dve.do(nc.vector.tensor_scalar_add, tmp[:, :, :], tmp[:, :, :], 1.0, after=[a2])
        a4 = L.act.do(nc.scalar.activation, lg[:, :, :], tmp[:, :, :], ACT.Ln, after=[a3])
        na = L.act.do(nc.scalar.activation, neg_a[:, :], a_log[:, :], ACT.Exp, after=[small])
        na = L.dve.do(nc.vector.tensor_scalar_mul, neg_a[:, :], neg_a[:, :], -1.0, after=[na])
        a5 = L.dve.do(nc.vector.scalar_tensor_tensor, sp["dt"][:, :, :], raw[:, :, :], 0.0, lg[:, :, :],
                      ALU.max, ALU.add, after=[a4])
        for d in range(2):
            va = L.dve.do(nc.vector.tensor_tensor, g3(da, d), g3(sp["dt"], d),
                          neg_a[:, d * NH:(d + 1) * NH].unsqueeze(1).to_broadcast([P, NCH, NH]), ALU.mult,
                          after=[a5, na])
        flat = lambda t: t[:, :, :].rearrange("p a b -> p (a b)")
        c = L.pe.do(nc.tensor.matmul, flat(cump), K["upto"], flat(da), start=True, stop=True, after=[va])
        t = L.pe.do(nc.tensor.matmul, flat(totp), K["ones"], flat(da), start=True, stop=True, after=[va])
        v0 = L.dve.do(nc.vector.tensor_copy, cum[:, :, :], cump[:, :, :], after=[c])
        v1 = L.dve.do(nc.vector.tensor_tensor, rest[:, :, :], totp[:, :, :], cum[:, :, :], ALU.subtract, after=[v0, t])
        L.act.do(nc.scalar.activation, sp["ecum"][:, :, :], cum[:, :, :], ACT.Exp, after=[v0])
        e2 = L.act.do(nc.scalar.activation, sp["eto"][:, :, :], rest[:, :, :], ACT.Exp, after=[v1])
        L.act.do(nc.scalar.activation, sp["etot"][:, :, :], totp[:, :, :], ACT.Exp, after=[v1])
        pt = lambda i: parts[:, :, i, :]
        cg = flat(cum).rearrange("p (g h) -> p g h", h=NH)
        rg = flat(rest).rearrange("p (g h) -> p g h", h=NH)
        s0 = L.dve.do(nc.vector.tensor_copy, pt(0), cg, after=[v0])
        s1 = L.dve.do(nc.vector.tensor_tensor, rg, cg, pt(0), ALU.subtract, after=[s0, e2])
        s2 = L.dve.do(nc.vector.tensor_copy, pt(1), rg, after=[s1])
        s3 = L.dve.do(nc.vector.tensor_tensor, pt(2), rg, pt(1), ALU.subtract, after=[s2])
        prev = None
        for i in range(2 * NCH):
            q = L.pe.do(nc.tensor.transpose, ctp[:, i % 8, :], parts[:, i, :, :].rearrange("p a h -> p (a h)"),
                        K["identb"], after=[s3, prev])
            if i % 8 == 7:
                prev = L.dve.do(nc.vector.tensor_copy, sp["cumT"][:, (i - 7) * P:(i + 1) * P],
                                ctp[:, :, :].rearrange("k a b -> k (a b)"), after=[q])
        L.run()


def mamba(nc, L, K, io, xnT, sp, acc):
    with ExitStack() as ctx:
        def sb(name, shape, dt=F32):
            return ctx.enter_context(nc.sbuf_tensor(name, shape, dt))

        def ps(name, shape, dt=F32):
            return ctx.enter_context(nc.psum_tensor(name, shape, dt))

        w_in = sb("w_in", [P, KD, 2 * DI + 2 * NST])
        w_out = [sb(f"w_out{d}", [P, CI, D]) for d in range(2)]
        chan = [sb(f"chan{d}", [P, CX * (TAPS + 1) + 2 * CI]) for d in range(2)]
        pre = sb("conv_in", [P, CX, TAPS - 1 + BLK])
        xs = sb("x_conv", [P, 2, CI, BLK])
        bc = sb("bc_conv", [P, BLK])
        BT = sb("b_t", [NST, 2, BLK])
        CT = sb("c_t", [NST, 2, BLK])
        zs = sb("z_gate", [P, 2, CI, BLK])
        ypre = sb("y_pre", [P, CI, BLK])
        yg = sb("y_gated", [P, CI, BLK])
        M = sb("decay", [P, 2, NH * P])
        btok = sb("b_tok", [P, 2, NST])
        xdt = sb("x_dt", [P, 2, DI])
        xw = sb("x_w", [P, 2, DI])
        us = sb("u_scaled", [P, DI])
        S = sb("state", [NST, DI])
        rms = sb("rms", [P, 2, CPB])
        rrms = sb("rrms", [P, 2, CPB])
        rot = [ps(f"rot{i}", [P, BLK]) for i in range(2)]
        Lp = ps("decay_psum", [P, NH * P])
        gb = ps("gb_psum", [P, BLK])
        xt = ps("xt_psum", [P, BLK])
        up = ps("u_psum", [P, BLK])
        yp = ps("y_psum", [P, BLK])

        wl = []
        for d in range(2):
            L.dma(L.sp, f"mamba_load{d}", w_out[d][:, :, :], io[f"w_out{d}"])
            wl.append(L.dma(L.sp, f"mamba_load{d}", chan[d][:, :], io[f"chan{d}"]))
        w_in_loaded = [L.dma(L.act, "w_in_load0", w_in[:, :, :], io["w_in0"]), None]
        tap = lambda d, c, i: chan[d][:, c * TAPS + i:c * TAPS + i + 1]
        cbias = lambda d, c: chan[d][:, CX * TAPS + c:CX * TAPS + c + 1]
        o1 = CX * (TAPS + 1)
        dp = lambda d, c: chan[d][:, o1 + c:o1 + c + 1]
        nw = lambda d, c: chan[d][:, o1 + CI + c:o1 + CI + c + 1]
        wscaled = []
        for d in range(2):
            for c in range(CI):
                s = L.dve.do(nc.vector.tensor_scalar_mul, w_out[d][:, c, :], w_out[d][:, c, :], nw(d, c),
                             after=[wl[d]])
            wscaled.append(s)

        blocks = [(d, b, j) for d in range(2) for b in range(BATCH) for j in range(BPS)]
        NB = len(blocks)

        def phys(n):
            d, b, j = blocks[n]
            return b * BPS + (j if d == 0 else BPS - 1 - j)

        def chunk_of(n, j):
            return phys(n) * CPB + (j if blocks[n][0] == 0 else CPB - 1 - j)

        def span(a, width, backward):
            if not backward:
                return slice(a, a + width)
            return slice(a + width - 1, a - 1 if a else None, -1)

        rot_free = [None, None]
        rot_n = [0]

        def next_rot():
            i = rot_n[0] % 2
            rot_n[0] += 1
            return i

        st = {}

        def project(n, tiles):
            d = blocks[n][0]
            sl = n % 2
            a = phys(n) * BLK
            if n == NB // 2 and w_in_loaded[1] is None:
                w_in_loaded[1] = L.dma(L.sp, "w_in_load1", w_in[:, :, :], io["w_in1"], after=[st["proj", n - 1]])
            for c in tiles:
                i = next_rot()
                col = DI + c * P if c < CX else (c - CX) * P
                for k in range(KD):
                    m = L.pe.do(nc.tensor.matmul, rot[i][:, :], w_in[:, k, col:col + P],
                                xnT[:, k, span(a, BLK, d)], start=(k == 0), stop=(k == KD - 1),
                                after=[rot_free[i], w_in_loaded[d]])
                st["proj", n] = m
                if c < CX:
                    e = L.act.do(nc.scalar.copy, pre[:, c, TAPS - 1:], rot[i][:, :],
                                 after=[m, st.get(("halo", n, c))])
                    rot_free[i] = e
                    out = xs[:, sl, c, :] if c < CI else bc[:, :]
                    guard = [st.get(("y", n - 2, CPB - 1)), st.get(("xt", n - 2, CPB - 1)), st.get(("silu", n - 1))]
                    v = L.dve.do(nc.vector.tensor_scalar, out, pre[:, c, TAPS - 1:], tap(d, c, TAPS - 1),
                                 cbias(d, c), ALU.mult, ALU.add, after=[e, wl[d], *guard])
                    for t in range(TAPS - 2, -1, -1):
                        v = L.dve.do(nc.vector.scalar_tensor_tensor, out, pre[:, c, t:t + BLK], tap(d, c, t),
                                     out, ALU.mult, ALU.add, after=[v])
                    if n + 1 < NB:
                        if blocks[n + 1][2]:
                            h = L.dve.do(nc.vector.tensor_copy, pre[:, c, 0:TAPS - 1], pre[:, c, BLK:], after=[v])
                        else:
                            h = L.dve.do(nc.vector.memset, pre[:, c, 0:TAPS - 1], 0.0, after=[v])
                        st["halo", n + 1, c] = h
                    st["conv", n] = v
                else:
                    e = L.act.do(nc.scalar.copy, zs[:, sl, c - CX, :], rot[i][:, :],
                                 after=[m, st.get(("gate", n - 2))])
                    rot_free[i] = e
                    st["z", n] = e

        def silu(n):
            sl = n % 2
            L.act.do(nc.scalar.activation, BT[:, sl, :], bc[0:NST, :], ACT.Silu,
                     after=[st["conv", n], st.get(("g", n - 2, CPB - 1))])
            s = L.act.do(nc.scalar.activation, CT[:, sl, :], bc[NST:P, :], ACT.Silu,
                         after=[st["conv", n], st.get(("u", n - 2, CPB - 1))])
            L.act.do(nc.scalar.activation, xs[:, sl, :, :], xs[:, sl, :, :], ACT.Silu)
            st["silu", n] = L.act.do(nc.scalar.activation, zs[:, sl, :, :], zs[:, sl, :, :], ACT.Silu,
                                     after=[st["z", n]])

        q = [0]

        def inside(n, j):
            d = blocks[n][0]
            sl, ch = n % 2, slice(j * P, (j + 1) * P)
            g = d * NCH + chunk_of(n, j)
            two = (n * CPB + j) % 2
            ct = sp["cumT"][:, g * P:(g + 1) * P]
            before = (n, j - 1) if j else (n - 1, CPB - 1)
            before2 = (n, j - 2) if j >= 2 else (n - 1, CPB - 2 + j)
            lw = [st.get(("exp", *before))]
            for half in range(2):
                bank = Lp[:, half * BLK:(half + 1) * BLK]
                L.pe.do(nc.tensor.matmul, bank, ct, K["negsel"][:, half * BLK:(half + 1) * BLK], start=True,
                        stop=False, skip_group_check=True, after=lw)
                L.pe.do(nc.tensor.matmul, bank, K["identb"], K["mask"], start=False, stop=False,
                        skip_group_check=True)
                for h in range(CPB):
                    hh = half * CPB + h
                    m = L.pe.do(nc.tensor.matmul, bank[:, h * P:(h + 1) * P], K["sel"][:, hh * P:(hh + 1) * P], ct,
                                start=False, stop=True, skip_group_check=True)
            e = L.act.do(nc.scalar.activation, M[:, two, :], Lp[:, :], ACT.Exp,
                         after=[m, st.get(("intra", *before2))])
            st["exp", n, j] = e
            free = [st.get(("m", *before)), st.get(("btok", *before))]
            L.pe.do(nc.tensor.matmul, gb[:, 0:P], BT[:, sl, ch], CT[:, sl, ch], start=True, stop=True,
                    after=[st["silu", n], *free])
            gm = L.pe.do(nc.tensor.transpose, gb[:, P:P + NST], BT[:, sl, ch], K["ident"][0:NST, 0:NST])
            st["g", n, j] = gm
            for c in range(CI):
                x = L.pe.do(nc.tensor.transpose, xt[:, c * P:(c + 1) * P], xs[:, sl, c, ch], K["ident"],
                            after=[st.get(("xdt", *before))])
            st["xt", n, j] = x
            mm = M[:, two, :]
            st["xdt", n, j] = L.dve.do(nc.vector.tensor_tensor, heads(xdt[:, two, :], NH, HP),
                                       heads(xt[:, :], NH, HP), over_last(sp_at("dt", d, n, j), HP), ALU.mult,
                                       after=[x, st.get(("intra", *before2)), st.get(("xw", *before2))])
            st["m", n, j] = L.dve.do(nc.vector.tensor_tensor, heads(mm, NH, P), heads(mm, NH, P),
                                     over_mid(gb[:, 0:P], NH), ALU.mult, after=[gm, e])
            st["btok", n, j] = L.dve.do(nc.vector.tensor_copy, btok[:, two, :], gb[:, P:P + NST],
                                        after=[st.get(("snew", *before2))])
            st["xw", n, j] = L.pool.do(nc.gpsimd.tensor_tensor, heads(xw[:, two, :], NH, HP),
                                       heads(xdt[:, two, :], NH, HP), over_last(sp_at("eto", d, n, j), HP), ALU.mult,
                                       after=[st["xdt", n, j], st.get(("snew", *before2))])

        def sp_at(what, d, n, j, rows=P):
            g = chunk_of(n, j)
            return sp[what][0:rows, d, g * NH:(g + 1) * NH]

        def across(n, j):
            d, _, jb = blocks[n]
            first = jb == 0 and j == 0
            sl, ch = n % 2, slice(j * P, (j + 1) * P)
            two = (n * CPB + j) % 2
            before = (n, j - 1) if j else (n - 1, CPB - 1)
            u_free = [st.get(("sadd", *before))]
            if not first:
                u = L.pe.do(nc.tensor.matmul, up[:, :], CT[:, sl, ch], S[:, :], start=True, stop=True,
                            after=[st["sadd", *before]])
                st["u", n, j] = u
                v = L.dve.do(nc.vector.tensor_tensor, heads(us[:, :], NH, HP), heads(up[:, :], NH, HP),
                             over_last(sp_at("ecum", d, n, j), HP), ALU.mult, after=[u, st.get(("intra", *before))])
                u_free = [v]
            else:
                st["u", n, j] = st["g", n, j]
            for h in range(NH):
                o = HP * (h % 2)
                m = L.pe.do(nc.tensor.matmul, yp[o:o + HP, (h // 2) * P:(h // 2 + 1) * P],
                            xdt[:, two, h * HP:(h + 1) * HP], M[:, two, h * P:(h + 1) * P], start=(h < 2),
                            stop=first, skip_group_check=True,
                            after=[st["m", n, j], st["xdt", n, j], st.get(("y", *before))])
            if not first:
                for c in range(CI):
                    m = L.pe.do(nc.tensor.matmul, yp[:, c * P:(c + 1) * P], us[:, c * P:(c + 1) * P], K["ident"],
                                start=False, stop=True, skip_group_check=True, after=[v])
            st["intra", n, j] = m
            s = L.pe.do(nc.tensor.matmul, up[0:NST, :], btok[:, two, :], xw[:, two, :], start=True, stop=True,
                        after=[st["btok", n, j], st["xw", n, j], *u_free])
            st["snew", n, j] = s
            if first:
                st["sadd", n, j] = L.dve.do(nc.vector.tensor_copy, S[:, :], up[0:NST, :], after=[s, st.get(("u", *before))])
            else:
                a = L.pool.do(nc.gpsimd.tensor_tensor, heads(S[:, :], NH, HP), heads(S[:, :], NH, HP),
                              over_last(sp_at("etot", d, n, j, NST), HP), ALU.mult, after=[u])
                st["sadd", n, j] = L.dve.do(nc.vector.tensor_tensor, S[:, :], up[0:NST, :], S[:, :], ALU.add,
                                            after=[s, a])
            for c in range(CI):
                y = L.dve.do(nc.vector.scalar_tensor_tensor, ypre[:, c, ch], xs[:, sl, c, ch], dp(d, c),
                             yp[:, c * P:(c + 1) * P], ALU.mult, ALU.add,
                             after=[m, st["ssum", n - 1] if n else None, wl[d]])
            st["y", n, j] = y

        def gate(n):
            d = blocks[n][0]
            sl = n % 2
            cols = span(0, BLK, d)
            g = L.pool.do(nc.gpsimd.tensor_tensor, yg[:, :, :], ypre[:, :, cols], zs[:, sl, :, cols], ALU.mult,
                          after=[st["y", n, CPB - 1], st["silu", n], st.get(("out", n - 1))])
            st["gate", n] = g
            s = L.act.do(nc.scalar.activation, ypre[:, :, :], yg[:, :, :], ACT.Square, after=[g])
            a = L.pool.do(nc.gpsimd.tensor_tensor, ypre[:, 0:2, :], ypre[:, 0:2, :], ypre[:, 2:4, :], ALU.add,
                          after=[s])
            st["sq", n] = L.pool.do(nc.gpsimd.tensor_tensor, ypre[:, 0, :], ypre[:, 0, :], ypre[:, 1, :], ALU.add,
                                    after=[a])

        def means(n):
            i = next_rot()
            for j in range(CPB):
                m = L.pe.do(nc.tensor.matmul, rot[i][:, j:j + 1], ypre[:, 0, j * P:(j + 1) * P], K["over_di"],
                            start=True, stop=True, after=[st["sq", n], rot_free[i]])
            st["ssum", n] = m
            v = L.dve.do(nc.vector.tensor_scalar_add, rms[:, n % 2, :], rot[i][:, 0:CPB], EPS, after=[m])
            rot_free[i] = v
            st["means", n] = v

        def roots(n):
            st["root", n] = L.act.do(nc.scalar.activation, rms[:, n % 2, :], rms[:, n % 2, :], ACT.Sqrt,
                                     after=[st["means", n]])
            st["rrms", n] = L.dve.do(nc.vector.reciprocal, rrms[:, n % 2, :], rms[:, n % 2, :],
                                     after=[st["root", n]])

        def project_out(n, js=range(CPB)):
            d = blocks[n][0]
            for j in js:
                i = next_rot()
                for c in range(CI):
                    m = L.pe.do(nc.tensor.matmul, rot[i][:, 0:D], yg[:, c, j * P:(j + 1) * P], w_out[d][:, c, :],
                                start=(c == 0), stop=(c == CI - 1), after=[rot_free[i], wscaled[d], st["gate", n]])
                st["out", n] = m
                g = phys(n) * CPB + j
                r = rrms[:, n % 2, j:j + 1]
                if d == 0:
                    rot_free[i] = L.act.do(nc.scalar.mul, acc[:, g, :], rot[i][:, 0:D], r, after=[m, st["rrms", n]])
                    st["acc", g] = rot_free[i]
                else:
                    rot_free[i] = L.dve.do(nc.vector.scalar_tensor_tensor, acc[:, g, :], rot[i][:, 0:D], r,
                                           acc[:, g, :], ALU.mult, ALU.add, after=[m, st["rrms", n], st["acc", g]])

        for c in range(CX):
            st["halo", 0, c] = L.dve.do(nc.vector.memset, pre[:, c, 0:TAPS - 1], 0.0)
        order = [4, 0, 1], [2, 3, 5], [6, 7, 8]
        for part in order:
            project(0, part)
        silu(0)
        inside(0, 0)
        for n in range(NB):
            for j in range(CPB - 1):
                inside(n, j + 1)
                if n + 1 < NB:
                    project(n + 1, order[j])
                if j == 0 and n:
                    means(n - 1)
                across(n, j)
            if n:
                roots(n - 1)
            if n + 1 < NB:
                silu(n + 1)
            across(n, CPB - 1)
            if n:
                project_out(n - 1)
            gate(n)
            if n + 1 < NB:
                inside(n + 1, 0)
        means(NB - 1)
        roots(NB - 1)
        project_out(NB - 1)
        L.run()


def residual_and_values(nc, L, K, io, mixed, srcT, V, src_mv, src_rstd, x1_dram):
    with ExitStack() as ctx:
        def sb(name, shape, dt=F32):
            return ctx.enter_context(nc.sbuf_tensor(name, shape, dt))

        def ps(name, shape, dt=F32):
            return ctx.enter_context(nc.psum_tensor(name, shape, dt))

        x = sb("x_again", [P, 4, CPB, D])
        src = sb("src", [P, 2, CPB, D])
        stat = sb("r_stat", [P, CPB, 6])
        mv = sb("r_mv", [P, 2, CPB, 2])
        std = sb("r_std", [P, 2, CPB])
        rstd = sb("r_rstd", [P, 2, CPB])
        stat2 = sb("s_stat", [P, CPB, 6])
        std2 = sb("s_std", [P, 2, CPB])
        w_v = sb("w_v", [P, KD, D])
        tbank = [ps(f"src_t{i}", [P, BLK]) for i in range(3)]
        vbank = [ps(f"v_psum{i}", [P, BLK]) for i in range(3)]

        xv = io["x"].rearrange("b (c p) d -> p (b c) d", p=P)
        wl = L.dma(L.act, "w_v_load", w_v[:, :, :], io["v_w"])
        one = L.pool.do(nc.gpsimd.memset, V[:, :, :, HD:HD + 1], 1.0)
        loads, tevac, vevac, added, transposed = [], [None] * 3, [None] * 3, [], []
        for b in range(NBLK):
            loads.append(L.dma(L.sp, f"x_again{b % 4}", x[:, b % 4, :, :], xv[:, b * CPB:(b + 1) * CPB, :],
                               after=[added[b - 4]] if b >= 4 else []))
            c0 = b * CPB
            r = stats_of(L, lambda i: mixed[:, c0 + i, :], stat, mv[:, b % 2, :, :], std[:, b % 2, :],
                         rstd[:, b % 2, :], CPB, lambda i: [])
            for i in range(CPB):
                n = L.dve.do(nc.vector.tensor_scalar, mixed[:, c0 + i, :], mixed[:, c0 + i, :],
                             mv[:, b % 2, i, 0:1], rstd[:, b % 2, i:i + 1], ALU.subtract, ALU.mult, after=[r])
            a = L.pool.do(nc.gpsimd.tensor_tensor, mixed[:, c0:c0 + CPB, :], mixed[:, c0:c0 + CPB, :],
                          x[:, b % 4, :, :], ALU.add, after=[n, loads[b]])
            added.append(a)
            L.x1_saved = L.dma(L.sp, "x1_save", x1_dram[:, c0:c0 + CPB, :], mixed[:, c0:c0 + CPB, :], after=[a])
        for b in range(NBLK):
            c0 = b * CPB
            r = stats_of(L, lambda i: mixed[:, c0 + i, :], stat2, src_mv[:, c0:c0 + CPB, :], std2[:, b % 2, :],
                         src_rstd[:, c0:c0 + CPB], CPB, lambda i: [added[b]])
            for i in range(CPB):
                g = c0 + i
                n = L.dve.do(nc.vector.tensor_scalar, src[:, b % 2, i, :], mixed[:, g, :],
                             src_mv[:, g, 0:1], src_rstd[:, g:g + 1], ALU.subtract, ALU.mult,
                             after=[r, transposed[b - 2] if b >= 2 else None])
            for k in range(KD):
                bank = (b * KD + k) % 3
                for i in range(CPB):
                    t = L.pe.do(nc.tensor.transpose, tbank[bank][:, i * P:(i + 1) * P],
                                src[:, b % 2, i, k * P:(k + 1) * P], K["ident"], after=[n, tevac[bank]])
                e = L.act.do(nc.scalar.copy, srcT[:, k, b * BLK:(b + 1) * BLK], tbank[bank][:, :], after=[t])
                tevac[bank] = e
            transposed.append(t)
            for i in range(0, CPB, 2):
                bank = (c0 + i) // 2 % 3
                for two in range(2):
                    g = c0 + i + two
                    for k in range(KD):
                        m = L.pe.do(nc.tensor.matmul, vbank[bank][:, two * D:(two + 1) * D],
                                    srcT[:, k, g * P:(g + 1) * P], w_v[:, k, :], start=(k == 0),
                                    stop=(k == KD - 1), skip_group_check=True, after=[e, wl, vevac[bank]])
                for two in range(2):
                    vevac[bank] = L.dve.do(nc.vector.tensor_copy, V[:, c0 + i + two, :, 0:HD],
                                           heads(vbank[bank][:, two * D:(two + 1) * D], AH, HD), after=[m, one])
        L.run()


Q_TERMS = (0, 0, 1, 1, 0, 2)
K_TERMS = (0, 1, 0, 1, 2, 0)
ROWS = len(Q_TERMS) * HD
MROWS = 3
HG = 4
NG = AH // HG
KT = SEQ // P
VW = HD + 1


def attention(nc, L, K, io, srcT, V, attn):
    with ExitStack() as ctx:
        def sb(name, shape, dt=F32):
            return ctx.enter_context(nc.sbuf_tensor(name, shape, dt))

        def ps(name, shape, dt=F32):
            return ctx.enter_context(nc.psum_tensor(name, shape, dt))

        w_qk = sb("w_qk", [P, KD, NG, 3 * HG * HD])
        w_sc = sb("w_sc", [P, NG, HG * HD])
        qs = sb("q_stack", [ROWS + MROWS, 2, HG, SEQ], BF16)
        ks = sb("k_stack", [ROWS + MROWS, 2, HG, SEQ], BF16)
        raw = sb("qk_raw", [P, 2, BLK])
        ez = sb("q_scale", [P, BLK])
        parts = sb("qk_parts", [P, 2, 3, BLK], BF16)
        pt = sb("p_exp", [P, 4, 2, BLK])
        mx = sb("max_part", [P, HG * CPB, CPB])
        neg = sb("max_neg", [P, HG * CPB])
        mparts = sb("max_parts", [P, HG * CPB, MROWS], BF16)
        mrow = sb("max_rows", [HG * MROWS, 2, BLK], BF16)
        pvs = sb("pv_out", [P, BLK])
        rden = sb("rden", [P, CPB * HG])
        ebank = [ps(f"score_psum{i}", [P, 2, BLK]) for i in range(2)]
        pv = ps("pv_psum", [P, BLK])
        rbank = [ps(f"round_psum{i}", [P, BLK]) for i in range(3)]

        qk_dram = nc.dram_tensor("qk_rows", (2, P, 3, SEQ), BF16, kind="Internal").ap()
        wl = L.dma(L.act, "w_qk_load", w_qk[:, :, :, :], io["w_qk"])
        wl = L.dma(L.act, "w_qk_load", w_sc[:, :, :], io["w_sc"])
        zero = L.dve.do(nc.vector.memset, pv[:, :], 0.0)
        one = L.dve.do(nc.vector.memset, ks[ROWS:, :, :, :], 1.0)

        groups = [(b, g) for b in range(BATCH) for g in range(NG)]
        units = [(n, q) for n in range(len(groups)) for q in range(SEQ // BLK)]
        st = {}
        left = [None] * len(rbank)
        turn = [0]

        def take():
            i = turn[0]
            turn[0] = (i + 1) % len(rbank)
            return i, rbank[i], left[i]

        def split(n, j):
            b, g = groups[n]
            w = HG * HD
            blocks = [(2 * j + i, raw[:, i, :], parts[:, i, :, :], slice(i * w, (i + 1) * w))
                      for i in range(2)]
            z = ez[:, :]

            def project(i):
                s, x, _, _ = blocks[i]
                cols = slice(b * SEQ + s * BLK, b * SEQ + (s + 1) * BLK)
                t, bank, last = take()
                for k in range(KD):
                    m = L.pe.do(nc.tensor.matmul, bank[:, :], w_qk[:, k, g, i * w:(i + 2) * w], srcT[:, k, cols],
                                start=(k == 0), stop=(k == KD - 1), after=[wl, last])
                left[t] = st["raw", s] = L.act.do(nc.scalar.copy, x, bank[:, :], after=[m, st.get(("rest2", s % 2))])

            def scale():
                t, bank, last = take()
                for s, x, _, q in blocks:
                    m = L.pe.do(nc.tensor.matmul, bank[q, :], w_sc[q, g, :], x[q, :], start=True, stop=True,
                                skip_group_check=True, after=[st["raw", s], last])
                e = L.act.do(nc.scalar.activation, z, bank[:, :], ACT.Exp, scale=-1.0, after=[m, st.get("scaled")])
                left[t] = e
                st["ez"] = L.pool.do(nc.gpsimd.tensor_scalar, z, z, HD ** 0.5 / 2, HD ** 0.5 / 2, ALU.mult,
                                        ALU.add, after=[e])

            def invert(c):
                st["inverse"] = L.dve.do(nc.vector.reciprocal, z[:, c * P:(c + 1) * P], z[:, c * P:(c + 1) * P],
                                            after=[st["ez"]])

            def multiply():
                for s, x, _, q in blocks:
                    st["scaled"] = L.pool.do(nc.gpsimd.tensor_tensor, x[q, :], x[q, :], z[q, :], ALU.mult,
                                                after=[st["inverse"]])

            def high():
                for s, x, p, _ in blocks:
                    e = L.act.do(nc.scalar.copy, p[:, 0, :], x, after=[st["scaled"], st.get(("saved", (s + 2) % 4))])
                    st["rest", s] = L.pool.do(nc.gpsimd.tensor_tensor, x, x, p[:, 0, :], ALU.subtract, after=[e])

            def low():
                for s, x, p, _ in blocks:
                    e = L.act.do(nc.scalar.copy, p[:, 1, :], x, after=[st["rest", s]])
                    st["rest2", s % 2] = L.pool.do(nc.gpsimd.tensor_tensor, p[:, 2, :], x, p[:, 1, :], ALU.subtract,
                                               after=[e])

            def save():
                for s, _, p, q in blocks:
                    k = slice(w - q.start, 2 * w - q.start)
                    for row, of in ((0, q), (w, k)):
                        st["saved", s] = L.dma(L.sp, f"parts_save{s}",
                                               qk_dram[n % 2, row:row + w, :, s * BLK:(s + 1) * BLK], p[of, :, :],
                                               after=[st["rest2", s % 2], st.get(("stacked", n - 2))])

            return ((0, lambda: project(0)), (1, lambda: project(1)), (2, scale), (4, lambda: invert(0)),
                    (5, lambda: invert(1)), (6, lambda: invert(2)), (7, lambda: invert(3)), (8, multiply), (10, high),
                    (12, low), (12, save))

        def stack(n):
            slot = n % 2

            def bring(t):
                saved = [st["saved", s] for s in range(SEQ // BLK)]
                for dst, base, part in ((qs, 0, Q_TERMS[t]), (ks, HG * HD, K_TERMS[t])):
                    rows = qk_dram[slot, base:base + HG * HD, part, :].rearrange("(h r) c -> r h c", h=HG)
                    st["stacked", n] = L.dma(L.sp, f"stack{slot}", dst[t * HD:(t + 1) * HD, slot, :, :], rows,
                                             after=saved + [st.get(("scored", n - 2))])

            return tuple((t, lambda t=t: bring(t)) for t in range(len(Q_TERMS)))

        def max_part(u, i, kb):
            n, q = units[u]
            h, c = i // CPB, i % CPB
            at = q * BLK + c * P
            j, bank, last = take()
            m = L.pe.do(nc.tensor.matmul, bank[:, :], qs[0:ROWS, n % 2, h, at:at + P],
                        ks[0:ROWS, n % 2, h, kb * BLK:(kb + 1) * BLK], start=True, stop=True,
                        after=[st["stacked", n], last])
            left[j] = st["maxed", u] = L.dve.do(nc.vector.tensor_reduce, mx[:, c * HG + h, kb:kb + 1], bank[:, :],
                                                AX_X, ALU.max, after=[m, st.get("negated")])

        def max_rows(u):
            n, q = units[u]

            def negate():
                e = L.dve.do(nc.vector.tensor_reduce, neg[:, :], mx[:, :, :], AX_X, ALU.max, negate=True,
                             after=[st["maxed", u], st.get("mparts")])
                st["negated"] = e
                for i in range(MROWS):
                    c = L.dve.do(nc.vector.tensor_copy, mparts[:, :, i], neg[:, :], after=[e, st.get("mturned")])
                    if i < MROWS - 1:
                        e = L.dve.do(nc.vector.tensor_tensor, neg[:, :], neg[:, :], mparts[:, :, i], ALU.subtract,
                                     after=[c])
                st["mparts"] = c

            def turn_rows():
                j, bank, last = take()
                turned = bank[0:HG * MROWS, 0:BLK // 2].bitcast(BF16)
                for i in range(CPB):
                    t = L.pe.do(nc.tensor.transpose, turned[:, i * P:(i + 1) * P],
                                mparts[:, i * HG:(i + 1) * HG, :].rearrange("p h r -> p (h r)"), K["identb"],
                                after=[st["mparts"], last])
                st["mturned"] = t
                e = L.act.do(nc.scalar.copy, mrow[:, u % 2, :], turned[:, :], after=[t, st.get(("mrows", u - 2))])
                left[j] = e
                for h in range(HG):
                    st["mrows", u] = L.dma(L.sp, f"max_row{u % 2}",
                                           qs[ROWS:ROWS + MROWS, n % 2, h, q * BLK:(q + 1) * BLK],
                                           mrow[h * MROWS:(h + 1) * MROWS, u % 2, :], after=[e])

            return (0, negate), (1, turn_rows)

        def score(u, k, pair):
            n, q = units[u]
            i = k * 2 + pair
            for two in range(2):
                h = pair * 2 + two
                m = L.pe.do(nc.tensor.matmul, ebank[pair][:, two, :], ks[:, n % 2, h, k * P:(k + 1) * P],
                            qs[:, n % 2, h, q * BLK:(q + 1) * BLK], start=True, stop=True,
                            after=[st["mrows", u], one, st.get(("efree", pair))])
            st["scored", n] = m
            e = L.act.do(nc.scalar.activation, pt[:, i % 4, :, :], ebank[pair][:, :, :], ACT.Exp,
                         after=[m, st.get(("pfree", i % 4))])
            st["efree", pair] = e
            st["exp", u, k, pair] = e

        def weigh(u, k):
            n, q = units[u]
            b, g = groups[n]
            for h in range(HG):
                i = k * 2 + h // 2
                m = L.pe.do(nc.tensor.matmul, pv[h * 32:h * 32 + VW, :], V[:, b * KT + k, g * HG + h, :],
                            pt[:, i % 4, h % 2, :], start=(k == 0), stop=(k == KT - 1), skip_group_check=True,
                            after=[st["exp", u, k, h // 2], zero, st.get("pvfree")])
                st["pfree", i % 4] = m
            if k == KT - 1:
                st["pvfree"] = L.act.do(nc.scalar.copy, pvs[:, :], pv[:, :], after=[m, st.get("pvturned")])

        def finish(u):
            n, q = units[u]
            b, g = groups[n]
            c0 = b * KT + q * CPB

            def turn_out():
                j, bank, last = take()
                for i in range(CPB):
                    t = L.pe.do(nc.tensor.transpose, bank[:, i * P:(i + 1) * P], pvs[:, i * P:(i + 1) * P],
                                K["ident"], after=[st["pvfree"], last])
                st["pvturned"] = t
                o = bank[:, :].rearrange("p (n w) -> p n w", w=32)
                r = L.dve.do(nc.vector.reciprocal, rden[:, :].unsqueeze(2), o[:, :, HD:HD + 1],
                             after=[t, st.get("divided")])
                for i in range(CPB):
                    e = L.dve.do(nc.vector.tensor_tensor,
                                 heads(attn[:, c0 + i, g * HG * HD:(g + 1) * HG * HD], HG, HD),
                                 o[:, i * HG:(i + 1) * HG, 0:HD], over_last(rden[:, i * HG:(i + 1) * HG], HD),
                                 ALU.mult, after=[r])
                left[j] = st["divided"] = e

            return ((0, turn_out),)

        due = {}

        def plan(t, steps):
            for wait, step in steps:
                due.setdefault(t + wait, []).append(step)

        LEAD = KT + 3
        SPLIT = 14
        total = len(units) * KT
        per_group = total // len(groups)
        for j in range(2):
            plan(-LEAD - 1 - (2 - j) * SPLIT, split(0, j))
        plan(-LEAD - 1, tuple((0, step) for _, step in stack(0)))
        for n in range(1, len(groups)):
            first = (n - 1) * per_group + 2
            t0 = max(first - 2 * SPLIT, 6 - LEAD)
            for j in range(2):
                plan(t0 + SPLIT * j, split(n, j))
            plan(max(first, t0 + 2 * SPLIT), stack(n))
        for u in range(len(units)):
            plan(u * KT - LEAD + KT - 1, max_rows(u))
            plan(u * KT + KT + 2, finish(u))
        for t in range(min(due), total + 4):
            scoring, weighing, ahead = 0 <= t < total, 0 < t <= total, 0 <= t + LEAD < total
            u, k = divmod(t, KT)
            mu, mk = divmod(t + LEAD, KT)
            if scoring:
                score(u, k, 0)
            if ahead:
                max_part(mu, mk, 0)
            if scoring:
                score(u, k, 1)
            if ahead:
                max_part(mu, mk, 1)
            if weighing:
                weigh(*divmod(t - 1, KT))
            if ahead:
                max_part(mu, mk, 2)
            if ahead:
                max_part(mu, mk, 3)
            for step in due.get(t, []):
                step()
        L.run()


TILES = NCH + NE - 1
WROW = KD * FF + FT * D + 2 * FT
BROW = FF + D + 1


def gate_and_route(nc, L, K, io, attn, gT, x1_dram, src_mv, src_rstd, wsum, pos, tile_w, tile_b, to_dram):
    with ExitStack() as ctx:
        def sb(name, shape, dt=F32):
            return ctx.enter_context(nc.sbuf_tensor(name, shape, dt))

        def ps(name, shape, dt=F32):
            return ctx.enter_context(nc.psum_tensor(name, shape, dt))

        w_gate = sb("w_gate", [P, KD, D])
        w_o = sb("w_o", [P, KD, D])
        w_r = sb("w_router", [P, KD, NE])
        gb = sb("gate_b", [P, KD])
        rowsv = sb("rows_n1", [P, 2, D])
        b_r = sb("router_b", [P, NE])
        iota = sb("iotas", [P, NE + TILES + 1])
        oT = sb("attn_t", [P, 2, KD, BLK])
        sig = sb("gate_sig", [P, 2, BLK])
        x1 = sb("x1_block", [P, 2, CPB, D])
        res = sb("attn_res", [P, 2, CPB, D])
        stat = sb("n1_stat", [P, CPB, 6])
        mv = sb("n1_mv", [P, 2, CPB, 2])
        std = sb("n1_std", [P, 2, CPB])
        rstd = sb("n1_rstd", [P, 2, CPB])
        xrT = sb("xr_t", [P, 2, KD, P])
        logit = sb("logits", [P, NCH, NE])
        top = sb("top_v", [P, NCH, NE])
        topi = sb("top_i", [P, NCH, NE], U32)
        topf = sb("top_f", [P, NCH, 2])
        sm = sb("route_small", [P, 4, NCH])
        hot = sb("one_hot", [P, NCH, NE])
        rank = sb("rank", [P, NCH, NE])
        cnt = sb("counts", [P, NCH, NE])
        inc = sb("counts_up", [P, NCH, NE])
        exp_ = sb("expert_small", [P, 4, NE])
        tl = sb("tile_small", [P, 2, TILES])
        tbank = [ps(f"o_t{i}", [P, BLK]) for i in range(2)]
        gbank = [ps(f"g_psum{i}", [P, BLK]) for i in range(2)]
        abank = [ps(f"a_psum{i}", [P, BLK]) for i in range(2)]
        lbank = ps("l_psum", [P, NCH, NE])
        rbank = ps("r_psum", [P, 2, NCH, NE])

        wl = None
        for t, n in ((w_gate[:, :, :], "gate_w"), (w_o[:, :, :], "attn_out_w"), (w_r[:, :, :], "router_w"),
                     (gb[:, :], "gate_b"), (rowsv[:, :, :], "n1"), (b_r[:, :], "router_b"), (iota[:, :], "iotas")):
            wl = L.dma(L.act, "gate_load", t, io[n])

        st = {}
        for b in range(NBLK):
            for k in range(KD):
                for i in range(CPB):
                    t = L.pe.do(nc.tensor.transpose, tbank[k][:, i * P:(i + 1) * P],
                                attn[:, b * CPB + i, k * P:(k + 1) * P], K["ident"], after=[st.get(("t", k))])
                e = L.dve.do(nc.vector.tensor_copy, oT[:, b % 2, k, :], tbank[k][:, :],
                             after=[t, st.get(("used", b - 2))])
                st["t", k] = e
            for c in range(KD):
                for k in range(KD):
                    m = L.pe.do(nc.tensor.matmul, gbank[c][:, :], w_gate[:, k, c * P:(c + 1) * P], oT[:, b % 2, k, :],
                                start=(k == 0), stop=(k == KD - 1), after=[e, wl, st.get(("sig", c))])
                s = L.act.do(nc.scalar.activation, sig[:, c, :], gbank[c][:, :], ACT.Sigmoid, bias=gb[:, c:c + 1],
                             after=[m, st.get(("sigread", c))])
                st["sig", c] = s
                st["sigread", c] = L.pool.do(nc.gpsimd.tensor_tensor, gT[:, c, b * BLK:(b + 1) * BLK],
                                             oT[:, b % 2, c, :], sig[:, c, :], ALU.mult, after=[s, e])
                st["used", b] = st["sigread", c]
            st["gated", b] = st["used", b]
        st["turned"] = t
        for b in range(NBLK):
            two = b % 2
            c0 = b * CPB
            ld = L.dma(L.sp, f"x1_load{two}", x1[:, two, :, :], x1_dram[:, c0:c0 + CPB, :],
                       after=[st.get(("res", b - 2)), L.x1_saved])
            for i in range(CPB):
                g = c0 + i
                bank = abank[(g // 2) % 2][:, (g % 2) * D:(g % 2 + 1) * D]
                for k in range(KD):
                    m = L.pe.do(nc.tensor.matmul, bank, gT[:, k, g * P:(g + 1) * P], w_o[:, k, :], start=(k == 0),
                                stop=(k == KD - 1), skip_group_check=True,
                                after=[st["gated", b], wl, st.get(("a", (g // 2) % 2)) if g % 2 == 0 else None])
                if g % 2 == 0:
                    continue
                for gg in (g - 1, g):
                    ii = gg - c0
                    s = L.dve.do(nc.vector.tensor_scalar, x1[:, two, ii, :], x1[:, two, ii, :], src_mv[:, gg, 0:1],
                                 src_rstd[:, gg:gg + 1], ALU.subtract, ALU.mult, after=[ld])
                    v = L.dve.do(nc.vector.tensor_tensor, res[:, two, ii, :], x1[:, two, ii, :],
                                 abank[(g // 2) % 2][:, (gg % 2) * D:(gg % 2 + 1) * D], ALU.add,
                                 after=[s, m, st.get(("xr", b - 2))])
                    st["res", b] = v
                st["a", (g // 2) % 2] = v
            r = stats_of(L, lambda i: res[:, two, i, :], stat, mv[:, two, :, :], std[:, two, :], rstd[:, two, :], CPB,
                         lambda i: [v])
            for i in range(CPB):
                n = L.dve.do(nc.vector.tensor_scalar, res[:, two, i, :], res[:, two, i, :], mv[:, two, i, 0:1],
                             rstd[:, two, i:i + 1], ALU.subtract, ALU.mult, after=[r])
            p = L.pool.do(nc.gpsimd.tensor_tensor, res[:, two, :, :], res[:, two, :, :], over_mid(rowsv[:, 0, :], CPB),
                          ALU.mult, after=[n, wl])
            p = L.pool.do(nc.gpsimd.tensor_tensor, attn[:, c0:c0 + CPB, :], res[:, two, :, :],
                          over_mid(rowsv[:, 1, :], CPB), ALU.add, after=[p, st["turned"]])
            st["xr", b] = p
            for i in range(CPB):
                g = c0 + i
                o = (g % 2) * 2 * P
                for k in range(KD):
                    t = L.pe.do(nc.tensor.transpose, tbank[g % 2][:, k * P:(k + 1) * P],
                                attn[:, g, k * P:(k + 1) * P], K["ident"], after=[p, st.get(("t", g % 2))])
                e = L.act.do(nc.scalar.copy, xrT[:, g % 2, :, :], heads(tbank[g % 2][:, 0:KD * P], KD, P),
                             after=[t, st.get(("logit", g - 2))])
                st["t", g % 2] = e
                for k in range(KD):
                    m = L.pe.do(nc.tensor.matmul, lbank[:, g, :], xrT[:, g % 2, k, :], w_r[:, k, :], start=(k == 0),
                                stop=(k == KD - 1), skip_group_check=True, after=[e, wl])
                st["logit", g] = m
        v = L.dve.do(nc.vector.tensor_tensor, logit[:, :, :], lbank[:, :, :], over_mid(b_r[:, :], NCH), ALU.add,
                     after=[m])
        for g in range(NCH):
            a = L.dve.do(nc.vector.max, top[:, g, :], logit[:, g, :], after=[v])
        for g in range(NCH):
            a = L.dve.do(nc.vector.max_index, topi[:, g, :], top[:, g, :], logit[:, g, :], after=[a] if g == 0 else [])
        f = L.dve.do(nc.vector.tensor_copy, topf[:, :, :], topi[:, :, 0:2], after=[a])
        ch = L.dve.do(nc.vector.tensor_tensor, sm[:, 0, :], topf[:, :, 0], topf[:, :, 1], ALU.max, after=[f])
        df = L.dve.do(nc.vector.tensor_tensor, sm[:, 1, :], top[:, :, 1], top[:, :, 0], ALU.subtract)
        ex = L.act.do(nc.scalar.activation, sm[:, 1, :], sm[:, 1, :], ACT.Exp, after=[df])
        ad = L.dve.do(nc.vector.tensor_scalar_add, sm[:, 2, :], sm[:, 1, :], 1.0, after=[ex])
        rc = L.dve.do(nc.vector.reciprocal, sm[:, 3, :], sm[:, 2, :], after=[ad])
        sc = L.dve.do(nc.vector.tensor_tensor, sm[:, 1, :], sm[:, 1, :], sm[:, 3, :], ALU.mult, after=[rc])
        L.dve.do(nc.vector.tensor_tensor, wsum[:, :], sm[:, 1, :], sm[:, 3, :], ALU.add, after=[sc])
        h = L.dve.do(nc.vector.tensor_tensor, hot[:, :, :], over_mid(iota[:, 0:NE], NCH), over_last(sm[:, 0, :], NE),
                     ALU.is_equal, after=[ch, wl])
        hf = hot[:, :, :].rearrange("p g e -> p (g e)")
        L.pe.do(nc.tensor.matmul, rbank[:, 0, :, :].rearrange("p g e -> p (g e)"), K["before"], hf, start=True,
                stop=True, skip_group_check=True, after=[h])
        c = L.pe.do(nc.tensor.matmul, rbank[:, 1, :, :].rearrange("p g e -> p (g e)"), K["ones"], hf, start=True,
                    stop=True, skip_group_check=True)
        cc = L.dve.do(nc.vector.tensor_copy, cnt[:, :, :], rbank[:, 1, :, :], after=[c])
        one = L.dve.do(nc.vector.memset, top[:, :, :], 1.0, after=[sc])
        for e in range(NE):
            i = L.dve.do(nc.vector.tensor_tensor_scan, inc[:, :, e], top[:, :, e], cnt[:, :, e], 0.0, ALU.mult, ALU.add,
                         after=[cc, one])
        rk = L.dve.do(nc.vector.tensor_tensor, rank[:, :, :], rbank[:, 0, :, :], inc[:, :, :], ALU.add, after=[i])
        rk = L.dve.do(nc.vector.tensor_tensor, rank[:, :, :], rank[:, :, :], cnt[:, :, :], ALU.subtract, after=[rk])
        q = L.dve.do(nc.vector.tensor_scalar, exp_[:, 0, :], inc[:, NCH - 1, :], P / 2 - 0.5, 1.0 / P, ALU.add,
                     ALU.mult)
        q = L.dve.do(nc.vector.tensor_scalar_add, exp_[:, 0, :], exp_[:, 0, :], 8388608.0, after=[q])
        q = L.dve.do(nc.vector.tensor_scalar_add, exp_[:, 0, :], exp_[:, 0, :], -8388608.0, after=[q])
        q = L.dve.do(nc.vector.tensor_tensor_scan, exp_[:, 1, :], top[:, 0, :], exp_[:, 0, :], 0.0, ALU.mult, ALU.add,
                     after=[q])
        q1 = L.dve.do(nc.vector.tensor_tensor, exp_[:, 2, :], exp_[:, 1, :], exp_[:, 0, :], ALU.subtract, after=[q])
        q1 = L.dve.do(nc.vector.tensor_scalar_mul, exp_[:, 2, :], exp_[:, 2, :], float(P), after=[q1])
        rk = L.dve.do(nc.vector.tensor_tensor, rank[:, :, :], rank[:, :, :], over_mid(exp_[:, 2, :], NCH), ALU.add,
                      after=[q1, rk])
        rk = L.dve.do(nc.vector.tensor_tensor, rank[:, :, :], rank[:, :, :], hot[:, :, :], ALU.mult, after=[rk])
        rk = L.dve.do(nc.vector.tensor_reduce, sm[:, 0, :], rank[:, :, :], AX_X, ALU.add, after=[rk])
        pp = L.dve.do(nc.vector.tensor_copy, pos[:, :], sm[:, 0, :], after=[rk])
        z = L.dve.do(nc.vector.memset, tl[:, 0, :], 0.0)
        for e in range(NE - 1):
            z = L.dve.do(nc.vector.scalar_tensor_tensor, tl[:, 0, :], iota[:, NE:NE + TILES], exp_[:, 1, e:e + 1],
                         tl[:, 0, :], ALU.is_ge, ALU.add, after=[z])
        L.dve.do(nc.vector.tensor_copy, tile_b[:, :], tl[:, 0, :], after=[z])
        z = L.dve.do(nc.vector.tensor_scalar, tl[:, 1, :], tl[:, 0, :], float(P), iota[:, NE + TILES:], ALU.mult,
                     ALU.add, after=[z])
        L.dve.do(nc.vector.tensor_copy, tile_w[:, :], tl[:, 1, :], after=[z])
        for g in range(NCH):
            L.scattered = L.dma(L.pool, "scatter", to_dram, bass.IndirectOffsetOnAxis(ap=pos[:, g:g + 1], axis=0),
                                after=[pp, L.zeroed], start=lambda o, i, s: nc.gpsimd.indirect_dma_start(o, i, s, None),
                                third=attn[:, g, :])
        L.run()


def experts(nc, L, K, io, tile_w, tile_b, to_dram, from_dram):
    RING = 4
    with ExitStack() as ctx:
        def sb(name, shape, dt=F32):
            return ctx.enter_context(nc.sbuf_tensor(name, shape, dt))

        def ps(name, shape, dt=F32):
            return ctx.enter_context(nc.psum_tensor(name, shape, dt))

        W = sb("expert_w", [P, RING, WROW])
        B = sb("expert_b", [P, RING, BROW])
        xg = sb("expert_x", [P, RING, D])
        xT = sb("expert_xt", [P, 2, KD, P])
        hb = sb("expert_h", [P, 2, FF])
        stat = sb("expert_stat", [P, 6])
        mv = sb("expert_mv", [P, 2, 2])
        var = sb("expert_var", [P, 2])
        rstd = sb("expert_rstd", [P, 2])
        power = sb("minus_half", [P, 1])
        gT = sb("expert_g", [P, 2, FT, P])
        sel = sb("expert_out", [P, 2, D])
        tb = [ps(f"e_t{i}", [P, BLK]) for i in range(2)]
        hp = [ps(f"e_h{i}", [P, BLK]) for i in range(2)]
        gp = [ps(f"e_g{i}", [P, BLK]) for i in range(2)]
        op = [ps(f"e_o{i}", [P, BLK]) for i in range(2)]
        half = L.pool.do(nc.gpsimd.memset, power[:, :], -0.5)
        st = {}

        def gather(dst, table, index):
            return dict(out=dst, in_=None, third=table, start=lambda o, i, s: nc.gpsimd.indirect_dma_start(
                o, None, s, bass.IndirectOffsetOnAxis(ap=index, axis=0)))

        def fetch(i):
            s = i % RING
            free = [st.get(("done", i - RING)), st.get(("gelu", i - RING)), st.get(("second", i - RING))]
            st["w", i] = L.dma(L.pool, f"expert_w{s}", after=free, **gather(W[:, s, :], io["expert_w"],
                                                                          tile_w[:, i:i + 1]))
            st["b", i] = L.dma(L.pool, f"expert_b{s}", after=free, **gather(B[:, s, :], io["expert_b"],
                                                                          tile_b[:, i:i + 1]))
            st["x", i] = L.dma(L.sp, f"expert_x{s}", xg[:, s, :], to_dram[i * P:(i + 1) * P, :],
                               after=[L.scattered, *free])

        def first(i):
            s, two = i % RING, i % 2
            for k in range(KD):
                t = L.pe.do(nc.tensor.transpose, tb[two][:, k * P:(k + 1) * P], xg[:, s, k * P:(k + 1) * P], K["ident"],
                            after=[st["x", i], st.get(("xt", i - 2))])
            e = L.act.do(nc.scalar.copy, xT[:, two, :, :], heads(tb[two][:, 0:KD * P], KD, P),
                         after=[t, st.get(("h", i - 2))])
            st["xt", i] = e
            for k in range(KD):
                m = L.pe.do(nc.tensor.matmul, hp[two][:, :], xT[:, two, k, :], W[:, s, k * FF:(k + 1) * FF],
                            start=(k == 0), stop=(k == KD - 1), after=[e, st["w", i], st.get(("hb", i - 2))])
            st["h", i] = m
            v = L.dve.do(nc.vector.tensor_tensor, hb[:, two, :], hp[two][:, :], B[:, s, 0:FF], ALU.add,
                         after=[m, st["b", i], st.get(("g", i - 2))])
            st["hb", i] = v
            v = L.dve.do(nc.vector.bn_stats, stat[:, :], hb[:, two, :], after=[v])
            v = L.dve.do(nc.vector.bn_aggr, mv[:, two, :], stat[:, :], after=[v])
            v = L.dve.do(nc.vector.tensor_scalar_add, var[:, two:two + 1], mv[:, two, 1:2], EPS, after=[v])
            r = L.pool.do(nc.gpsimd.tensor_tensor, rstd[:, two:two + 1], var[:, two:two + 1], power[:, :], ALU.pow,
                          after=[v, half])
            st["n", i] = L.dve.do(nc.vector.tensor_scalar, hb[:, two, :], hb[:, two, :], mv[:, two, 0:1],
                                  rstd[:, two:two + 1], ALU.subtract, ALU.mult, after=[r])

        def second(i):
            s, two = i % RING, i % 2
            for c in range(FT):
                t = L.pe.do(nc.tensor.transpose, gp[two][:, c * P:(c + 1) * P], hb[:, two, c * P:(c + 1) * P],
                            K["ident"], after=[st["n", i], st.get(("gelu", i - 2))])
            st["g", i] = t
            o = KD * FF + FT * D
            for c in range(FT):
                e = L.act.do(nc.scalar.activation, gT[:, two, c, :], gp[two][:, c * P:(c + 1) * P], ACT.Gelu,
                             scale=W[:, s, o + c:o + c + 1], bias=W[:, s, o + FT + c:o + FT + c + 1],
                             after=[t, st["w", i], st.get(("second", i - 2))])
            st["gelu", i] = e

        def third(i):
            s, two = i % RING, i % 2
            o = KD * FF
            for c in range(FT):
                m = L.pe.do(nc.tensor.matmul, op[two][:, 0:D], gT[:, two, c, :], W[:, s, o + c * D:o + (c + 1) * D],
                            start=(c == 0), stop=(c == FT - 1), after=[st["gelu", i], st.get(("ob", i - 2))])
            st["second", i] = m
            v = L.dve.do(nc.vector.tensor_tensor, sel[:, two, :], op[two][:, 0:D], B[:, s, FF:FF + D], ALU.add,
                         after=[m, st.get(("saved", i - 2))])
            st["ob", i] = v
            v = L.dve.do(nc.vector.scalar_tensor_tensor, sel[:, two, :], sel[:, two, :], B[:, s, FF + D:], xg[:, s, :],
                         ALU.mult, ALU.add, after=[v])
            st["done", i] = v
            st["saved", i] = L.dma(L.sp, f"expert_save{two}", from_dram[i * P:(i + 1) * P, :], sel[:, two, :],
                                   after=[v])

        for i in range(RING - 2):
            fetch(i)
        for i in range(TILES + 2):
            if i < TILES:
                first(i)
            if 1 <= i <= TILES:
                second(i - 1)
            if 2 <= i:
                third(i - 2)
            if i + RING - 2 < TILES:
                fetch(i + RING - 2)
        L.saved = [st["saved", TILES - 1], st["saved", TILES - 2]]
        L.run()


def finish_tokens(nc, L, K, io, xr, wsum, pos, from_dram, x1_dram, out):
    with ExitStack() as ctx:
        def sb(name, shape, dt=F32):
            return ctx.enter_context(nc.sbuf_tensor(name, shape, dt))

        x1 = sb("x1_final", [P, NCH, D])
        sel = sb("selected", [P, NCH, D])
        rowsv = sb("rows_n2", [P, 2, D])
        stat = sb("f_stat", [P, CPB, 6])
        mv = sb("f_mv", [P, 2, 2, CPB, 2])
        std = sb("f_std", [P, 2, 2, CPB])
        rstd = sb("f_rstd", [P, 2, 2, CPB])
        ov = out.rearrange("b (c p) d -> p (b c) d", p=P)
        wl = L.dma(L.act, "n2_load", rowsv[:, :, :], io["n2"])
        x1l, back = [], []
        for b in range(NBLK):
            c = slice(b * CPB, (b + 1) * CPB)
            x1l.append(L.dma(L.sp, f"x1_final{b}", x1[:, c, :], x1_dram[:, c, :]))
            for g in range(b * CPB, (b + 1) * CPB):
                s = L.dma(L.pool, f"back{b}", sel[:, g, :], None, after=L.saved,
                          start=lambda o, i, s, g=g: nc.gpsimd.indirect_dma_start(
                              o, i, s, bass.IndirectOffsetOnAxis(ap=pos[:, g:g + 1], axis=0)), third=from_dram)
            back.append(s)
        for b in range(NBLK):
            two, c0 = b % 2, b * CPB
            for i in range(CPB):
                v = L.dve.do(nc.vector.scalar_tensor_tensor, sel[:, c0 + i, :], sel[:, c0 + i, :],
                             wsum[:, c0 + i:c0 + i + 1], xr[:, c0 + i, :], ALU.mult, ALU.add, after=[back[b]])
            for norm in range(2):
                r = stats_of(L, lambda i: sel[:, c0 + i, :], stat, mv[:, two, norm, :, :], std[:, two, norm, :],
                             rstd[:, two, norm, :], CPB, lambda i: [v])
                for i in range(CPB):
                    v = L.dve.do(nc.vector.tensor_scalar, sel[:, c0 + i, :], sel[:, c0 + i, :],
                                 mv[:, two, norm, i, 0:1], rstd[:, two, norm, i:i + 1], ALU.subtract, ALU.mult,
                                 after=[r])
                blk = sel[:, c0:c0 + CPB, :]
                if norm == 0:
                    v = L.pool.do(nc.gpsimd.tensor_tensor, blk, blk, over_mid(rowsv[:, 0, :], CPB), ALU.mult,
                                  after=[v, wl])
                    v = L.dve.do(nc.vector.tensor_tensor, blk, blk, over_mid(rowsv[:, 1, :], CPB), ALU.add, after=[v])
                else:
                    v = L.pool.do(nc.gpsimd.tensor_tensor, blk, blk, x1[:, c0:c0 + CPB, :], ALU.add,
                                  after=[v, x1l[b]])
            s = L.dma(L.sp, "out_store", ov[:, c0:c0 + CPB, :], blk, after=[v])
        L.sp.do(nc.sync.wait_ge, s.sem, s.value)
        L.run()


C_PARTS = [("ident", P), ("flip", P), ("upto", P), ("ones", P), ("before", P), ("over_di", 1), ("mask", BLK),
           ("sel", NH * P), ("negsel", NH * P)]
C_BF16 = ("mask", "sel", "negsel")
C_AT, _at = {}, 0
for _n, _w in C_PARTS:
    C_AT[_n] = (_at, _w)
    _at += _w
C_WIDTH = _at


def constants():
    import numpy as np
    t = {n: np.zeros((P, w), np.float32) for n, w in C_PARTS}
    i = np.arange(P)
    t["ident"][i, i] = 1
    t["flip"][i, P - 1 - i] = 1
    t["upto"][:] = i[:, None] <= i[None, :]
    t["ones"][:] = 1
    t["before"][:] = i[:, None] < i[None, :]
    t["over_di"][:] = 1.0 / DI
    t["mask"][:] = np.tile(np.where(i[:, None] <= i[None, :], 0.0, -1e30), (1, CPB))
    for part in range(3):
        for h in range(NH):
            t["sel"][part * NH + h, h * P:(h + 1) * P] = 1
    t["negsel"][:] = -t["sel"]
    return np.concatenate([t[n] for n, _ in C_PARTS], axis=1)


C_WIDE = sum(w for n, w in C_PARTS if n not in C_BF16)


def load_constants(nc, L, ctx, io):
    cf = ctx.enter_context(nc.sbuf_tensor("const_f32", [P, C_WIDE], F32))
    identb = ctx.enter_context(nc.sbuf_tensor("const_ident_bf16", [P, P], BF16))
    K = {n: cf[:, C_AT[n][0]:C_AT[n][0] + C_AT[n][1]] for n, _ in C_PARTS if n not in C_BF16}
    a = L.dma(L.act, "const_load", cf[:, :], io["consts"][:, 0:C_WIDE])
    L.dve.do(nc.vector.tensor_copy, identb[:, :], K["ident"], after=[a])
    K["identb"] = identb[:, :]
    return K


def load_scan_constants(nc, L, ctx, io, K):
    cb = ctx.enter_context(nc.sbuf_tensor("const_bf16", [P, C_WIDTH - C_WIDE], BF16))
    with nc.sbuf_tensor("const_stage", [P, C_WIDTH - C_WIDE], F32) as stage:
        a = L.dma(L.act, "mask_load", stage[:, :], io["consts"][:, C_WIDE:C_WIDTH])
        for n in C_BF16:
            o, w = C_AT[n]
            o -= C_WIDE
            rows = P if n == "mask" else 3 * NH
            K[n] = cb[0:rows, o:o + w]
            L.dve.do(nc.vector.tensor_copy, K[n], stage[0:rows, o:o + w], after=[a])
        L.run()


def build(nc, io, out, upto=9):
    with ExitStack() as ctx:
        L = Lanes(nc, ctx)
        x1_dram = nc.dram_tensor("x1_scratch", (P, NCH, D), F32, kind="Internal").ap()
        to_dram = nc.dram_tensor("expert_rows", (TILES * P, D), F32, kind="Internal").ap()
        from_dram = nc.dram_tensor("expert_results", (TILES * P, D), F32, kind="Internal").ap()

        def sb(scope, name, shape, dt=F32):
            return scope.enter_context(nc.sbuf_tensor(name, shape, dt))

        main = sb(ctx, "tokens", [P, NCH, D])
        turned = sb(ctx, "tokens_t", [P, KD, TOK])
        src_mv = sb(ctx, "src_mv", [P, NCH, 2])
        src_rstd = sb(ctx, "src_rstd", [P, NCH])
        K = load_constants(nc, L, ctx, io)
        with nc.sbuf_tensor("zeros", [P, D], F32) as zeros:
            z = L.dve.do(nc.vector.memset, zeros[:, :], 0.0)
            for i in range(TILES):
                L.zeroed = L.dma(L.sp, "zero_rows", to_dram[i * P:(i + 1) * P, :], zeros[:, :], after=[z])
            L.sp.do(nc.sync.wait_ge, L.zeroed.sem, L.zeroed.value)
            L.run()
        with ExitStack() as scan:
            load_scan_constants(nc, L, scan, io, K)
            sp = {n: sb(scan, "scan_" + n, [P, 2, NCH * NH]) for n in ("dt", "ecum", "eto", "etot")}
            sp["cumT"] = sb(scan, "scan_cum_t", [3 * NH, 2 * TOK], BF16)
            norm_and_steps(nc, L, K, io, turned, sp)
            mamba(nc, L, K, io, turned, sp, main)
        if upto > 2:
            with ExitStack() as att:
                V = sb(att, "values", [P, NCH, AH, VW])
                residual_and_values(nc, L, K, io, main, turned, V, src_mv, src_rstd, x1_dram)
                if upto > 3:
                    attention(nc, L, K, io, turned, V, main)
        if upto > 4:
            wsum = sb(ctx, "top_sum", [P, NCH])
            pos = sb(ctx, "token_row", [P, NCH], U32)
            tile_w = sb(ctx, "tile_w_row", [P, TILES], U32)
            tile_b = sb(ctx, "tile_b_row", [P, TILES], U32)
            gate_and_route(nc, L, K, io, main, turned, x1_dram, src_mv, src_rstd, wsum, pos, tile_w, tile_b, to_dram)
            if upto > 5:
                experts(nc, L, K, io, tile_w, tile_b, to_dram, from_dram)
                finish_tokens(nc, L, K, io, main, wsum, pos, from_dram, x1_dram, out)
        if upto <= 5:
            s = L.dma(L.sp, "out_store", out.rearrange("b (c p) d -> p (b c) d", p=P), main[:, :, :])
            L.sp.do(nc.sync.wait_ge, s.sem, s.value)
            L.run()


def layout(a):
    import numpy as np
    a = {n.replace("L0_attn_", "").replace("L0_ffn_", ""): np.asarray(v) for n, v in a.items()}

    def kt(w):
        return np.ascontiguousarray(w.reshape(-1, P, w.shape[1]).transpose(1, 0, 2))

    def rows(v):
        return np.ascontiguousarray(np.broadcast_to(v.reshape(1, -1), (P, v.size)))

    def cols(v):
        return v.reshape(-1, P).T

    o = {"x": a["x"], "consts": constants()}
    proj = DI + CX * P
    o["w_dt"] = kt(np.concatenate([a["f_in_w"][proj:].T, a["b_in_w"][proj:].T], axis=1))
    o["dt_bias"] = rows(np.concatenate([a["f_dt_bias"], a["b_dt_bias"]]))
    o["a_log"] = rows(np.concatenate([a["f_A_log"], a["b_A_log"]]))
    for d, f in enumerate("fb"):
        o[f"w_in{d}"] = kt(a[f + "_in_w"][:proj].T)
        o[f"w_out{d}"] = kt(a[f + "_out_w"].T)
        taps = a[f + "_conv_w"].reshape(CX, P, TAPS).transpose(1, 0, 2).reshape(P, CX * TAPS)
        o[f"chan{d}"] = np.concatenate([taps, cols(a[f + "_conv_b"]), cols(np.repeat(a[f + "_Dp"], HP)),
                                        cols(a[f + "_norm_w"])], axis=1)
    o["v_w"] = kt(a["v_w"])
    q = a["q_w"].reshape(KD, P, NG, HG * HD)
    k = a["k_w"].reshape(KD, P, NG, HG * HD)
    o["w_qk"] = np.concatenate([q, k, q], axis=3).transpose(1, 0, 2, 3)
    sc = np.zeros((NG, HG, HD, HG, HD), np.float32)
    for h in range(HG):
        sc[:, h, :, h, :] = a["scale_w"].reshape(NG, HG, HD)[:, h, :, None]
    sc = sc.reshape(NG, HG * HD, HG * HD).transpose(1, 0, 2)
    o["w_sc"] = np.concatenate([sc, sc], axis=0)
    o["gate_w"], o["attn_out_w"], o["router_w"] = kt(a["gate_w"]), kt(a["out_w"]), kt(a["moe_gate_w"])
    o["gate_b"] = cols(a["gate_b"])
    o["n1"] = rows(np.stack([a["n1_g"], a["n1_b"]])).reshape(P, 2, D)
    o["n2"] = rows(np.stack([a["n2_g"], a["n2_b"]])).reshape(P, 2, D)
    o["router_b"] = rows(a["moe_gate_b"])
    o["iotas"] = np.concatenate([np.tile(np.concatenate([np.arange(NE), np.arange(TILES)]), (P, 1)),
                                 np.arange(P)[:, None]], axis=1).astype(np.float32)
    part = lambda w: w.reshape(NE, -1, P, w.shape[-1]).transpose(0, 2, 1, 3).reshape(NE, P, -1)
    o["expert_w"] = np.concatenate([part(a["w1"]), part(a["w2"]), a["ln_g"].reshape(NE, FT, P).transpose(0, 2, 1),
                                    a["ln_b"].reshape(NE, FT, P).transpose(0, 2, 1)], axis=2).reshape(NE * P, WROW)
    o["expert_b"] = np.concatenate([a["b1"], a["b2"], a["res_scale"][:, None]], axis=1)
    return {k: np.ascontiguousarray(v) for k, v in o.items()}


def kernel(**inputs):
    import concourse.bacc as bacc
    from concourse.bass_utils import run_bass_kernel_spmd

    nc = bacc.Bacc("TRN2", target_bir_lowering=False, num_devices=1)
    arrays = layout(inputs)
    io = {n: nc.dram_tensor("in_" + n, v.shape, mybir.dt.from_np(v.dtype), kind="ExternalInput").ap()
          for n, v in arrays.items()}
    out = nc.dram_tensor("out", (BATCH, SEQ, D), F32, kind="ExternalOutput").ap()
    build(nc, io, out)
    r = run_bass_kernel_spmd(nc, [{"in_" + n: v for n, v in arrays.items()}], core_ids=[0])
    return r.results[0]["out"]
```

```python
from contextlib import ExitStack

import concourse.bass as bass
from concourse import mybir
from concourse.alu_op_type import AluOpType as ALU

F32 = mybir.dt.float32
BF16 = mybir.dt.bfloat16
U32 = mybir.dt.uint32
ACT = mybir.ActivationFunctionType
AX_X = mybir.AxisListType.X

P = 128
BATCH, SEQ, D = 2, 2048, 256
TOK = BATCH * SEQ
NCH = TOK // P
KD = D // P
BLK = 512
CPB = BLK // P
NBLK = TOK // BLK
BPS = SEQ // BLK
DI, NST, NH, HP = 512, 64, 8, 64
CI = DI // P
CX = (DI + 2 * NST) // P
TAPS = 4
EPS = 1e-5
AH, HD = 16, 16
NE, FF = 8, 512
FT = FF // P


class Step:

    def __init__(self, lane, emit, after):
        self.lane, self.emit, self.after = lane, emit, after
        self.signals = False
        self.sem = self.value = None
        for s in after:
            s.signals = True


class Lane:

    def __init__(self, engine, sem):
        self.engine, self.sem, self.count = engine, sem, 0
        self.queue, self.seen = [], {}

    def do(self, instruction, *operands, after=(), **options):
        s = Step(self, lambda: instruction(*operands, **options), [a for a in after if a is not None])
        self.queue.append(s)
        return s

    def number(self):
        for s in self.queue:
            if s.sem is None and s.signals:
                self.count += 1
                s.sem, s.value = self.sem, self.count

    def emit(self):
        for s in self.queue:
            for a in s.after:
                if self.seen.get(a.sem.name, 0) < a.value:
                    self.engine.wait_ge(a.sem, a.value)
                    self.seen[a.sem.name] = a.value
            made = s.emit()
            if s.sem is self.sem:
                made.then_inc(self.sem, 1)
            elif s.sem is not None:
                made.then_inc(s.sem, 16)
        self.queue = []


class Lanes:

    def __init__(self, nc, ctx):
        self.nc, self.ctx = nc, ctx
        self.pe = Lane(nc.tensor, ctx.enter_context(nc.semaphore("pe_done")))
        self.act = Lane(nc.scalar, ctx.enter_context(nc.semaphore("act_done")))
        self.dve = Lane(nc.vector, ctx.enter_context(nc.semaphore("dve_done")))
        self.pool = Lane(nc.gpsimd, ctx.enter_context(nc.semaphore("pool_done")))
        self.sp = Lane(nc.sync, ctx.enter_context(nc.semaphore("sp_done")))
        self.arrivals = {}

    def dma(self, lane, name, out, in_, after=(), start=None, **options):
        if name not in self.arrivals:
            self.arrivals[name] = [self.ctx.enter_context(self.nc.semaphore(name)), 0]
        entry = self.arrivals[name]
        entry[1] += 16
        third = (options.pop("third"),) if "third" in options else ()
        s = lane.do(start or lane.engine.dma_start, out, in_, *third, after=after, **options)
        s.sem, s.value = entry[0], entry[1]
        return s

    def run(self):
        lanes = (self.pe, self.act, self.dve, self.pool, self.sp)
        for lane in lanes:
            lane.number()
        with self.nc.Block() as block:
            @block.tensor
            def _(_e):
                self.pe.emit()

            @block.scalar
            def _(_e):
                self.act.emit()

            @block.vector
            def _(_e):
                self.dve.emit()

            @block.gpsimd
            def _(_e):
                self.pool.emit()

            @block.sync
            def _(_e):
                self.sp.emit()


def heads(ap, n, w):
    return ap.rearrange("p (h q) -> p h q", h=n, q=w)


def over_last(ap, w):
    return ap.unsqueeze(2).to_broadcast([ap.shape[0], ap.shape[1], w])


def over_mid(ap, n):
    return ap.unsqueeze(1).to_broadcast([ap.shape[0], n, ap.shape[1]])


def stats_of(L, src, stat, mv, rstd, power, n, after, free=()):
    made = [L.dve.do(L.nc.vector.bn_stats, stat[:, i, :], src(i), after=[*after, *free]) for i in range(n)]
    for i in range(n):
        last = L.dve.do(L.nc.vector.bn_aggr, mv[:, i, :], stat[:, i, :], after=[made[i]])
    biased = L.dve.do(L.nc.vector.tensor_scalar_add, rstd[:, 0:n], mv[:, 0:n, 1], EPS, after=[last])
    return L.pool.do(L.nc.gpsimd.tensor_tensor, rstd[:, 0:n], rstd[:, 0:n], power.to_broadcast([P, n]), ALU.pow,
                     after=[biased])


def norm_and_steps(nc, L, K, io, xnT, sp):
    with ExitStack() as ctx:
        def sb(name, shape, dt=F32):
            return ctx.enter_context(nc.sbuf_tensor(name, shape, dt))

        def ps(name, shape, dt=F32):
            return ctx.enter_context(nc.psum_tensor(name, shape, dt))

        x = sb("x_in", [P, NCH, D])
        xn = sb("x_normed", [P, 2, CPB, D])
        stat = sb("ln_stat", [P, NCH, 6])
        mv = sb("ln_mv", [P, NCH, 2])
        rstd = sb("ln_rstd", [P, NCH])
        wdt = sb("w_dt", [P, KD, 2 * NH])
        dt_bias = sb("dt_bias", [P, 2 * NH])
        a_log = sb("a_log", [P, 2 * NH])
        neg_a = sb("neg_a", [P, 2 * NH])
        raw = sb("dt_raw", [P, 2, NCH * NH])
        tmp = sb("dt_tmp", [P, 2, NCH * NH])
        lg = sb("dt_log", [P, 2, NCH * NH])
        da = sb("dt_a", [P, 2, NCH * NH])
        cum = sb("cum", [P, 2, NCH * NH])
        rest = sb("cum_rest", [P, 2, NCH * NH])
        parts = sb("cum_parts", [P, 2 * NCH, 3, NH], BF16)
        tbank = [ps(f"x_t{i}", [P, BLK]) for i in range(3)]
        dtp = ps("dt_psum", [P, NCH, 2, NH])
        flip = ps("flip_psum", [P, NCH * NH])
        cump = ps("cum_psum", [P, 2, NCH * NH])
        totp = ps("tot_psum", [P, 2, NCH * NH])
        ctp = ps("cum_t_psum", [3 * NH, 8, P], BF16)[:, :, :]

        xv = io["x"].rearrange("b (c p) d -> p (b c) d", p=P)
        loads = [L.dma(L.sp, f"x_load{b}", x[:, b * CPB:(b + 1) * CPB, :], xv[:, b * CPB:(b + 1) * CPB, :])
                 for b in range(NBLK)]
        small = [L.dma(L.act, "dt_load", wdt[:, :, :], io["w_dt"]),
                 L.dma(L.act, "dt_load", dt_bias[:, :], io["dt_bias"]),
                 L.dma(L.act, "dt_load", a_log[:, :], io["a_log"])][-1]

        evac, st = [None] * 3, {}

        def stats(b):
            c = slice(b * CPB, (b + 1) * CPB)
            st["stats", b] = stats_of(L, lambda i: x[:, b * CPB + i, :], stat[:, c, :], mv[:, c, :], rstd[:, c],
                                      K["power"], CPB, [loads[b]])

        def turn(b):
            c0 = b * CPB
            for i in range(CPB):
                nx = L.dve.do(nc.vector.tensor_scalar, xn[:, b % 2, i, :], x[:, c0 + i, :],
                              mv[:, c0 + i, 0:1], rstd[:, c0 + i:c0 + i + 1], ALU.subtract, ALU.mult,
                              after=[st["stats", b], st.get(("turned", b - 2))])
            for k in range(KD):
                bank = (b * KD + k) % 3
                for i in range(CPB):
                    t = L.pe.do(nc.tensor.transpose, tbank[bank][:, i * P:(i + 1) * P],
                                xn[:, b % 2, i, k * P:(k + 1) * P], K["ident"], after=[nx, evac[bank]])
                st["turned", b] = t
                st["x_t", b] = evac[bank] = L.act.do(nc.scalar.copy, xnT[:, k, b * BLK:(b + 1) * BLK],
                                                     tbank[bank][:, :], after=[t])

        def steps_of(b):
            for g in range(b * CPB, (b + 1) * CPB):
                for k in range(KD):
                    st["dt"] = L.pe.do(nc.tensor.matmul, dtp[:, g, :, :].rearrange("p a h -> p (a h)"),
                                       xnT[:, k, g * P:(g + 1) * P], wdt[:, k, :], start=(k == 0),
                                       stop=(k == KD - 1), after=[st["x_t", b], small])

        for b in range(NBLK + 2):
            for lag, step in enumerate((stats, turn, steps_of)):
                if 0 <= b - lag < NBLK:
                    step(b - lag)
        dt_last = st["dt"]
        bias = [dt_bias[:, d * NH:(d + 1) * NH].unsqueeze(1).to_broadcast([P, NCH, NH]) for d in range(2)]
        g3 = lambda t, d: t[:, d, :].rearrange("p (g h) -> p g h", h=NH)
        f0 = L.dve.do(nc.vector.tensor_tensor, g3(raw, 0), dtp[:, :, 0, :], bias[0], ALU.add, after=[dt_last, small])
        f1 = L.dve.do(nc.vector.tensor_tensor, g3(tmp, 1), dtp[:, :, 1, :], bias[1], ALU.add, after=[dt_last])
        fl = L.pe.do(nc.tensor.matmul, flip[:, :], K["flip"], tmp[:, 1, :], start=True, stop=True, after=[f1])
        f2 = L.dve.do(nc.vector.tensor_copy, raw[:, 1, :], flip[:, :], after=[fl])
        a0 = L.dve.do(nc.vector.tensor_scalar_mul, tmp[:, :, :], raw[:, :, :], -1.0, after=[f0, f2])
        a1 = L.dve.do(nc.vector.tensor_tensor, tmp[:, :, :], tmp[:, :, :], raw[:, :, :], ALU.min, after=[a0])
        a2 = L.act.do(nc.scalar.activation, tmp[:, :, :], tmp[:, :, :], ACT.Exp, after=[a1])
        a3 = L.dve.do(nc.vector.tensor_scalar_add, tmp[:, :, :], tmp[:, :, :], 1.0, after=[a2])
        a4 = L.act.do(nc.scalar.activation, lg[:, :, :], tmp[:, :, :], ACT.Ln, after=[a3])
        na = L.act.do(nc.scalar.activation, neg_a[:, :], a_log[:, :], ACT.Exp, after=[small])
        na = L.dve.do(nc.vector.tensor_scalar_mul, neg_a[:, :], neg_a[:, :], -1.0, after=[na])
        a5 = L.dve.do(nc.vector.scalar_tensor_tensor, sp["dt"][:, :, :], raw[:, :, :], 0.0, lg[:, :, :],
                      ALU.max, ALU.add, after=[a4])
        for d in range(2):
            va = L.dve.do(nc.vector.tensor_tensor, g3(da, d), g3(sp["dt"], d),
                          neg_a[:, d * NH:(d + 1) * NH].unsqueeze(1).to_broadcast([P, NCH, NH]), ALU.mult,
                          after=[a5, na])
        flat = lambda t: t[:, :, :].rearrange("p a b -> p (a b)")
        c = L.pe.do(nc.tensor.matmul, flat(cump), K["upto"], flat(da), start=True, stop=True, after=[va])
        t = L.pe.do(nc.tensor.matmul, flat(totp), K["ones"], flat(da), start=True, stop=True, after=[va])
        v0 = L.dve.do(nc.vector.tensor_copy, cum[:, :, :], cump[:, :, :], after=[c])
        v1 = L.dve.do(nc.vector.tensor_tensor, rest[:, :, :], totp[:, :, :], cum[:, :, :], ALU.subtract, after=[v0, t])
        L.act.do(nc.scalar.activation, sp["ecum"][:, :, :], cum[:, :, :], ACT.Exp, after=[v0])
        e2 = L.act.do(nc.scalar.activation, sp["eto"][:, :, :], rest[:, :, :], ACT.Exp, after=[v1])
        L.act.do(nc.scalar.activation, sp["etot"][:, :, :], totp[:, :, :], ACT.Exp, after=[v1])
        pt = lambda i: parts[:, :, i, :]
        cg = flat(cum).rearrange("p (g h) -> p g h", h=NH)
        rg = flat(rest).rearrange("p (g h) -> p g h", h=NH)
        s0 = L.dve.do(nc.vector.tensor_copy, pt(0), cg, after=[v0])
        s1 = L.dve.do(nc.vector.tensor_tensor, rg, cg, pt(0), ALU.subtract, after=[s0, e2])
        s2 = L.dve.do(nc.vector.tensor_copy, pt(1), rg, after=[s1])
        s3 = L.dve.do(nc.vector.tensor_tensor, pt(2), rg, pt(1), ALU.subtract, after=[s2])
        turned, read = [ctp, heads(tbank[0][0:3 * NH, :].bitcast(BF16), 8, P)], [None, None]
        for i in range(2 * NCH):
            two = i // 8 % 2
            q = L.pe.do(nc.tensor.transpose, turned[two][:, i % 8, :], parts[:, i, :, :].rearrange("p a h -> p (a h)"),
                        K["identb"], after=[s3, read[two]])
            if i % 8 == 7:
                read[two] = L.dve.do(nc.vector.tensor_copy, heads(sp["cumT"][:, (i - 7) * P:(i + 1) * P], 8, P),
                                     turned[two], after=[q])


def mamba(nc, L, K, io, xnT, sp, w_in, chan, w_in_loaded, chan_loaded, acc):
    with ExitStack() as ctx:
        def sb(name, shape, dt=F32):
            return ctx.enter_context(nc.sbuf_tensor(name, shape, dt))

        def ps(name, shape, dt=F32):
            return ctx.enter_context(nc.psum_tensor(name, shape, dt))

        w_out = [sb(f"w_out{d}", [P, CI, D]) for d in range(2)]
        pre = sb("conv_in", [P, CX, TAPS - 1 + BLK])
        xs = sb("x_conv", [P, 2, CI, BLK])
        bc = sb("bc_conv", [P, BLK])
        BT = sb("b_t", [NST, 2, BLK])
        CT = sb("c_t", [NST, 2, BLK])
        zs = sb("z_gate", [P, 2, CI, BLK])
        ypre = sb("y_pre", [P, 2, CI, P])
        yg = sb("y_gated", [P, 2, CI, P])
        sq = sb("y_squares", [P, 2, CI, P])
        M = sb("decay", [P, 2, NH * P])
        btok = sb("b_tok", [P, 2, NST])
        xdt = sb("x_dt", [P, 2, DI])
        xw = sb("x_w", [P, 2, DI])
        us = sb("u_scaled", [P, DI])
        S = sb("state", [NST, DI])
        ms = sb("mean_square", [P, 2])
        rrms = sb("rrms", [P, 2])
        rot = [ps(f"rot{i}", [P, BLK]) for i in range(2)]
        Lp = ps("decay_psum", [P, NH * P])
        gb = ps("gb_psum", [P, BLK])
        xt = ps("xt_psum", [P, BLK])
        up = ps("u_psum", [P, BLK])
        yp = ps("y_psum", [P, BLK])

        wl = []
        for d in range(2):
            wl.append(L.dma(L.sp, f"w_out_load{d}", w_out[d][:, :, :], io[f"w_out{d}"]))
        tap = lambda d, c, i: chan[d][:, c * TAPS + i:c * TAPS + i + 1]
        cbias = lambda d, c: chan[d][:, CX * TAPS + c:CX * TAPS + c + 1]
        o1 = CX * (TAPS + 1)
        dp = lambda d, c: chan[d][:, o1 + c:o1 + c + 1]
        nw = lambda d, c: chan[d][:, o1 + CI + c:o1 + CI + c + 1]
        wscaled = []
        for d in range(2):
            for c in range(CI):
                s = L.dve.do(nc.vector.tensor_scalar_mul, w_out[d][:, c, :], w_out[d][:, c, :], nw(d, c),
                             after=[wl[d], chan_loaded])
            wscaled.append(s)

        blocks = [(d, b, j) for d in range(2) for b in range(BATCH) for j in range(BPS)]
        NB = len(blocks)

        def phys(n):
            d, b, j = blocks[n]
            return b * BPS + (j if d == 0 else BPS - 1 - j)

        def chunk_of(n, j):
            return phys(n) * CPB + (j if blocks[n][0] == 0 else CPB - 1 - j)

        def span(a, width, backward):
            if not backward:
                return slice(a, a + width)
            return slice(a + width - 1, a - 1 if a else None, -1)

        rot_free = [None, None]
        rot_n = [0]

        def next_rot():
            i = rot_n[0] % 2
            rot_n[0] += 1
            return i

        st = {}

        def project(n, tiles):
            d = blocks[n][0]
            sl = n % 2
            a = phys(n) * BLK
            if n == NB // 2 and w_in_loaded[1] is None:
                w_in_loaded[1] = L.dma(L.sp, "w_in_load1", w_in[:, :, :], io["w_in1"], after=[st["proj", n - 1]])
            for c in tiles:
                i = next_rot()
                col = DI + c * P if c < CX else (c - CX) * P
                for k in range(KD):
                    m = L.pe.do(nc.tensor.matmul, rot[i][:, :], w_in[:, k, col:col + P],
                                xnT[:, k, span(a, BLK, d)], start=(k == 0), stop=(k == KD - 1),
                                after=[rot_free[i], w_in_loaded[d]])
                st["proj", n] = m
                if c < CX:
                    e = L.act.do(nc.scalar.copy, pre[:, c, TAPS - 1:], rot[i][:, :],
                                 after=[m, st.get(("halo", n, c))])
                    rot_free[i] = e
                    out = xs[:, sl, c, :] if c < CI else bc[:, :]
                    guard = [st.get(("y", n - 2, CPB - 1)), st.get(("xt", n - 2, CPB - 1)), st.get(("silu", n - 1))]
                    v = L.dve.do(nc.vector.tensor_scalar, out, pre[:, c, TAPS - 1:], tap(d, c, TAPS - 1),
                                 cbias(d, c), ALU.mult, ALU.add, after=[e, chan_loaded, *guard])
                    for t in range(TAPS - 2, -1, -1):
                        v = L.dve.do(nc.vector.scalar_tensor_tensor, out, pre[:, c, t:t + BLK], tap(d, c, t),
                                     out, ALU.mult, ALU.add, after=[v])
                    if n + 1 < NB:
                        if blocks[n + 1][2]:
                            h = L.dve.do(nc.vector.tensor_copy, pre[:, c, 0:TAPS - 1], pre[:, c, BLK:], after=[v])
                        else:
                            h = L.dve.do(nc.vector.memset, pre[:, c, 0:TAPS - 1], 0.0, after=[v])
                        st["halo", n + 1, c] = h
                    st["conv", n, c] = v
                else:
                    lane, copy = (L.dve, nc.vector.tensor_copy) if c == CX + CI - 1 else (L.act, nc.scalar.copy)
                    e = lane.do(copy, zs[:, sl, c - CX, :], rot[i][:, :],
                                after=[m, st.get(("gate", n - 2, CPB - 1))])
                    rot_free[i] = e
                    st["z", n] = e

        def silu_x(n):
            sl = n % 2
            L.act.do(nc.scalar.activation, BT[:, sl, :], bc[0:NST, :], ACT.Silu,
                     after=[st["conv", n, CI], st.get(("g", n - 2, CPB - 1))])
            s = L.act.do(nc.scalar.activation, CT[:, sl, :], bc[NST:P, :], ACT.Silu,
                         after=[st["conv", n, CI], st.get(("u", n - 2, CPB - 1))])
            st["silu_bc", n] = s
            st["silu", n] = L.act.do(nc.scalar.activation, xs[:, sl, :, :], xs[:, sl, :, :], ACT.Silu,
                                     after=[s, *[st["conv", n, c] for c in range(CI)]])

        def silu_z(n):
            sl = n % 2
            st["silu_z", n] = L.act.do(nc.scalar.activation, zs[:, sl, :, :], zs[:, sl, :, :], ACT.Silu,
                                     after=[st["z", n]])

        def decays(n, j):
            d = blocks[n][0]
            g = d * NCH + chunk_of(n, j)
            two = (n * CPB + j) % 2
            ct = sp["cumT"][:, g * P:(g + 1) * P]
            before = (n, j - 1) if j else (n - 1, CPB - 1)
            before2 = (n, j - 2) if j >= 2 else (n - 1, CPB - 2 + j)
            lw = [st.get(("exp", *before))]
            for half in range(2):
                bank = Lp[:, half * BLK:(half + 1) * BLK]
                L.pe.do(nc.tensor.matmul, bank, ct, K["negsel"][:, half * BLK:(half + 1) * BLK], start=True,
                        stop=False, skip_group_check=True, after=lw)
                L.pe.do(nc.tensor.matmul, bank, K["identb"], K["mask"], start=False, stop=False,
                        skip_group_check=True)
                for h in range(CPB):
                    hh = half * CPB + h
                    m = L.pe.do(nc.tensor.matmul, bank[:, h * P:(h + 1) * P], K["sel"][:, hh * P:(hh + 1) * P], ct,
                                start=False, stop=True, skip_group_check=True)
            e = L.act.do(nc.scalar.activation, M[:, two, :], Lp[:, :], ACT.Exp,
                         after=[m, st.get(("intra", *before2))])
            st["exp", n, j] = e

        def products(n, j):
            d = blocks[n][0]
            sl, ch = n % 2, slice(j * P, (j + 1) * P)
            two = (n * CPB + j) % 2
            before = (n, j - 1) if j else (n - 1, CPB - 1)
            before2 = (n, j - 2) if j >= 2 else (n - 1, CPB - 2 + j)
            e = st["exp", n, j]
            free = [st.get(("m", *before)), st.get(("btok", *before))]
            L.pe.do(nc.tensor.matmul, gb[:, 0:P], BT[:, sl, ch], CT[:, sl, ch], start=True, stop=True,
                    after=[st["silu_bc", n], *free])
            gm = L.pe.do(nc.tensor.transpose, gb[:, P:P + NST], BT[:, sl, ch], K["ident"][0:NST, 0:NST])
            st["g", n, j] = gm
            for c in range(CI):
                x = L.pe.do(nc.tensor.transpose, xt[:, c * P:(c + 1) * P], xs[:, sl, c, ch], K["ident"],
                            after=[st["silu", n], st.get(("xdt", *before))])
            st["xt", n, j] = x
            mm = M[:, two, :]
            st["xdt", n, j] = L.dve.do(nc.vector.tensor_tensor, heads(xdt[:, two, :], NH, HP),
                                       heads(xt[:, :], NH, HP), over_last(sp_at("dt", d, n, j), HP), ALU.mult,
                                       after=[x, st.get(("intra", *before2)), st.get(("xw", *before2))])
            st["m", n, j] = L.dve.do(nc.vector.tensor_tensor, heads(mm, NH, P), heads(mm, NH, P),
                                     over_mid(gb[:, 0:P], NH), ALU.mult, after=[gm, e])
            st["btok", n, j] = L.dve.do(nc.vector.tensor_copy, btok[:, two, :], gb[:, P:P + NST],
                                        after=[st.get(("snew", *before2))])
            st["xw", n, j] = L.pool.do(nc.gpsimd.tensor_tensor, heads(xw[:, two, :], NH, HP),
                                       heads(xdt[:, two, :], NH, HP), over_last(sp_at("eto", d, n, j), HP), ALU.mult,
                                       after=[st["xdt", n, j], st.get(("snew", *before2))])

        def sp_at(what, d, n, j, rows=P):
            g = chunk_of(n, j)
            return sp[what][0:rows, d, g * NH:(g + 1) * NH]

        def from_state(n, j):
            d, _, jb = blocks[n]
            before = (n, j - 1) if j else (n - 1, CPB - 1)
            st["u_free", n, j] = st.get(("sadd", *before))
            if jb == 0 and j == 0:
                st["u", n, j] = st["g", n, j]
                return
            u = L.pe.do(nc.tensor.matmul, up[:, :], CT[:, n % 2, j * P:(j + 1) * P], S[:, :], start=True, stop=True,
                        after=[st["sadd", *before]])
            st["u", n, j] = u
            v = L.dve.do(nc.vector.tensor_tensor, heads(us[:, :], NH, HP), heads(up[:, :], NH, HP),
                         over_last(sp_at("ecum", d, n, j), HP), ALU.mult, after=[u, st.get(("intra", *before))])
            st["us", n, j] = st["u_free", n, j] = v
            st["decayed", n, j] = L.pool.do(nc.gpsimd.tensor_tensor, heads(S[:, :], NH, HP), heads(S[:, :], NH, HP),
                                            over_last(sp_at("etot", d, n, j, NST), HP), ALU.mult, after=[u])

        def across(n, j):
            d, _, jb = blocks[n]
            first = jb == 0 and j == 0
            sl, ch = n % 2, slice(j * P, (j + 1) * P)
            two = (n * CPB + j) % 2
            before = (n, j - 1) if j else (n - 1, CPB - 1)
            before2 = (n, j - 2) if j >= 2 else (n - 1, CPB - 2 + j)
            for h in range(NH):
                o = HP * (h % 2)
                m = L.pe.do(nc.tensor.matmul, yp[o:o + HP, (h // 2) * P:(h // 2 + 1) * P],
                            xdt[:, two, h * HP:(h + 1) * HP], M[:, two, h * P:(h + 1) * P], start=(h < 2),
                            stop=first, skip_group_check=True,
                            after=[st["m", n, j], st["xdt", n, j], st.get(("y", *before))])
            if not first:
                for c in range(CI):
                    m = L.pe.do(nc.tensor.matmul, yp[:, c * P:(c + 1) * P], us[:, c * P:(c + 1) * P], K["ident"],
                                start=False, stop=True, skip_group_check=True, after=[st["us", n, j]])
            st["intra", n, j] = m
            s = L.pe.do(nc.tensor.matmul, up[0:NST, :], btok[:, two, :], xw[:, two, :], start=True, stop=True,
                        after=[st["btok", n, j], st["xw", n, j], st["u_free", n, j]])
            st["snew", n, j] = s
            if first:
                st["sadd", n, j] = L.dve.do(nc.vector.tensor_copy, S[:, :], up[0:NST, :], after=[s, st.get(("u", *before))])
            else:
                st["sadd", n, j] = L.dve.do(nc.vector.tensor_tensor, S[:, :], up[0:NST, :], S[:, :], ALU.add,
                                            after=[s, st["decayed", n, j]])
            for c in range(CI):
                y = L.dve.do(nc.vector.scalar_tensor_tensor, ypre[:, two, c, :], xs[:, sl, c, ch], dp(d, c),
                             yp[:, c * P:(c + 1) * P], ALU.mult, ALU.add,
                             after=[m, st.get(("gate", *before2))])
            st["y", n, j] = y
            st["gate", n, j] = L.dve.do(nc.vector.tensor_tensor, yg[:, two, :, :], ypre[:, two, :, span(0, P, d)],
                                        zs[:, sl, :, span(j * P, P, d)], ALU.mult,
                                        after=[y, st["silu_z", n], st.get(("out", *before2)), st.get(("sq", *before2))])
            q = L.pool.do(nc.gpsimd.tensor_tensor, sq[:, two, :, :], yg[:, two, :, :], yg[:, two, :, :], ALU.mult,
                          after=[st["gate", n, j], st.get(("ssum", *before2))])
            q = L.pool.do(nc.gpsimd.tensor_tensor, sq[:, two, 0:2, :], sq[:, two, 0:2, :], sq[:, two, 2:4, :],
                          ALU.add, after=[q])
            st["sq", n, j] = L.pool.do(nc.gpsimd.tensor_tensor, sq[:, two, 0, :], sq[:, two, 0, :],
                                       sq[:, two, 1, :], ALU.add, after=[q])

        def project_out(n, j):
            d = blocks[n][0]
            two = (n * CPB + j) % 2
            before2 = (n, j - 2) if j >= 2 else (n - 1, CPB - 2 + j)
            i = next_rot()
            mean = rot[i][:, 0:1]
            m = L.pe.do(nc.tensor.matmul, mean, sq[:, two, 0, :], K["over_di"], start=True, stop=True,
                        after=[st["sq", n, j], rot_free[i]])
            st["ssum", n, j] = m
            v = L.dve.do(nc.vector.tensor_scalar_add, ms[:, two:two + 1], mean, EPS,
                         after=[m, st.get(("rrms", *before2))])
            rot_free[i] = v
            st["rrms", n, j] = L.pool.do(nc.gpsimd.tensor_tensor, rrms[:, two:two + 1], ms[:, two:two + 1],
                                         K["power"], ALU.pow, after=[v, st.get(("acc", *before2))])
            i = next_rot()
            for c in range(CI):
                m = L.pe.do(nc.tensor.matmul, rot[i][:, 0:D], yg[:, two, c, :], w_out[d][:, c, :],
                            start=(c == 0), stop=(c == CI - 1), after=[rot_free[i], wscaled[d]])
            st["out", n, j] = m
            g = chunk_of(n, j)
            r = rrms[:, two:two + 1]
            if d == 0:
                e = L.act.do(nc.scalar.mul, acc[:, g, :], rot[i][:, 0:D], r, after=[m, st["rrms", n, j]])
                st["acc", g] = e
            else:
                e = L.dve.do(nc.vector.scalar_tensor_tensor, acc[:, g, :], rot[i][:, 0:D], r, acc[:, g, :],
                             ALU.mult, ALU.add, after=[m, st["rrms", n, j], st["acc", g]])
            rot_free[i] = st["acc", n, j] = e

        for c in range(CX):
            st["halo", 0, c] = L.dve.do(nc.vector.memset, pre[:, c, 0:TAPS - 1], 0.0)
        order = [4, 0, 5], [1, 2, 6], [3, 7], [8]
        for part in order:
            project(0, part)
        decays(0, 0)
        silu_x(0)
        silu_z(0)
        products(0, 0)
        chunks = [(n, j) for n in range(NB) for j in range(CPB)]
        for (n, j), before, following in zip(chunks, [None] + chunks, chunks[1:] + [None]):
            last, more = j == CPB - 1, n + 1 < NB
            if following:
                decays(*following)
            if more and last:
                silu_x(n + 1)
            if j:
                if following and not last:
                    products(*following)
                from_state(n, j)
            if more:
                project(n + 1, order[j][:1])
            if more and last:
                silu_z(n + 1)
            if not j:
                products(*following)
                from_state(n, j)
            if before:
                project_out(*before)
            across(n, j)
            if more:
                project(n + 1, order[j][1:])
            if following and last:
                products(*following)
        project_out(*chunks[-1])
        L.run()


def residual_and_values(nc, L, K, io, mixed, srcT, V, src_mv, src_rstd, x1_dram):
    with ExitStack() as ctx:
        def sb(name, shape, dt=F32):
            return ctx.enter_context(nc.sbuf_tensor(name, shape, dt))

        def ps(name, shape, dt=F32):
            return ctx.enter_context(nc.psum_tensor(name, shape, dt))

        x = sb("x_again", [P, 4, CPB, D])
        src = sb("src", [P, 2, CPB, D])
        stat = sb("r_stat", [P, 2, CPB, 6])
        mv = sb("r_mv", [P, 2, CPB, 2])
        rstd = sb("r_rstd", [P, 2, CPB])
        stat2 = sb("s_stat", [P, 2, CPB, 6])
        w_v = sb("w_v", [P, KD, D])
        tbank = [ps(f"src_t{i}", [P, BLK]) for i in range(3)]
        vbank = [ps(f"v_psum{i}", [P, BLK]) for i in range(3)]

        xv = io["x"].rearrange("b (c p) d -> p (b c) d", p=P)
        wl = L.dma(L.act, "w_v_load", w_v[:, :, :], io["v_w"])
        one = L.pool.do(nc.gpsimd.memset, V[:, :, :, HD:HD + 1], 1.0)
        loads, tevac, vevac, st = [], [None] * 3, [None] * 3, {}

        def load(b):
            loads.append(L.dma(L.sp, f"x_again{b % 4}", x[:, b % 4, :, :], xv[:, b * CPB:(b + 1) * CPB, :],
                               after=[st.get(("x1", b - 4))]))

        def mixed_stats(b):
            st["mixed", b] = stats_of(L, lambda i: mixed[:, b * CPB + i, :], stat[:, b % 2, :, :], mv[:, b % 2, :, :],
                                      rstd[:, b % 2, :], K["power"], CPB, [], [st.get(("normed", b - 2))])

        def residual(b):
            c0 = b * CPB
            for i in range(CPB):
                n = L.dve.do(nc.vector.tensor_scalar, mixed[:, c0 + i, :], mixed[:, c0 + i, :],
                             mv[:, b % 2, i, 0:1], rstd[:, b % 2, i:i + 1], ALU.subtract, ALU.mult,
                             after=[st["mixed", b]])
            st["normed", b] = n
            st["x1", b] = L.pool.do(nc.gpsimd.tensor_tensor, mixed[:, c0:c0 + CPB, :], mixed[:, c0:c0 + CPB, :],
                                    x[:, b % 4, :, :], ALU.add, after=[n, loads[b]])
            L.x1_saved = L.dma(L.sp, "x1_save", x1_dram[:, c0:c0 + CPB, :], mixed[:, c0:c0 + CPB, :],
                               after=[st["x1", b]])

        def src_stats(b):
            c = slice(b * CPB, (b + 1) * CPB)
            st["src_stats", b] = stats_of(L, lambda i: mixed[:, b * CPB + i, :], stat2[:, b % 2, :, :],
                                          src_mv[:, c, :], src_rstd[:, c], K["power"], CPB, [st["x1", b]],
                                          [st.get(("src_stats", b - 2))])

        def turn(b):
            c0 = b * CPB
            for i in range(CPB):
                g = c0 + i
                n = L.dve.do(nc.vector.tensor_scalar, src[:, b % 2, i, :], mixed[:, g, :],
                             src_mv[:, g, 0:1], src_rstd[:, g:g + 1], ALU.subtract, ALU.mult,
                             after=[st["src_stats", b], st.get(("turned", b - 2))])
            for k in range(KD):
                bank = (b * KD + k) % 3
                for i in range(CPB):
                    t = L.pe.do(nc.tensor.transpose, tbank[bank][:, i * P:(i + 1) * P],
                                src[:, b % 2, i, k * P:(k + 1) * P], K["ident"], after=[n, tevac[bank]])
                st["src_t", b] = tevac[bank] = L.act.do(nc.scalar.copy, srcT[:, k, b * BLK:(b + 1) * BLK],
                                                        tbank[bank][:, :], after=[t])
            st["turned", b] = t

        def values(b):
            for g in range(b * CPB, (b + 1) * CPB, 2):
                bank = g // 2 % 3
                for two in range(2):
                    at = slice((g + two) * P, (g + two + 1) * P)
                    for k in range(KD):
                        m = L.pe.do(nc.tensor.matmul, vbank[bank][:, two * D:(two + 1) * D], srcT[:, k, at],
                                    w_v[:, k, :], start=(k == 0), stop=(k == KD - 1), skip_group_check=True,
                                    after=[st["src_t", b], wl, vevac[bank]])
                for two in range(2):
                    vevac[bank] = L.act.do(nc.scalar.copy, V[:, g + two, :, 0:HD],
                                           heads(vbank[bank][:, two * D:(two + 1) * D], AH, HD), after=[m, one])

        for b in range(NBLK + 4):
            for lag, step in enumerate((load, mixed_stats, residual, src_stats, turn, values)):
                at = b if lag == 0 else b - lag + 1
                if 0 <= at < NBLK:
                    step(at)
        L.run()


Q_TERMS = (0, 0, 1, 1, 0, 2)
K_TERMS = (0, 1, 0, 1, 2, 0)
ROWS = len(Q_TERMS) * HD
MROWS = 3
HG = 4
NG = AH // HG
KT = SEQ // P
VW = HD + 1


def attention(nc, L, K, io, srcT, V, attn):
    with ExitStack() as ctx:
        def sb(name, shape, dt=F32):
            return ctx.enter_context(nc.sbuf_tensor(name, shape, dt))

        def ps(name, shape, dt=F32):
            return ctx.enter_context(nc.psum_tensor(name, shape, dt))

        w_qk = sb("w_qk", [P, KD, NG, 3 * HG * HD])
        w_sc = sb("w_sc", [P, NG, HG * HD])
        qs = sb("q_stack", [ROWS + MROWS, 2, HG, SEQ], BF16)
        ks = sb("k_stack", [ROWS + MROWS, 2, HG, SEQ], BF16)
        raw = sb("qk_raw", [P, 2, BLK])
        ez = sb("q_scale", [P, BLK])
        parts = sb("qk_parts", [P, 2, 3, BLK], BF16)
        pt = sb("p_exp", [P, 4, 2, BLK])
        mx = sb("max_part", [P, HG * CPB, CPB])
        neg = sb("max_neg", [P, HG * CPB])
        mparts = sb("max_parts", [P, HG * CPB, MROWS], BF16)
        mrow = sb("max_rows", [HG * MROWS, 2, BLK], BF16)
        pvs = sb("pv_out", [P, BLK])
        rden = sb("rden", [P, CPB * HG])
        ebank = [ps(f"score_psum{i}", [P, 2, BLK]) for i in range(2)]
        pv = ps("pv_psum", [P, BLK])
        rbank = [ps(f"round_psum{i}", [P, BLK]) for i in range(3)]

        qk_dram = nc.dram_tensor("qk_rows", (2, P, 3, SEQ), BF16, kind="Internal").ap()
        wl = L.dma(L.act, "w_qk_load", w_qk[:, :, :, :], io["w_qk"])
        wl = L.dma(L.act, "w_qk_load", w_sc[:, :, :], io["w_sc"])
        zero = L.dve.do(nc.vector.memset, pv[:, :], 0.0)
        one = L.dve.do(nc.vector.memset, ks[ROWS:, :, :, :], 1.0)

        groups = [(b, g) for b in range(BATCH) for g in range(NG)]
        units = [(n, q) for n in range(len(groups)) for q in range(SEQ // BLK)]
        st = {}
        left = [None] * len(rbank)
        turn = [0]

        def take():
            i = turn[0]
            turn[0] = (i + 1) % len(rbank)
            return i, rbank[i], left[i]

        def split(n, j):
            b, g = groups[n]
            w = HG * HD
            blocks = [(2 * j + i, raw[:, i, :], parts[:, i, :, :], slice(i * w, (i + 1) * w))
                      for i in range(2)]
            z = ez[:, :]

            def project(i):
                s, x, _, _ = blocks[i]
                cols = slice(b * SEQ + s * BLK, b * SEQ + (s + 1) * BLK)
                t, bank, last = take()
                for k in range(KD):
                    m = L.pe.do(nc.tensor.matmul, bank[:, :], w_qk[:, k, g, i * w:(i + 2) * w], srcT[:, k, cols],
                                start=(k == 0), stop=(k == KD - 1), after=[wl, last])
                left[t] = st["raw", s] = L.act.do(nc.scalar.copy, x, bank[:, :], after=[m, st.get(("rest2", s % 2))])

            def scale():
                t, bank, last = take()
                for s, x, _, q in blocks:
                    m = L.pe.do(nc.tensor.matmul, bank[q, :], w_sc[q, g, :], x[q, :], start=True, stop=True,
                                skip_group_check=True, after=[st["raw", s], last])
                e = L.act.do(nc.scalar.activation, z, bank[:, :], ACT.Exp, scale=-1.0, after=[m, st.get("scaled")])
                left[t] = e
                st["ez"] = L.pool.do(nc.gpsimd.tensor_scalar, z, z, HD ** 0.5 / 2, HD ** 0.5 / 2, ALU.mult,
                                        ALU.add, after=[e])

            def invert(c):
                st["inverse"] = L.dve.do(nc.vector.reciprocal, z[:, c * P:(c + 1) * P], z[:, c * P:(c + 1) * P],
                                            after=[st["ez"]])

            def multiply():
                for s, x, _, q in blocks:
                    st["scaled"] = L.pool.do(nc.gpsimd.tensor_tensor, x[q, :], x[q, :], z[q, :], ALU.mult,
                                                after=[st["inverse"]])

            def high():
                for s, x, p, _ in blocks:
                    e = L.act.do(nc.scalar.copy, p[:, 0, :], x, after=[st["scaled"], st.get(("saved", (s + 2) % 4))])
                    st["rest", s] = L.pool.do(nc.gpsimd.tensor_tensor, x, x, p[:, 0, :], ALU.subtract, after=[e])

            def low():
                for s, x, p, _ in blocks:
                    e = L.act.do(nc.scalar.copy, p[:, 1, :], x, after=[st["rest", s]])
                    st["rest2", s % 2] = L.pool.do(nc.gpsimd.tensor_tensor, p[:, 2, :], x, p[:, 1, :], ALU.subtract,
                                               after=[e])

            def save():
                for s, _, p, q in blocks:
                    k = slice(w - q.start, 2 * w - q.start)
                    for row, of in ((0, q), (w, k)):
                        st["saved", s] = L.dma(L.sp, f"parts_save{s}",
                                               qk_dram[n % 2, row:row + w, :, s * BLK:(s + 1) * BLK], p[of, :, :],
                                               after=[st["rest2", s % 2], st.get(("stacked", n - 2))])

            return ((0, lambda: project(0)), (1, lambda: project(1)), (2, scale), (4, lambda: invert(0)),
                    (5, lambda: invert(1)), (6, lambda: invert(2)), (7, lambda: invert(3)), (8, multiply), (10, high),
                    (12, low), (12, save))

        def stack(n):
            slot = n % 2

            def bring(t):
                saved = [st["saved", s] for s in range(SEQ // BLK)]
                for dst, base, part in ((qs, 0, Q_TERMS[t]), (ks, HG * HD, K_TERMS[t])):
                    rows = qk_dram[slot, base:base + HG * HD, part, :].rearrange("(h r) c -> r h c", h=HG)
                    st["stacked", n] = L.dma(L.sp, f"stack{slot}", dst[t * HD:(t + 1) * HD, slot, :, :], rows,
                                             after=saved + [st.get(("scored", n - 2))])

            return tuple((t, lambda t=t: bring(t)) for t in range(len(Q_TERMS)))

        def max_part(u, i, kb):
            n, q = units[u]
            h, c = i // CPB, i % CPB
            at = q * BLK + c * P
            j, bank, last = take()
            m = L.pe.do(nc.tensor.matmul, bank[:, :], qs[0:ROWS, n % 2, h, at:at + P],
                        ks[0:ROWS, n % 2, h, kb * BLK:(kb + 1) * BLK], start=True, stop=True,
                        after=[st["stacked", n], last])
            left[j] = st["maxed", u] = L.dve.do(nc.vector.tensor_reduce, mx[:, c * HG + h, kb:kb + 1], bank[:, :],
                                                AX_X, ALU.max, after=[m, st.get("negated")])

        def max_rows(u):
            n, q = units[u]

            def negate():
                e = L.dve.do(nc.vector.tensor_reduce, neg[:, :], mx[:, :, :], AX_X, ALU.max, negate=True,
                             after=[st["maxed", u], st.get("mparts")])
                st["negated"] = e
                for i in range(MROWS):
                    c = L.dve.do(nc.vector.tensor_copy, mparts[:, :, i], neg[:, :], after=[e, st.get("mturned")])
                    if i < MROWS - 1:
                        e = L.dve.do(nc.vector.tensor_tensor, neg[:, :], neg[:, :], mparts[:, :, i], ALU.subtract,
                                     after=[c])
                st["mparts"] = c

            def turn_rows():
                j, bank, last = take()
                turned = bank[0:HG * MROWS, 0:BLK // 2].bitcast(BF16)
                for i in range(CPB):
                    t = L.pe.do(nc.tensor.transpose, turned[:, i * P:(i + 1) * P],
                                mparts[:, i * HG:(i + 1) * HG, :].rearrange("p h r -> p (h r)"), K["identb"],
                                after=[st["mparts"], last])
                st["mturned"] = t
                e = L.act.do(nc.scalar.copy, mrow[:, u % 2, :], turned[:, :], after=[t, st.get(("mrows", u - 2))])
                left[j] = e
                for h in range(HG):
                    st["mrows", u] = L.dma(L.sp, f"max_row{u % 2}",
                                           qs[ROWS:ROWS + MROWS, n % 2, h, q * BLK:(q + 1) * BLK],
                                           mrow[h * MROWS:(h + 1) * MROWS, u % 2, :], after=[e])

            return (0, negate), (1, turn_rows)

        def score(u, k, pair):
            n, q = units[u]
            i = k * 2 + pair
            for two in range(2):
                h = pair * 2 + two
                m = L.pe.do(nc.tensor.matmul, ebank[pair][:, two, :], ks[:, n % 2, h, k * P:(k + 1) * P],
                            qs[:, n % 2, h, q * BLK:(q + 1) * BLK], start=True, stop=True,
                            after=[st["mrows", u], one, st.get(("efree", pair))])
            st["scored", n] = m
            e = L.act.do(nc.scalar.activation, pt[:, i % 4, :, :], ebank[pair][:, :, :], ACT.Exp,
                         after=[m, st.get(("pfree", i % 4))])
            st["efree", pair] = e
            st["exp", u, k, pair] = e

        def weigh(u, k):
            n, q = units[u]
            b, g = groups[n]
            for h in range(HG):
                i = k * 2 + h // 2
                m = L.pe.do(nc.tensor.matmul, pv[h * 32:h * 32 + VW, :], V[:, b * KT + k, g * HG + h, :],
                            pt[:, i % 4, h % 2, :], start=(k == 0), stop=(k == KT - 1), skip_group_check=True,
                            after=[st["exp", u, k, h // 2], zero, st.get("pvfree")])
                st["pfree", i % 4] = m
            if k == KT - 1:
                st["pvfree"] = L.act.do(nc.scalar.copy, pvs[:, :], pv[:, :], after=[m, st.get("pvturned")])

        def finish(u):
            n, q = units[u]
            b, g = groups[n]
            c0 = b * KT + q * CPB

            def turn_out():
                j, bank, last = take()
                for i in range(CPB):
                    t = L.pe.do(nc.tensor.transpose, bank[:, i * P:(i + 1) * P], pvs[:, i * P:(i + 1) * P],
                                K["ident"], after=[st["pvfree"], last])
                st["pvturned"] = t
                o = bank[:, :].rearrange("p (n w) -> p n w", w=32)
                r = L.dve.do(nc.vector.reciprocal, rden[:, :].unsqueeze(2), o[:, :, HD:HD + 1],
                             after=[t, st.get("divided")])
                for i in range(CPB):
                    e = L.dve.do(nc.vector.tensor_tensor,
                                 heads(attn[:, c0 + i, g * HG * HD:(g + 1) * HG * HD], HG, HD),
                                 o[:, i * HG:(i + 1) * HG, 0:HD], over_last(rden[:, i * HG:(i + 1) * HG], HD),
                                 ALU.mult, after=[r])
                left[j] = st["divided"] = e

            return ((0, turn_out),)

        due = {}

        def plan(t, steps):
            for wait, step in steps:
                due.setdefault(t + wait, []).append(step)

        LEAD = KT + 3
        SPLIT = 14
        total = len(units) * KT
        per_group = total // len(groups)
        for j in range(2):
            plan(-LEAD - 1 - (2 - j) * SPLIT, split(0, j))
        plan(-LEAD - 1, tuple((0, step) for _, step in stack(0)))
        for n in range(1, len(groups)):
            first = (n - 1) * per_group + 2
            t0 = max(first - 2 * SPLIT, 6 - LEAD)
            for j in range(2):
                plan(t0 + SPLIT * j, split(n, j))
            plan(max(first, t0 + 2 * SPLIT), stack(n))
        for u in range(len(units)):
            plan(u * KT - LEAD + KT - 1, max_rows(u))
            plan(u * KT + KT + 2, finish(u))
        for t in range(min(due), total + 4):
            scoring, weighing, ahead = 0 <= t < total, 0 < t <= total, 0 <= t + LEAD < total
            u, k = divmod(t, KT)
            mu, mk = divmod(t + LEAD, KT)
            if scoring:
                score(u, k, 0)
            if ahead:
                max_part(mu, mk, 0)
            if scoring:
                score(u, k, 1)
            if ahead:
                max_part(mu, mk, 1)
            if weighing:
                weigh(*divmod(t - 1, KT))
            if ahead:
                max_part(mu, mk, 2)
            if ahead:
                max_part(mu, mk, 3)
            for step in due.get(t, []):
                step()
        L.run()


TILES = NCH + NE - 1
WROW = KD * FF + FT * D + 2 * FT
BROW = FF + D + 1


def gate_and_route(nc, L, K, io, attn, gT, x1_dram, src_mv, src_rstd, wsum, pos, tile_w, tile_b, to_dram):
    with ExitStack() as ctx:
        def sb(name, shape, dt=F32):
            return ctx.enter_context(nc.sbuf_tensor(name, shape, dt))

        def ps(name, shape, dt=F32):
            return ctx.enter_context(nc.psum_tensor(name, shape, dt))

        w_gate = sb("w_gate", [P, KD, D])
        w_o = sb("w_o", [P, KD, D])
        w_r = sb("w_router", [P, KD, NE])
        gb = sb("gate_b", [P, KD])
        rowsv = sb("rows_n1", [P, 2, D])
        b_r = sb("router_b", [P, NE])
        iota = sb("iotas", [P, NE + TILES + 1])
        oT = sb("attn_t", [P, 2, KD, BLK])
        sig = sb("gate_sig", [P, 2, BLK])
        x1 = sb("x1_block", [P, 3, CPB, D])
        res = sb("attn_res", [P, 3, CPB, D])
        stat = sb("n1_stat", [P, 2, CPB, 6])
        mv = sb("n1_mv", [P, 2, CPB, 2])
        rstd = sb("n1_rstd", [P, 2, CPB])
        xrT = sb("xr_t", [P, 2, 2, KD * P])
        logit = sb("logits", [P, NCH, NE])
        top = sb("top_v", [P, NCH, NE])
        topi = sb("top_i", [P, NCH, NE], U32)
        topf = sb("top_f", [P, NCH, 2])
        sm = sb("route_small", [P, 4, NCH])
        hot = sb("one_hot", [P, NCH, NE])
        rank = sb("rank", [P, NCH, NE])
        cnt = sb("counts", [P, NCH, NE])
        inc = sb("counts_up", [P, NCH, NE])
        exp_ = sb("expert_small", [P, 4, NE])
        tl = sb("tile_small", [P, 2, TILES])
        tbank = [ps(f"o_t{i}", [P, BLK]) for i in range(2)]
        gbank = [ps(f"g_psum{i}", [P, BLK]) for i in range(2)]
        abank = [ps(f"a_psum{i}", [P, BLK]) for i in range(2)]
        lbank = ps("l_psum", [P, NCH, NE])
        rbank = ps("r_psum", [P, 2, NCH, NE])

        wl = None
        for t, n in ((w_gate[:, :, :], "gate_w"), (w_o[:, :, :], "attn_out_w"), (w_r[:, :, :], "router_w"),
                     (gb[:, :], "gate_b"), (rowsv[:, :, :], "n1"), (b_r[:, :], "router_b"), (iota[:, :], "iotas")):
            wl = L.dma(L.act, "gate_load", t, io[n])

        st = {}

        def load(b):
            st["x1", b] = L.dma(L.sp, f"x1_load{b % 3}", x1[:, b % 3, :, :], x1_dram[:, b * CPB:(b + 1) * CPB, :],
                                after=[st.get(("src", b - 3)), L.x1_saved])

        def turn(b):
            for k in range(KD):
                for i in range(CPB):
                    t = L.pe.do(nc.tensor.transpose, tbank[k][:, i * P:(i + 1) * P],
                                attn[:, b * CPB + i, k * P:(k + 1) * P], K["ident"], after=[st.get(("t", k))])
                st["t", k] = st["turned", b, k] = L.act.do(nc.scalar.copy, oT[:, b % 2, k, :], tbank[k][:, :],
                                                           after=[t, st.get(("gated", b - 2))])

        def gate(b):
            for c in range(KD):
                for k in range(KD):
                    m = L.pe.do(nc.tensor.matmul, gbank[c][:, :], w_gate[:, k, c * P:(c + 1) * P], oT[:, b % 2, k, :],
                                start=(k == 0), stop=(k == KD - 1), after=[st["turned", b, k], wl, st.get(("sig", c))])
                st["sig", c] = L.act.do(nc.scalar.activation, sig[:, c, :], gbank[c][:, :], ACT.Sigmoid,
                                        bias=gb[:, c:c + 1], after=[m, st.get(("sigread", c))])
                st["sigread", c] = L.pool.do(nc.gpsimd.tensor_tensor, gT[:, c, b * BLK:(b + 1) * BLK],
                                             oT[:, b % 2, c, :], sig[:, c, :], ALU.mult, after=[st["sig", c]])
            st["gated", b] = st["sigread", c]

        def source(b):
            for i in range(CPB):
                g = b * CPB + i
                st["src", b] = L.dve.do(nc.vector.tensor_scalar, x1[:, b % 3, i, :], x1[:, b % 3, i, :],
                                        src_mv[:, g, 0:1], src_rstd[:, g:g + 1], ALU.subtract, ALU.mult,
                                        after=[st["x1", b]])

        def project(b):
            for half in range(2):
                for i in (2 * half, 2 * half + 1):
                    g = b * CPB + i
                    for k in range(KD):
                        m = L.pe.do(nc.tensor.matmul, abank[half][:, (i % 2) * D:(i % 2 + 1) * D],
                                    gT[:, k, g * P:(g + 1) * P], w_o[:, k, :], start=(k == 0),
                                    stop=(k == KD - 1), skip_group_check=True,
                                    after=[st["gated", b], wl, st.get(("a", half))])
                i = slice(2 * half, 2 * half + 2)
                st["a", half] = L.dve.do(nc.vector.tensor_tensor, res[:, b % 3, i, :], x1[:, b % 3, i, :],
                                         heads(abank[half][:, :], 2, D), ALU.add,
                                         after=[st["src", b], m, st.get(("centered", b - 3))])
            st["src", b] = st["a", half]
            st["stats", b] = stats_of(L, lambda i: res[:, b % 3, i, :], stat[:, b % 2, :, :], mv[:, b % 2, :, :],
                                      rstd[:, b % 2, :], K["power"], CPB, [st["a", half]], [st.get(("xr", b - 2))])

        def norm(b):
            for i in range(CPB):
                c = L.dve.do(nc.vector.scalar_tensor_tensor, res[:, b % 3, i, :], res[:, b % 3, i, :],
                             mv[:, b % 2, i, 0:1], rowsv[:, 0, :], ALU.subtract, ALU.mult, after=[st["stats", b], wl])
                st["xr", b] = L.dve.do(nc.vector.scalar_tensor_tensor, attn[:, b * CPB + i, :], res[:, b % 3, i, :],
                                       rstd[:, b % 2, i:i + 1], rowsv[:, 1, :], ALU.mult, ALU.add,
                                       after=[c, st["turned", b, KD - 1]])
            st["centered", b] = st["xr", b]

        def turn_xr(b):
            for half in range(2):
                for i in range(2):
                    g = b * CPB + 2 * half + i
                    for k in range(KD):
                        t = L.pe.do(nc.tensor.transpose, tbank[half][:, (i * KD + k) * P:(i * KD + k + 1) * P],
                                    attn[:, g, k * P:(k + 1) * P], K["ident"], after=[st["xr", b], st.get(("t", half))])
                st["t", half] = st["xr_t", b, half] = L.act.do(nc.scalar.copy, xrT[:, half, :, :],
                                                               heads(tbank[half][:, :], 2, KD * P),
                                                               after=[t, st.get(("logit", half))])

        def route(b):
            for half in range(2):
                for i in range(2):
                    g = b * CPB + 2 * half + i
                    for k in range(KD):
                        m = L.pe.do(nc.tensor.matmul, lbank[:, g, :], xrT[:, half, i, k * P:(k + 1) * P], w_r[:, k, :],
                                    start=(k == 0), stop=(k == KD - 1), skip_group_check=True,
                                    after=[st["xr_t", b, half], wl])
                st["logit", half] = m

        lags = ((load, 0), (turn, 0), (source, 1), (gate, 1), (project, 2), (norm, 3), (route, 5), (turn_xr, 4))
        for b in range(NBLK + 5):
            for step, lag in lags:
                if 0 <= b - lag < NBLK:
                    step(b - lag)
        m = st["logit", 1]
        v = L.dve.do(nc.vector.tensor_tensor, logit[:, :, :], lbank[:, :, :], over_mid(b_r[:, :], NCH), ALU.add,
                     after=[m])
        for g in range(NCH):
            a = L.dve.do(nc.vector.max, top[:, g, :], logit[:, g, :], after=[v])
        for g in range(NCH):
            a = L.dve.do(nc.vector.max_index, topi[:, g, :], top[:, g, :], logit[:, g, :], after=[a] if g == 0 else [])
        f = L.dve.do(nc.vector.tensor_copy, topf[:, :, :], topi[:, :, 0:2], after=[a])
        ch = L.dve.do(nc.vector.tensor_tensor, sm[:, 0, :], topf[:, :, 0], topf[:, :, 1], ALU.max, after=[f])
        df = L.dve.do(nc.vector.tensor_tensor, sm[:, 1, :], top[:, :, 1], top[:, :, 0], ALU.subtract)
        ex = L.act.do(nc.scalar.activation, sm[:, 1, :], sm[:, 1, :], ACT.Exp, after=[df])
        ad = L.dve.do(nc.vector.tensor_scalar_add, sm[:, 2, :], sm[:, 1, :], 1.0, after=[ex])
        rc = L.dve.do(nc.vector.reciprocal, sm[:, 3, :], sm[:, 2, :], after=[ad])
        sc = L.dve.do(nc.vector.tensor_tensor, sm[:, 1, :], sm[:, 1, :], sm[:, 3, :], ALU.mult, after=[rc])
        L.dve.do(nc.vector.tensor_tensor, wsum[:, :], sm[:, 1, :], sm[:, 3, :], ALU.add, after=[sc])
        h = L.dve.do(nc.vector.tensor_tensor, hot[:, :, :], over_mid(iota[:, 0:NE], NCH), over_last(sm[:, 0, :], NE),
                     ALU.is_equal, after=[ch, wl])
        hf = hot[:, :, :].rearrange("p g e -> p (g e)")
        L.pe.do(nc.tensor.matmul, rbank[:, 0, :, :].rearrange("p g e -> p (g e)"), K["before"], hf, start=True,
                stop=True, skip_group_check=True, after=[h])
        c = L.pe.do(nc.tensor.matmul, rbank[:, 1, :, :].rearrange("p g e -> p (g e)"), K["ones"], hf, start=True,
                    stop=True, skip_group_check=True)
        cc = L.dve.do(nc.vector.tensor_copy, cnt[:, :, :], rbank[:, 1, :, :], after=[c])
        one = L.dve.do(nc.vector.memset, top[:, :, :], 1.0, after=[sc])
        for e in range(NE):
            i = L.dve.do(nc.vector.tensor_tensor_scan, inc[:, :, e], top[:, :, e], cnt[:, :, e], 0.0, ALU.mult, ALU.add,
                         after=[cc, one])
        rk = L.dve.do(nc.vector.tensor_tensor, rank[:, :, :], rbank[:, 0, :, :], inc[:, :, :], ALU.add, after=[i])
        rk = L.dve.do(nc.vector.tensor_tensor, rank[:, :, :], rank[:, :, :], cnt[:, :, :], ALU.subtract, after=[rk])
        q = L.dve.do(nc.vector.tensor_scalar, exp_[:, 0, :], inc[:, NCH - 1, :], P / 2 - 0.5, 1.0 / P, ALU.add,
                     ALU.mult)
        q = L.dve.do(nc.vector.tensor_scalar_add, exp_[:, 0, :], exp_[:, 0, :], 8388608.0, after=[q])
        q = L.dve.do(nc.vector.tensor_scalar_add, exp_[:, 0, :], exp_[:, 0, :], -8388608.0, after=[q])
        q = L.dve.do(nc.vector.tensor_tensor_scan, exp_[:, 1, :], top[:, 0, :], exp_[:, 0, :], 0.0, ALU.mult, ALU.add,
                     after=[q])
        q1 = L.dve.do(nc.vector.tensor_tensor, exp_[:, 2, :], exp_[:, 1, :], exp_[:, 0, :], ALU.subtract, after=[q])
        q1 = L.dve.do(nc.vector.tensor_scalar_mul, exp_[:, 2, :], exp_[:, 2, :], float(P), after=[q1])
        rk = L.dve.do(nc.vector.tensor_tensor, rank[:, :, :], rank[:, :, :], over_mid(exp_[:, 2, :], NCH), ALU.add,
                      after=[q1, rk])
        rk = L.dve.do(nc.vector.tensor_tensor, rank[:, :, :], rank[:, :, :], hot[:, :, :], ALU.mult, after=[rk])
        rk = L.dve.do(nc.vector.tensor_reduce, sm[:, 0, :], rank[:, :, :], AX_X, ALU.add, after=[rk])
        pp = L.dve.do(nc.vector.tensor_copy, pos[:, :], sm[:, 0, :], after=[rk])
        z = L.dve.do(nc.vector.memset, tl[:, 0, :], 0.0)
        for e in range(NE - 1):
            z = L.dve.do(nc.vector.scalar_tensor_tensor, tl[:, 0, :], iota[:, NE:NE + TILES], exp_[:, 1, e:e + 1],
                         tl[:, 0, :], ALU.is_ge, ALU.add, after=[z])
        L.dve.do(nc.vector.tensor_copy, tile_b[:, :], tl[:, 0, :], after=[z])
        z = L.dve.do(nc.vector.tensor_scalar, tl[:, 1, :], tl[:, 0, :], float(P), iota[:, NE + TILES:], ALU.mult,
                     ALU.add, after=[z])
        L.dve.do(nc.vector.tensor_copy, tile_w[:, :], tl[:, 1, :], after=[z])
        for g in range(NCH):
            L.scattered = L.dma(L.pool, "scatter", to_dram, bass.IndirectOffsetOnAxis(ap=pos[:, g:g + 1], axis=0),
                                after=[pp, L.zeroed], start=lambda o, i, s: nc.gpsimd.indirect_dma_start(o, i, s, None),
                                third=attn[:, g, :])
        L.run()


def experts(nc, L, K, io, tile_w, tile_b, to_dram, from_dram):
    RING = 4
    with ExitStack() as ctx:
        def sb(name, shape, dt=F32):
            return ctx.enter_context(nc.sbuf_tensor(name, shape, dt))

        def ps(name, shape, dt=F32):
            return ctx.enter_context(nc.psum_tensor(name, shape, dt))

        W = sb("expert_w", [P, RING, WROW])
        B = sb("expert_b", [P, RING, BROW])
        xg = sb("expert_x", [P, RING, D])
        xT = sb("expert_xt", [P, 2, KD, P])
        hb = sb("expert_h", [P, 2, FF])
        stat = sb("expert_stat", [P, 6])
        mv = sb("expert_mv", [P, 2, 2])
        var = sb("expert_var", [P, 2])
        rstd = sb("expert_rstd", [P, 2])
        gT = sb("expert_g", [P, 2, FT, P])
        sel = sb("expert_out", [P, 2, D])
        tb = [ps(f"e_t{i}", [P, BLK]) for i in range(2)]
        hp = [ps(f"e_h{i}", [P, BLK]) for i in range(2)]
        gp = [ps(f"e_g{i}", [P, BLK]) for i in range(2)]
        op = [ps(f"e_o{i}", [P, BLK]) for i in range(2)]
        st = {}

        def gather(dst, table, index):
            return dict(out=dst, in_=None, third=table, start=lambda o, i, s: nc.gpsimd.indirect_dma_start(
                o, None, s, bass.IndirectOffsetOnAxis(ap=index, axis=0)))

        def fetch(i):
            s = i % RING
            free = [st.get(("done", i - RING)), st.get(("gelu", i - RING)), st.get(("second", i - RING))]
            st["w", i] = L.dma(L.pool, f"expert_w{s}", after=free, **gather(W[:, s, :], io["expert_w"],
                                                                          tile_w[:, i:i + 1]))
            st["b", i] = L.dma(L.pool, f"expert_b{s}", after=free, **gather(B[:, s, :], io["expert_b"],
                                                                          tile_b[:, i:i + 1]))
            st["x", i] = L.dma(L.sp, f"expert_x{s}", xg[:, s, :], to_dram[i * P:(i + 1) * P, :],
                               after=[L.scattered, *free])

        def first(i):
            s, two = i % RING, i % 2
            for k in range(KD):
                t = L.pe.do(nc.tensor.transpose, tb[two][:, k * P:(k + 1) * P], xg[:, s, k * P:(k + 1) * P], K["ident"],
                            after=[st["x", i], st.get(("xt", i - 2))])
            e = L.act.do(nc.scalar.copy, xT[:, two, :, :], heads(tb[two][:, 0:KD * P], KD, P),
                         after=[t, st.get(("h", i - 2))])
            st["xt", i] = e
            for k in range(KD):
                m = L.pe.do(nc.tensor.matmul, hp[two][:, :], xT[:, two, k, :], W[:, s, k * FF:(k + 1) * FF],
                            start=(k == 0), stop=(k == KD - 1), after=[e, st["w", i], st.get(("hb", i - 2))])
            st["h", i] = m
            v = L.dve.do(nc.vector.tensor_tensor, hb[:, two, :], hp[two][:, :], B[:, s, 0:FF], ALU.add,
                         after=[m, st["b", i], st.get(("g", i - 2))])
            st["hb", i] = v
            v = L.dve.do(nc.vector.bn_stats, stat[:, :], hb[:, two, :], after=[v])
            v = L.dve.do(nc.vector.bn_aggr, mv[:, two, :], stat[:, :], after=[v])
            v = L.dve.do(nc.vector.tensor_scalar_add, var[:, two:two + 1], mv[:, two, 1:2], EPS, after=[v])
            r = L.pool.do(nc.gpsimd.tensor_tensor, rstd[:, two:two + 1], var[:, two:two + 1], K["power"], ALU.pow,
                          after=[v])
            st["n", i] = L.dve.do(nc.vector.tensor_scalar, hb[:, two, :], hb[:, two, :], mv[:, two, 0:1],
                                  rstd[:, two:two + 1], ALU.subtract, ALU.mult, after=[r])

        def second(i):
            s, two = i % RING, i % 2
            for c in range(FT):
                t = L.pe.do(nc.tensor.transpose, gp[two][:, c * P:(c + 1) * P], hb[:, two, c * P:(c + 1) * P],
                            K["ident"], after=[st["n", i], st.get(("gelu", i - 2))])
            st["g", i] = t
            o = KD * FF + FT * D
            for c in range(FT):
                e = L.act.do(nc.scalar.activation, gT[:, two, c, :], gp[two][:, c * P:(c + 1) * P], ACT.Gelu,
                             scale=W[:, s, o + c:o + c + 1], bias=W[:, s, o + FT + c:o + FT + c + 1],
                             after=[t, st["w", i], st.get(("second", i - 2))])
            st["gelu", i] = e

        def third(i):
            s, two = i % RING, i % 2
            o = KD * FF
            for c in range(FT):
                m = L.pe.do(nc.tensor.matmul, op[two][:, 0:D], gT[:, two, c, :], W[:, s, o + c * D:o + (c + 1) * D],
                            start=(c == 0), stop=(c == FT - 1), after=[st["gelu", i], st.get(("ob", i - 2))])
            st["second", i] = m
            v = L.dve.do(nc.vector.tensor_tensor, sel[:, two, :], op[two][:, 0:D], B[:, s, FF:FF + D], ALU.add,
                         after=[m, st.get(("saved", i - 2))])
            st["ob", i] = v
            v = L.dve.do(nc.vector.scalar_tensor_tensor, sel[:, two, :], sel[:, two, :], B[:, s, FF + D:], xg[:, s, :],
                         ALU.mult, ALU.add, after=[v])
            st["done", i] = v
            st["saved", i] = L.dma(L.sp, f"expert_save{two}", from_dram[i * P:(i + 1) * P, :], sel[:, two, :],
                                   after=[v])

        for i in range(RING - 2):
            fetch(i)
        for i in range(TILES + 2):
            if i < TILES:
                first(i)
            if 1 <= i <= TILES:
                second(i - 1)
            if 2 <= i:
                third(i - 2)
            if i + RING - 2 < TILES:
                fetch(i + RING - 2)
        L.saved = [st["saved", TILES - 1], st["saved", TILES - 2]]
        L.run()


def finish_tokens(nc, L, K, io, xr, wsum, pos, from_dram, x1_dram, out):
    with ExitStack() as ctx:
        def sb(name, shape, dt=F32):
            return ctx.enter_context(nc.sbuf_tensor(name, shape, dt))

        x1 = sb("x1_final", [P, NCH, D])
        sel = sb("selected", [P, NCH, D])
        rowsv = sb("rows_n2", [P, 2, D])
        stat = sb("f_stat", [P, 2, 2, CPB, 6])
        mv = sb("f_mv", [P, 2, 2, CPB, 2])
        rstd = sb("f_rstd", [P, 2, 2, CPB])
        ov = out.rearrange("b (c p) d -> p (b c) d", p=P)
        wl = L.dma(L.act, "n2_load", rowsv[:, :, :], io["n2"])
        x1l, back = [], []
        for b in range(NBLK):
            c = slice(b * CPB, (b + 1) * CPB)
            x1l.append(L.dma(L.sp, f"x1_final{b}", x1[:, c, :], x1_dram[:, c, :]))
            for g in range(b * CPB, (b + 1) * CPB):
                s = L.dma(L.pool, f"back{b}", sel[:, g, :], None, after=L.saved,
                          start=lambda o, i, s, g=g: nc.gpsimd.indirect_dma_start(
                              o, i, s, bass.IndirectOffsetOnAxis(ap=pos[:, g:g + 1], axis=0)), third=from_dram)
            back.append(s)
        st = {}

        def stats(b, norm, after):
            st["stats", b, norm] = stats_of(L, lambda i: sel[:, b * CPB + i, :], stat[:, b % 2, norm, :, :],
                                            mv[:, b % 2, norm, :, :], rstd[:, b % 2, norm, :], K["power"], CPB,
                                            after, [st.get(("normed", b - 2, norm))])

        def weigh(b):
            for g in range(b * CPB, (b + 1) * CPB):
                v = L.dve.do(nc.vector.scalar_tensor_tensor, sel[:, g, :], sel[:, g, :], wsum[:, g:g + 1], xr[:, g, :],
                             ALU.mult, ALU.add, after=[back[b]])
            stats(b, 0, [v])

        def norm2(b):
            for i in range(CPB):
                row = sel[:, b * CPB + i, :]
                v = L.dve.do(nc.vector.scalar_tensor_tensor, row, row, mv[:, b % 2, 0, i, 0:1], rowsv[:, 0, :],
                             ALU.subtract, ALU.mult, after=[st["stats", b, 0], wl])
                v = L.dve.do(nc.vector.scalar_tensor_tensor, row, row, rstd[:, b % 2, 0, i:i + 1], rowsv[:, 1, :],
                             ALU.mult, ALU.add, after=[v])
            st["normed", b, 0] = v
            stats(b, 1, [v])

        def residual(b):
            for i in range(CPB):
                row = sel[:, b * CPB + i, :]
                v = L.dve.do(nc.vector.tensor_scalar, row, row, mv[:, b % 2, 1, i, 0:1], rstd[:, b % 2, 1, i:i + 1],
                             ALU.subtract, ALU.mult, after=[st["stats", b, 1]])
            st["normed", b, 1] = v
            c = slice(b * CPB, (b + 1) * CPB)
            v = L.pool.do(nc.gpsimd.tensor_tensor, sel[:, c, :], sel[:, c, :], x1[:, c, :], ALU.add,
                          after=[v, x1l[b]])
            st["store"] = L.dma(L.sp, "out_store", ov[:, c, :], sel[:, c, :], after=[v])

        for b in range(NBLK + 2):
            for lag, step in enumerate((weigh, norm2, residual)):
                if 0 <= b - lag < NBLK:
                    step(b - lag)
        s = st["store"]
        L.sp.do(nc.sync.wait_ge, s.sem, s.value)
        L.run()


C_PARTS = [("ident", P), ("flip", P), ("upto", P), ("ones", P), ("before", P), ("over_di", 1), ("mask", BLK),
           ("sel", NH * P), ("negsel", NH * P)]
C_BF16 = ("mask", "sel", "negsel")
C_AT, _at = {}, 0
for _n, _w in C_PARTS:
    C_AT[_n] = (_at, _w)
    _at += _w
C_WIDTH = _at


def constants():
    import numpy as np
    t = {n: np.zeros((P, w), np.float32) for n, w in C_PARTS}
    i = np.arange(P)
    t["ident"][i, i] = 1
    t["flip"][i, P - 1 - i] = 1
    t["upto"][:] = i[:, None] <= i[None, :]
    t["ones"][:] = 1
    t["before"][:] = i[:, None] < i[None, :]
    t["over_di"][:] = 1.0 / DI
    t["mask"][:] = np.tile(np.where(i[:, None] <= i[None, :], 0.0, -1e30), (1, CPB))
    for part in range(3):
        for h in range(NH):
            t["sel"][part * NH + h, h * P:(h + 1) * P] = 1
    t["negsel"][:] = -t["sel"]
    return np.concatenate([t[n] for n, _ in C_PARTS], axis=1)


C_WIDE = sum(w for n, w in C_PARTS if n not in C_BF16)


def load_constants(nc, L, ctx, io):
    cf = ctx.enter_context(nc.sbuf_tensor("const_f32", [P, C_WIDE], F32))
    identb = ctx.enter_context(nc.sbuf_tensor("const_ident_bf16", [P, P], BF16))
    K = {n: cf[:, C_AT[n][0]:C_AT[n][0] + C_AT[n][1]] for n, _ in C_PARTS if n not in C_BF16}
    a = L.dma(L.act, "const_load", cf[:, :], io["consts"][:, 0:C_WIDE])
    L.dve.do(nc.vector.tensor_copy, identb[:, :], K["ident"], after=[a])
    power = ctx.enter_context(nc.sbuf_tensor("minus_half", [P, 1], F32))
    L.dve.do(nc.vector.memset, power[:, :], -0.5)
    K["power"] = power[:, :]
    K["identb"] = identb[:, :]
    return K


def load_scan_constants(nc, L, K, io, cb, stage):
    a = L.dma(L.act, "mask_load", stage[:, :], io["consts"][:, C_WIDE:C_WIDTH])
    for n in C_BF16:
        o, w = C_AT[n]
        o -= C_WIDE
        rows = P if n == "mask" else 3 * NH
        K[n] = cb[0:rows, o:o + w]
        L.act.do(nc.scalar.copy, K[n], stage[0:rows, o:o + w], after=[a])


def build(nc, io, out, upto=9):
    with ExitStack() as ctx:
        L = Lanes(nc, ctx)
        x1_dram = nc.dram_tensor("x1_scratch", (P, NCH, D), F32, kind="Internal").ap()
        to_dram = nc.dram_tensor("expert_rows", (TILES * P, D), F32, kind="Internal").ap()
        from_dram = nc.dram_tensor("expert_results", (TILES * P, D), F32, kind="Internal").ap()

        def sb(scope, name, shape, dt=F32):
            return scope.enter_context(nc.sbuf_tensor(name, shape, dt))

        main = sb(ctx, "tokens", [P, NCH, D])
        turned = sb(ctx, "tokens_t", [P, KD, TOK])
        src_mv = sb(ctx, "src_mv", [P, NCH, 2])
        src_rstd = sb(ctx, "src_rstd", [P, NCH])
        K = load_constants(nc, L, ctx, io)
        zeros = sb(ctx, "zeros", [P, D])
        L.dve.do(nc.vector.memset, zeros[:, :], 0.0)
        with ExitStack() as scan:
            sp = {n: sb(scan, "scan_" + n, [P, 2, NCH * NH]) for n in ("dt", "ecum", "eto", "etot")}
            sp["cumT"] = sb(scan, "scan_cum_t", [3 * NH, 2 * TOK], BF16)
            cb = sb(scan, "const_bf16", [P, C_WIDTH - C_WIDE], BF16)
            w_in = sb(scan, "w_in", [P, KD, 2 * DI + 2 * NST])
            chan = [sb(scan, f"chan{d}", [P, CX * (TAPS + 1) + 2 * CI]) for d in range(2)]
            with nc.sbuf_tensor("const_stage", [P, C_WIDTH - C_WIDE], F32) as stage:
                load_scan_constants(nc, L, K, io, cb, stage)
                norm_and_steps(nc, L, K, io, turned, sp)
                for d in range(2):
                    chan_loaded = L.dma(L.sp, "chan_load", chan[d][:, :], io[f"chan{d}"])
                w_in_loaded = [L.dma(L.sp, "w_in_load0", w_in[:, :, :], io["w_in0"]), None]
                L.run()
            L.zeroed = L.dma(L.act, "zero_rows", to_dram.rearrange("(t p) d -> p t d", p=P),
                             over_mid(zeros[:, :], TILES))
            mamba(nc, L, K, io, turned, sp, w_in, chan, w_in_loaded, chan_loaded, main)
        if upto > 2:
            with ExitStack() as att:
                V = sb(att, "values", [P, NCH, AH, VW])
                residual_and_values(nc, L, K, io, main, turned, V, src_mv, src_rstd, x1_dram)
                if upto > 3:
                    attention(nc, L, K, io, turned, V, main)
        if upto > 4:
            wsum = sb(ctx, "top_sum", [P, NCH])
            pos = sb(ctx, "token_row", [P, NCH], U32)
            tile_w = sb(ctx, "tile_w_row", [P, TILES], U32)
            tile_b = sb(ctx, "tile_b_row", [P, TILES], U32)
            gate_and_route(nc, L, K, io, main, turned, x1_dram, src_mv, src_rstd, wsum, pos, tile_w, tile_b, to_dram)
            if upto > 5:
                experts(nc, L, K, io, tile_w, tile_b, to_dram, from_dram)
                finish_tokens(nc, L, K, io, main, wsum, pos, from_dram, x1_dram, out)
        if upto <= 5:
            s = L.dma(L.sp, "out_store", out.rearrange("b (c p) d -> p (b c) d", p=P), main[:, :, :])
            L.sp.do(nc.sync.wait_ge, s.sem, s.value)
            L.run()


def layout(a):
    import numpy as np
    a = {n.replace("L0_attn_", "").replace("L0_ffn_", ""): np.asarray(v) for n, v in a.items()}

    def kt(w):
        return np.ascontiguousarray(w.reshape(-1, P, w.shape[1]).transpose(1, 0, 2))

    def rows(v):
        return np.ascontiguousarray(np.broadcast_to(v.reshape(1, -1), (P, v.size)))

    def cols(v):
        return v.reshape(-1, P).T

    o = {"x": a["x"], "consts": constants()}
    proj = DI + CX * P
    o["w_dt"] = kt(np.concatenate([a["f_in_w"][proj:].T, a["b_in_w"][proj:].T], axis=1))
    o["dt_bias"] = rows(np.concatenate([a["f_dt_bias"], a["b_dt_bias"]]))
    o["a_log"] = rows(np.concatenate([a["f_A_log"], a["b_A_log"]]))
    for d, f in enumerate("fb"):
        o[f"w_in{d}"] = kt(a[f + "_in_w"][:proj].T)
        o[f"w_out{d}"] = kt(a[f + "_out_w"].T)
        taps = a[f + "_conv_w"].reshape(CX, P, TAPS).transpose(1, 0, 2).reshape(P, CX * TAPS)
        o[f"chan{d}"] = np.concatenate([taps, cols(a[f + "_conv_b"]), cols(np.repeat(a[f + "_Dp"], HP)),
                                        cols(a[f + "_norm_w"])], axis=1)
    o["v_w"] = kt(a["v_w"])
    q = a["q_w"].reshape(KD, P, NG, HG * HD)
    k = a["k_w"].reshape(KD, P, NG, HG * HD)
    o["w_qk"] = np.concatenate([q, k, q], axis=3).transpose(1, 0, 2, 3)
    sc = np.zeros((NG, HG, HD, HG, HD), np.float32)
    for h in range(HG):
        sc[:, h, :, h, :] = a["scale_w"].reshape(NG, HG, HD)[:, h, :, None]
    sc = sc.reshape(NG, HG * HD, HG * HD).transpose(1, 0, 2)
    o["w_sc"] = np.concatenate([sc, sc], axis=0)
    o["gate_w"], o["attn_out_w"], o["router_w"] = kt(a["gate_w"]), kt(a["out_w"]), kt(a["moe_gate_w"])
    o["gate_b"] = cols(a["gate_b"])
    o["n1"] = rows(np.stack([a["n1_g"], a["n1_b"]])).reshape(P, 2, D)
    o["n2"] = rows(np.stack([a["n2_g"], a["n2_b"]])).reshape(P, 2, D)
    o["router_b"] = rows(a["moe_gate_b"])
    o["iotas"] = np.concatenate([np.tile(np.concatenate([np.arange(NE), np.arange(TILES)]), (P, 1)),
                                 np.arange(P)[:, None]], axis=1).astype(np.float32)
    part = lambda w: w.reshape(NE, -1, P, w.shape[-1]).transpose(0, 2, 1, 3).reshape(NE, P, -1)
    o["expert_w"] = np.concatenate([part(a["w1"]), part(a["w2"]), a["ln_g"].reshape(NE, FT, P).transpose(0, 2, 1),
                                    a["ln_b"].reshape(NE, FT, P).transpose(0, 2, 1)], axis=2).reshape(NE * P, WROW)
    o["expert_b"] = np.concatenate([a["b1"], a["b2"], a["res_scale"][:, None]], axis=1)
    return {k: np.ascontiguousarray(v) for k, v in o.items()}


def kernel(**inputs):
    import concourse.bacc as bacc
    from concourse.bass_utils import run_bass_kernel_spmd

    nc = bacc.Bacc("TRN2", target_bir_lowering=False, num_devices=1)
    arrays = layout(inputs)
    io = {n: nc.dram_tensor("in_" + n, v.shape, mybir.dt.from_np(v.dtype), kind="ExternalInput").ap()
          for n, v in arrays.items()}
    out = nc.dram_tensor("out", (BATCH, SEQ, D), F32, kind="ExternalOutput").ap()
    build(nc, io, out)
    r = run_bass_kernel_spmd(nc, [{"in_" + n: v for n, v in arrays.items()}], core_ids=[0])
    return r.results[0]["out"]
```

```python
from contextlib import ExitStack

import concourse.bass as bass
from concourse import mybir
from concourse.alu_op_type import AluOpType as ALU

F32 = mybir.dt.float32
BF16 = mybir.dt.bfloat16
U32 = mybir.dt.uint32
ACT = mybir.ActivationFunctionType
AX_X = mybir.AxisListType.X

P = 128
BATCH, SEQ, D = 2, 2048, 256
TOK = BATCH * SEQ
NCH = TOK // P
KD = D // P
BLK = 512
CPB = BLK // P
NBLK = TOK // BLK
BPS = SEQ // BLK
DI, NST, NH, HP = 512, 64, 8, 64
CI = DI // P
CX = (DI + 2 * NST) // P
TAPS = 4
EPS = 1e-5
AH, HD = 16, 16
NE, FF = 8, 512
FT = FF // P


class Step:

    def __init__(self, lane, emit, after):
        self.lane, self.emit, self.after = lane, emit, after
        self.signals = False
        self.sem = self.value = None
        for s in after:
            s.signals = True


class Lane:

    def __init__(self, engine, sem):
        self.engine, self.sem, self.count = engine, sem, 0
        self.queue, self.seen = [], {}

    def do(self, instruction, *operands, after=(), **options):
        s = Step(self, lambda: instruction(*operands, **options), [a for a in after if a is not None])
        self.queue.append(s)
        return s

    def number(self):
        for s in self.queue:
            if s.sem is None and s.signals:
                self.count += 1
                s.sem, s.value = self.sem, self.count

    def emit(self):
        for s in self.queue:
            for a in s.after:
                if self.seen.get(a.sem.name, 0) < a.value:
                    self.engine.wait_ge(a.sem, a.value)
                    self.seen[a.sem.name] = a.value
            made = s.emit()
            if s.sem is self.sem:
                made.then_inc(self.sem, 1)
            elif s.sem is not None:
                made.then_inc(s.sem, 16)
        self.queue = []


class Lanes:

    def __init__(self, nc, ctx):
        self.nc, self.ctx = nc, ctx
        self.pe = Lane(nc.tensor, ctx.enter_context(nc.semaphore("pe_done")))
        self.act = Lane(nc.scalar, ctx.enter_context(nc.semaphore("act_done")))
        self.dve = Lane(nc.vector, ctx.enter_context(nc.semaphore("dve_done")))
        self.pool = Lane(nc.gpsimd, ctx.enter_context(nc.semaphore("pool_done")))
        self.sp = Lane(nc.sync, ctx.enter_context(nc.semaphore("sp_done")))
        self.arrivals = {}

    def dma(self, lane, name, out, in_, after=(), start=None, **options):
        if name not in self.arrivals:
            self.arrivals[name] = [self.ctx.enter_context(self.nc.semaphore(name)), 0]
        entry = self.arrivals[name]
        entry[1] += 16
        third = (options.pop("third"),) if "third" in options else ()
        s = lane.do(start or lane.engine.dma_start, out, in_, *third, after=after, **options)
        s.sem, s.value = entry[0], entry[1]
        return s

    def run(self):
        lanes = (self.pe, self.act, self.dve, self.pool, self.sp)
        for lane in lanes:
            lane.number()
        with self.nc.Block() as block:
            @block.tensor
            def _(_e):
                self.pe.emit()

            @block.scalar
            def _(_e):
                self.act.emit()

            @block.vector
            def _(_e):
                self.dve.emit()

            @block.gpsimd
            def _(_e):
                self.pool.emit()

            @block.sync
            def _(_e):
                self.sp.emit()


def heads(ap, n, w):
    return ap.rearrange("p (h q) -> p h q", h=n, q=w)


def over_last(ap, w):
    return ap.unsqueeze(2).to_broadcast([ap.shape[0], ap.shape[1], w])


def over_mid(ap, n):
    return ap.unsqueeze(1).to_broadcast([ap.shape[0], n, ap.shape[1]])


def stats_of(L, src, stat, mv, rstd, power, n, after, free=()):
    made = [L.dve.do(L.nc.vector.bn_stats, stat[:, i, :], src(i), after=[*after, *free]) for i in range(n)]
    for i in range(n):
        last = L.dve.do(L.nc.vector.bn_aggr, mv[:, i, :], stat[:, i, :], after=[made[i]])
    biased = L.dve.do(L.nc.vector.tensor_scalar_add, rstd[:, 0:n], mv[:, 0:n, 1], EPS, after=[last])
    return L.pool.do(L.nc.gpsimd.tensor_tensor, rstd[:, 0:n], rstd[:, 0:n], power.to_broadcast([P, n]), ALU.pow,
                     after=[biased])


def norm_and_steps(nc, L, K, io, xnT, sp):
    with ExitStack() as ctx:
        def sb(name, shape, dt=F32):
            return ctx.enter_context(nc.sbuf_tensor(name, shape, dt))

        def ps(name, shape, dt=F32):
            return ctx.enter_context(nc.psum_tensor(name, shape, dt))

        x = sb("x_in", [P, NCH, D])
        xn = sb("x_normed", [P, 2, CPB, D])
        stat = sb("ln_stat", [P, NCH, 6])
        mv = sb("ln_mv", [P, NCH, 2])
        rstd = sb("ln_rstd", [P, NCH])
        wdt = sb("w_dt", [P, KD, 2 * NH])
        dt_bias = sb("dt_bias", [P, 2 * NH])
        a_log = sb("a_log", [P, 2 * NH])
        neg_a = sb("neg_a", [P, 2 * NH])
        raw = sb("dt_raw", [P, 2, NCH * NH])
        tmp = sb("dt_tmp", [P, 2, NCH * NH])
        lg = sb("dt_log", [P, 2, NCH * NH])
        da = sb("dt_a", [P, 2, NCH * NH])
        cum = sb("cum", [P, 2, NCH * NH])
        rest = sb("cum_rest", [P, 2, NCH * NH])
        parts = sb("cum_parts", [P, 2 * NCH, 3, NH], BF16)
        tbank = [ps(f"x_t{i}", [P, BLK]) for i in range(3)]
        dtp = ps("dt_psum", [P, NCH, 2, NH])
        flip = ps("flip_psum", [P, NCH * NH])
        cump = ps("cum_psum", [P, 2, NCH * NH])
        totp = ps("tot_psum", [P, 2, NCH * NH])
        ctp = ps("cum_t_psum", [3 * NH, 8, P], BF16)[:, :, :]

        xv = io["x"].rearrange("b (c p) d -> p (b c) d", p=P)
        loads = [L.dma(L.sp, f"x_load{b}", x[:, b * CPB:(b + 1) * CPB, :], xv[:, b * CPB:(b + 1) * CPB, :])
                 for b in range(NBLK)]
        small = [L.dma(L.act, "dt_load", wdt[:, :, :], io["w_dt"]),
                 L.dma(L.act, "dt_load", dt_bias[:, :], io["dt_bias"]),
                 L.dma(L.act, "dt_load", a_log[:, :], io["a_log"])][-1]

        evac, st = [None] * 3, {}

        def stats(b):
            c = slice(b * CPB, (b + 1) * CPB)
            st["stats", b] = stats_of(L, lambda i: x[:, b * CPB + i, :], stat[:, c, :], mv[:, c, :], rstd[:, c],
                                      K["power"], CPB, [loads[b]])

        def turn(b):
            c0 = b * CPB
            for i in range(CPB):
                nx = L.dve.do(nc.vector.tensor_scalar, xn[:, b % 2, i, :], x[:, c0 + i, :],
                              mv[:, c0 + i, 0:1], rstd[:, c0 + i:c0 + i + 1], ALU.subtract, ALU.mult,
                              after=[st["stats", b], st.get(("turned", b - 2))])
            for k in range(KD):
                bank = (b * KD + k) % 3
                for i in range(CPB):
                    t = L.pe.do(nc.tensor.transpose, tbank[bank][:, i * P:(i + 1) * P],
                                xn[:, b % 2, i, k * P:(k + 1) * P], K["ident"], after=[nx, evac[bank]])
                st["turned", b] = t
                st["x_t", b] = evac[bank] = L.act.do(nc.scalar.copy, xnT[:, k, b * BLK:(b + 1) * BLK],
                                                     tbank[bank][:, :], after=[t])

        def steps_of(b):
            for g in range(b * CPB, (b + 1) * CPB):
                for k in range(KD):
                    st["dt"] = L.pe.do(nc.tensor.matmul, dtp[:, g, :, :].rearrange("p a h -> p (a h)"),
                                       xnT[:, k, g * P:(g + 1) * P], wdt[:, k, :], start=(k == 0),
                                       stop=(k == KD - 1), after=[st["x_t", b], small])

        for b in range(NBLK + 2):
            for lag, step in enumerate((stats, turn, steps_of)):
                if 0 <= b - lag < NBLK:
                    step(b - lag)
        dt_last = st["dt"]
        bias = [dt_bias[:, d * NH:(d + 1) * NH].unsqueeze(1).to_broadcast([P, NCH, NH]) for d in range(2)]
        g3 = lambda t, d: t[:, d, :].rearrange("p (g h) -> p g h", h=NH)
        f0 = L.dve.do(nc.vector.tensor_tensor, g3(raw, 0), dtp[:, :, 0, :], bias[0], ALU.add, after=[dt_last, small])
        f1 = L.dve.do(nc.vector.tensor_tensor, g3(tmp, 1), dtp[:, :, 1, :], bias[1], ALU.add, after=[dt_last])
        fl = L.pe.do(nc.tensor.matmul, flip[:, :], K["flip"], tmp[:, 1, :], start=True, stop=True, after=[f1])
        f2 = L.dve.do(nc.vector.tensor_copy, raw[:, 1, :], flip[:, :], after=[fl])
        a0 = L.dve.do(nc.vector.tensor_scalar_mul, tmp[:, :, :], raw[:, :, :], -1.0, after=[f0, f2])
        a1 = L.dve.do(nc.vector.tensor_tensor, tmp[:, :, :], tmp[:, :, :], raw[:, :, :], ALU.min, after=[a0])
        a2 = L.act.do(nc.scalar.activation, tmp[:, :, :], tmp[:, :, :], ACT.Exp, after=[a1])
        a3 = L.dve.do(nc.vector.tensor_scalar_add, tmp[:, :, :], tmp[:, :, :], 1.0, after=[a2])
        a4 = L.act.do(nc.scalar.activation, lg[:, :, :], tmp[:, :, :], ACT.Ln, after=[a3])
        na = L.act.do(nc.scalar.activation, neg_a[:, :], a_log[:, :], ACT.Exp, after=[small])
        na = L.dve.do(nc.vector.tensor_scalar_mul, neg_a[:, :], neg_a[:, :], -1.0, after=[na])
        a5 = L.dve.do(nc.vector.scalar_tensor_tensor, sp["dt"][:, :, :], raw[:, :, :], 0.0, lg[:, :, :],
                      ALU.max, ALU.add, after=[a4])
        for d in range(2):
            va = L.dve.do(nc.vector.tensor_tensor, g3(da, d), g3(sp["dt"], d),
                          neg_a[:, d * NH:(d + 1) * NH].unsqueeze(1).to_broadcast([P, NCH, NH]), ALU.mult,
                          after=[a5, na])
        flat = lambda t: t[:, :, :].rearrange("p a b -> p (a b)")
        c = L.pe.do(nc.tensor.matmul, flat(cump), K["upto"], flat(da), start=True, stop=True, after=[va])
        t = L.pe.do(nc.tensor.matmul, flat(totp), K["ones"], flat(da), start=True, stop=True, after=[va])
        v0 = L.dve.do(nc.vector.tensor_copy, cum[:, :, :], cump[:, :, :], after=[c])
        v1 = L.dve.do(nc.vector.tensor_tensor, rest[:, :, :], totp[:, :, :], cum[:, :, :], ALU.subtract, after=[v0, t])
        e2 = L.act.do(nc.scalar.activation, sp["eto"][:, :, :], rest[:, :, :], ACT.Exp, after=[v1])
        L.act.do(nc.scalar.activation, sp["etot"][:, :, :], totp[:, :, :], ACT.Exp, after=[v1])
        pt = lambda i: parts[:, :, i, :]
        cg = flat(cum).rearrange("p (g h) -> p g h", h=NH)
        rg = flat(rest).rearrange("p (g h) -> p g h", h=NH)
        s0 = L.dve.do(nc.vector.tensor_copy, pt(0), cg, after=[v0])
        s1 = L.dve.do(nc.vector.tensor_tensor, rg, cg, pt(0), ALU.subtract, after=[s0, e2])
        s2 = L.dve.do(nc.vector.tensor_copy, pt(1), rg, after=[s1])
        s3 = L.dve.do(nc.vector.tensor_tensor, pt(2), rg, pt(1), ALU.subtract, after=[s2])
        turned, read = [ctp, heads(tbank[0][0:3 * NH, :].bitcast(BF16), 8, P)], [None, None]
        for i in range(2 * NCH):
            two = i // 8 % 2
            q = L.pe.do(nc.tensor.transpose, turned[two][:, i % 8, :], parts[:, i, :, :].rearrange("p a h -> p (a h)"),
                        K["identb"], after=[s3, read[two]])
            if i % 8 == 7:
                read[two] = L.dve.do(nc.vector.tensor_copy, heads(sp["cumT"][:, (i - 7) * P:(i + 1) * P], 8, P),
                                     turned[two], after=[q])


def mamba(nc, L, K, io, zeros, to_dram, xnT, sp, w_in, chan, w_in_loaded, chan_loaded, acc):
    with ExitStack() as ctx:
        def sb(name, shape, dt=F32):
            return ctx.enter_context(nc.sbuf_tensor(name, shape, dt))

        def ps(name, shape, dt=F32):
            return ctx.enter_context(nc.psum_tensor(name, shape, dt))

        w_out = [sb(f"w_out{d}", [P, CI, D]) for d in range(2)]
        pre = sb("conv_in", [P, CX, TAPS - 1 + BLK])
        xs = sb("x_conv", [P, 2, CI, BLK])
        bc = sb("bc_conv", [P, BLK])
        BT = sb("b_t", [NST, 2, BLK])
        CT = sb("c_t", [NST, 2, BLK])
        zs = sb("z_gate", [P, 2, CI, BLK])
        ypre = sb("y_pre", [P, 2, CI, P])
        yg = sb("y_gated", [P, 2, CI, P])
        sq = sb("y_squares", [P, 2, CI, P])
        M = sb("decay", [P, 2, NH * P])
        btok = sb("b_tok", [P, 2, NST])
        xdt = sb("x_dt", [P, 2, DI])
        xw = sb("x_w", [P, 2, DI])
        ce = sb("c_decayed", [NST, 2, NH * P])
        S = sb("state", [NST, 2, DI])
        ms = sb("mean_square", [P, 2])
        rrms = sb("rrms", [P, 2])
        rot = [ps(f"rot{i}", [P, BLK]) for i in range(2)]
        Lp = ps("decay_psum", [P, NH * P])
        gb = ps("gb_psum", [P, BLK])
        xt = ps("xt_psum", [P, BLK])
        up = ps("state_psum", [NST, BLK])
        yp = ps("y_psum", [P, BLK])

        wl = []
        for d in range(2):
            wl.append(L.dma(L.sp, f"w_out_load{d}", w_out[d][:, :, :], io[f"w_out{d}"]))
        for k in range(KD):
            L.zeroed = L.dma(L.sp, "zero_rows", to_dram.rearrange("(t p) (k c) -> p t k c", p=P, k=KD)[:, :, k, :],
                             over_mid(zeros[:, :], TILES))
        tap = lambda d, c, i: chan[d][:, c * TAPS + i:c * TAPS + i + 1]
        cbias = lambda d, c: chan[d][:, CX * TAPS + c:CX * TAPS + c + 1]
        o1 = CX * (TAPS + 1)
        dp = lambda d, c: chan[d][:, o1 + c:o1 + c + 1]
        nw = lambda d, c: chan[d][:, o1 + CI + c:o1 + CI + c + 1]
        wscaled = []
        for d in range(2):
            for c in range(CI):
                s = L.dve.do(nc.vector.tensor_scalar_mul, w_out[d][:, c, :], w_out[d][:, c, :], nw(d, c),
                             after=[wl[d], chan_loaded])
            wscaled.append(s)

        blocks = [(d, b, j) for d in range(2) for b in range(BATCH) for j in range(BPS)]
        NB = len(blocks)

        def phys(n):
            d, b, j = blocks[n]
            return b * BPS + (j if d == 0 else BPS - 1 - j)

        def chunk_of(n, j):
            return phys(n) * CPB + (j if blocks[n][0] == 0 else CPB - 1 - j)

        def span(a, width, backward):
            if not backward:
                return slice(a, a + width)
            return slice(a + width - 1, a - 1 if a else None, -1)

        rot_free = [None, None]
        rot_n = [0]

        def next_rot():
            i = rot_n[0] % 2
            rot_n[0] += 1
            return i

        st = {}

        def project(n, tiles):
            d = blocks[n][0]
            sl = n % 2
            a = phys(n) * BLK
            if n == NB // 2 and w_in_loaded[1] is None:
                w_in_loaded[1] = L.dma(L.sp, "w_in_load1", w_in[:, :, :], io["w_in1"], after=[st["proj", n - 1]])
            for c in tiles:
                i = next_rot()
                col = DI + c * P if c < CX else (c - CX) * P
                for k in range(KD):
                    m = L.pe.do(nc.tensor.matmul, rot[i][:, :], w_in[:, k, col:col + P],
                                xnT[:, k, span(a, BLK, d)], start=(k == 0), stop=(k == KD - 1),
                                after=[rot_free[i], w_in_loaded[d]])
                st["proj", n] = m
                if c < CX:
                    e = L.act.do(nc.scalar.copy, pre[:, c, TAPS - 1:], rot[i][:, :],
                                 after=[m, st.get(("halo", n, c))])
                    rot_free[i] = e
                    out = xs[:, sl, c, :] if c < CI else bc[:, :]
                    guard = [st.get(("y", n - 2, CPB - 1)), st.get(("xt", n - 2, CPB - 1)), st.get(("silu", n - 1))]
                    v = L.dve.do(nc.vector.tensor_scalar, out, pre[:, c, TAPS - 1:], tap(d, c, TAPS - 1),
                                 cbias(d, c), ALU.mult, ALU.add, after=[e, chan_loaded, *guard])
                    for t in range(TAPS - 2, -1, -1):
                        v = L.dve.do(nc.vector.scalar_tensor_tensor, out, pre[:, c, t:t + BLK], tap(d, c, t),
                                     out, ALU.mult, ALU.add, after=[v])
                    if n + 1 < NB:
                        if blocks[n + 1][2]:
                            h = L.dve.do(nc.vector.tensor_copy, pre[:, c, 0:TAPS - 1], pre[:, c, BLK:], after=[v])
                        else:
                            h = L.dve.do(nc.vector.memset, pre[:, c, 0:TAPS - 1], 0.0, after=[v])
                        st["halo", n + 1, c] = h
                    st["conv", n, c] = v
                else:
                    lane, copy = (L.dve, nc.vector.tensor_copy) if c == CX + CI - 1 else (L.act, nc.scalar.copy)
                    e = lane.do(copy, zs[:, sl, c - CX, :], rot[i][:, :],
                                after=[m, st.get(("gate", n - 2, CPB - 1))])
                    rot_free[i] = e
                    st["z", n] = e

        def silu_x(n):
            sl = n % 2
            L.act.do(nc.scalar.activation, BT[:, sl, :], bc[0:NST, :], ACT.Silu,
                     after=[st["conv", n, CI], st.get(("g", n - 2, CPB - 1))])
            s = L.act.do(nc.scalar.activation, CT[:, sl, :], bc[NST:P, :], ACT.Silu,
                         after=[st["conv", n, CI], st.get(("ce", n - 2, CPB - 1))])
            st["silu_bc", n] = s
            st["silu", n] = L.act.do(nc.scalar.activation, xs[:, sl, :, :], xs[:, sl, :, :], ACT.Silu,
                                     after=[s, *[st["conv", n, c] for c in range(CI)]])

        def silu_z(n):
            sl = n % 2
            st["silu_z", n] = L.act.do(nc.scalar.activation, zs[:, sl, :, :], zs[:, sl, :, :], ACT.Silu,
                                     after=[st["z", n]])

        def decays_to(n, j):
            d, _, jb = blocks[n]
            g = d * NCH + chunk_of(n, j)
            two = (n * CPB + j) % 2
            before = (n, j - 1) if j else (n - 1, CPB - 1)
            before2 = (n, j - 2) if j >= 2 else (n - 1, CPB - 2 + j)
            for h in range(NH):
                m = L.pe.do(nc.tensor.matmul, Lp[:, h * P:(h + 1) * P], K["sel"][:, h * P:(h + 1) * P],
                            sp["cumT"][:, g * P:(g + 1) * P], start=(h % CPB == 0), stop=False, skip_group_check=True,
                            after=[st.get(("exp", *before))])
            st["to", n, j] = None
            if jb or j:
                st["to", n, j] = L.act.do(nc.scalar.activation, ce[:, two, :], Lp[0:NST, :], ACT.Exp,
                                          after=[m, st.get(("intra", *before2))])

        def decays(n, j):
            g = blocks[n][0] * NCH + chunk_of(n, j)
            two = (n * CPB + j) % 2
            before2 = (n, j - 2) if j >= 2 else (n - 1, CPB - 2 + j)
            for half in range(2):
                bank = Lp[:, half * BLK:(half + 1) * BLK]
                L.pe.do(nc.tensor.matmul, bank, sp["cumT"][:, g * P:(g + 1) * P],
                        K["negsel"][:, half * BLK:(half + 1) * BLK], start=False, stop=False, skip_group_check=True,
                        after=[st["to", n, j]])
                m = L.pe.do(nc.tensor.matmul, bank, K["identb"], K["mask"], start=False, stop=True,
                            skip_group_check=True)
            e = L.act.do(nc.scalar.activation, M[:, two, :], Lp[:, :], ACT.Exp,
                         after=[m, st.get(("intra", *before2))])
            st["exp", n, j] = e

        def products(n, j):
            d = blocks[n][0]
            sl, ch = n % 2, slice(j * P, (j + 1) * P)
            two = (n * CPB + j) % 2
            before = (n, j - 1) if j else (n - 1, CPB - 1)
            before2 = (n, j - 2) if j >= 2 else (n - 1, CPB - 2 + j)
            e = st["exp", n, j]
            free = [st.get(("m", *before)), st.get(("btok", *before))]
            L.pe.do(nc.tensor.matmul, gb[:, 0:P], BT[:, sl, ch], CT[:, sl, ch], start=True, stop=True,
                    after=[st["silu_bc", n], *free])
            gm = L.pe.do(nc.tensor.transpose, gb[:, P:P + NST], BT[:, sl, ch], K["ident"][0:NST, 0:NST])
            st["g", n, j] = gm
            for c in range(CI):
                x = L.pe.do(nc.tensor.transpose, xt[:, c * P:(c + 1) * P], xs[:, sl, c, ch], K["ident"],
                            after=[st["silu", n], st.get(("xdt", *before))])
            st["xt", n, j] = x
            mm = M[:, two, :]
            st["xdt", n, j] = L.dve.do(nc.vector.tensor_tensor, heads(xdt[:, two, :], NH, HP),
                                       heads(xt[:, :], NH, HP), over_last(sp_at("dt", d, n, j), HP), ALU.mult,
                                       after=[x, st.get(("intra", *before2)), st.get(("xw", *before2))])
            st["m", n, j] = L.dve.do(nc.vector.tensor_tensor, heads(mm, NH, P), heads(mm, NH, P),
                                     over_mid(gb[:, 0:P], NH), ALU.mult, after=[gm, e])
            st["btok", n, j] = L.dve.do(nc.vector.tensor_copy, btok[:, two, :], gb[:, P:P + NST],
                                        after=[st.get(("snew", *before2))])
            st["xw", n, j] = L.pool.do(nc.gpsimd.tensor_tensor, heads(xw[:, two, :], NH, HP),
                                       heads(xdt[:, two, :], NH, HP), over_last(sp_at("eto", d, n, j), HP), ALU.mult,
                                       after=[st["xdt", n, j], st.get(("snew", *before2))])
            st["ce", n, j] = st["g", n, j]
            if st["to", n, j]:
                ceh = heads(ce[:, two, :], NH, P)
                st["ce", n, j] = L.pool.do(nc.gpsimd.tensor_tensor, ceh, ceh, over_mid(CT[:, sl, ch], NH), ALU.mult,
                                           after=[st["to", n, j], st["silu_bc", n]])

        def sp_at(what, d, n, j, rows=P):
            g = chunk_of(n, j)
            return sp[what][0:rows, d, g * NH:(g + 1) * NH]

        def across(n, j):
            d, _, jb = blocks[n]
            first = jb == 0 and j == 0
            sl, ch = n % 2, slice(j * P, (j + 1) * P)
            two = (n * CPB + j) % 2
            before = (n, j - 1) if j else (n - 1, CPB - 1)
            before2 = (n, j - 2) if j >= 2 else (n - 1, CPB - 2 + j)
            if not first:
                st["decayed", n, j] = L.pool.do(nc.gpsimd.tensor_tensor, heads(S[:, two, :], NH, HP),
                                                heads(S[:, 1 - two, :], NH, HP),
                                                over_last(sp_at("etot", d, n, j, NST), HP), ALU.mult,
                                                after=[st["sadd", *before], st.get(("intra", *before))])
            for h in range(NH):
                o = HP * (h % 2)
                m = L.pe.do(nc.tensor.matmul, yp[o:o + HP, (h // 2) * P:(h // 2 + 1) * P],
                            xdt[:, two, h * HP:(h + 1) * HP], M[:, two, h * P:(h + 1) * P], start=(h < 2),
                            stop=first, skip_group_check=True,
                            after=[st["m", n, j], st["xdt", n, j], st.get(("y", *before))])
            if not first:
                for h in range(NH):
                    o = HP * (h % 2)
                    m = L.pe.do(nc.tensor.matmul, yp[o:o + HP, (h // 2) * P:(h // 2 + 1) * P],
                                S[:, 1 - two, h * HP:(h + 1) * HP], ce[:, two, h * P:(h + 1) * P], start=False,
                                stop=True, skip_group_check=True, after=[st["sadd", *before], st["ce", n, j]])
            st["intra", n, j] = m
            s = L.pe.do(nc.tensor.matmul, up[:, :], btok[:, two, :], xw[:, two, :], start=True, stop=True,
                        after=[st["btok", n, j], st["xw", n, j], st.get(("sadd", *before))])
            st["snew", n, j] = s
            if first:
                st["sadd", n, j] = L.dve.do(nc.vector.tensor_copy, S[:, two, :], up[:, :],
                                            after=[s, st.get(("intra", *before))])
            else:
                st["sadd", n, j] = L.dve.do(nc.vector.tensor_tensor, S[:, two, :], up[:, :], S[:, two, :], ALU.add,
                                            after=[s, st["decayed", n, j]])
            for c in range(CI):
                y = L.dve.do(nc.vector.scalar_tensor_tensor, ypre[:, two, c, :], xs[:, sl, c, ch], dp(d, c),
                             yp[:, c * P:(c + 1) * P], ALU.mult, ALU.add,
                             after=[m, st.get(("gate", *before2))])
            st["y", n, j] = y
            st["gate", n, j] = L.dve.do(nc.vector.tensor_tensor, yg[:, two, :, :], ypre[:, two, :, span(0, P, d)],
                                        zs[:, sl, :, span(j * P, P, d)], ALU.mult,
                                        after=[y, st["silu_z", n], st.get(("out", *before2)), st.get(("sq", *before2))])
            q = L.pool.do(nc.gpsimd.tensor_tensor, sq[:, two, :, :], yg[:, two, :, :], yg[:, two, :, :], ALU.mult,
                          after=[st["gate", n, j], st.get(("ssum", *before2))])
            q = L.pool.do(nc.gpsimd.tensor_tensor, sq[:, two, 0:2, :], sq[:, two, 0:2, :], sq[:, two, 2:4, :],
                          ALU.add, after=[q])
            st["sq", n, j] = L.pool.do(nc.gpsimd.tensor_tensor, sq[:, two, 0, :], sq[:, two, 0, :],
                                       sq[:, two, 1, :], ALU.add, after=[q])

        def project_out(n, j):
            d = blocks[n][0]
            two = (n * CPB + j) % 2
            before2 = (n, j - 2) if j >= 2 else (n - 1, CPB - 2 + j)
            i = next_rot()
            mean = rot[i][:, 0:1]
            m = L.pe.do(nc.tensor.matmul, mean, sq[:, two, 0, :], K["over_di"], start=True, stop=True,
                        after=[st["sq", n, j], rot_free[i]])
            st["ssum", n, j] = m
            v = L.dve.do(nc.vector.tensor_scalar_add, ms[:, two:two + 1], mean, EPS,
                         after=[m, st.get(("rrms", *before2))])
            rot_free[i] = v
            st["rrms", n, j] = L.pool.do(nc.gpsimd.tensor_tensor, rrms[:, two:two + 1], ms[:, two:two + 1],
                                         K["power"], ALU.pow, after=[v, st.get(("acc", *before2))])
            i = next_rot()
            for c in range(CI):
                m = L.pe.do(nc.tensor.matmul, rot[i][:, 0:D], yg[:, two, c, :], w_out[d][:, c, :],
                            start=(c == 0), stop=(c == CI - 1), after=[rot_free[i], wscaled[d]])
            st["out", n, j] = m
            g = chunk_of(n, j)
            r = rrms[:, two:two + 1]
            if d == 0:
                e = L.act.do(nc.scalar.mul, acc[:, g, :], rot[i][:, 0:D], r, after=[m, st["rrms", n, j]])
                st["acc", g] = e
            else:
                e = L.dve.do(nc.vector.scalar_tensor_tensor, acc[:, g, :], rot[i][:, 0:D], r, acc[:, g, :],
                             ALU.mult, ALU.add, after=[m, st["rrms", n, j], st["acc", g]])
            rot_free[i] = st["acc", n, j] = e

        for c in range(CX):
            st["halo", 0, c] = L.dve.do(nc.vector.memset, pre[:, c, 0:TAPS - 1], 0.0)
        order = [4, 0, 5], [1, 2, 6], [3, 7], [8]
        for part in order:
            project(0, part)
        decays_to(0, 0)
        decays(0, 0)
        silu_x(0)
        silu_z(0)
        products(0, 0)
        decays_to(0, 1)
        chunks = [(n, j) for n in range(NB) for j in range(CPB)]
        for i, (n, j) in enumerate(chunks):
            before, following, second = [chunks[i + o] if 0 <= i + o < len(chunks) else None for o in (-1, 1, 2)]
            last, more = j == CPB - 1, n + 1 < NB
            if following:
                decays(*following)
            if more and last:
                silu_x(n + 1)
            if j and following and not last:
                products(*following)
            if more:
                project(n + 1, order[j][:1])
            if more and last:
                silu_z(n + 1)
            if not j:
                products(*following)
            if before:
                project_out(*before)
            across(n, j)
            if second:
                decays_to(*second)
            if more:
                project(n + 1, order[j][1:])
            if following and last:
                products(*following)
        project_out(*chunks[-1])
        L.run()


def residual_and_values(nc, L, K, io, mixed, srcT, S, V, src_mv, src_rstd, x1_dram):
    with ExitStack() as ctx:
        def sb(name, shape, dt=F32):
            return ctx.enter_context(nc.sbuf_tensor(name, shape, dt))

        def ps(name, shape, dt=F32):
            return ctx.enter_context(nc.psum_tensor(name, shape, dt))

        x = sb("x_again", [P, 3, CPB, D])
        src = sb("src", [P, 2, CPB, D])
        stat = sb("r_stat", [P, 2, CPB, 6])
        mv = sb("r_mv", [P, 2, CPB, 2])
        rstd = sb("r_rstd", [P, 2, CPB])
        stat2 = sb("s_stat", [P, 2, CPB, 6])
        w_v = sb("w_v", [P, KD, D])
        tbank = [ps(f"src_t{i}", [P, BLK]) for i in range(3)]
        vbank = [ps(f"v_psum{i}", [P, BLK]) for i in range(3)]
        S.use([ps(f"split_psum{i}", [P, BLK]) for i in range(2)], (L.dve, nc.vector))

        xv = io["x"].rearrange("b (c p) d -> p (b c) d", p=P)
        wl = L.dma(L.act, "w_v_load", w_v[:, :, :], io["v_w"])
        one = L.pool.do(nc.gpsimd.memset, V[:, :, :, HD:HD + 1], 1.0)
        loads, tevac, vevac, st = [], [None] * 3, [None] * 3, {}

        def load(b):
            loads.append(L.dma(L.sp, f"x_again{b % 3}", x[:, b % 3, :, :], xv[:, b * CPB:(b + 1) * CPB, :],
                               after=[st.get(("x1", b - 3))]))

        def mixed_stats(b):
            st["mixed", b] = stats_of(L, lambda i: mixed[:, b * CPB + i, :], stat[:, b % 2, :, :], mv[:, b % 2, :, :],
                                      rstd[:, b % 2, :], K["power"], CPB, [], [st.get(("normed", b - 2))])

        def residual(b):
            c0 = b * CPB
            for i in range(CPB):
                n = L.dve.do(nc.vector.tensor_scalar, mixed[:, c0 + i, :], mixed[:, c0 + i, :],
                             mv[:, b % 2, i, 0:1], rstd[:, b % 2, i:i + 1], ALU.subtract, ALU.mult,
                             after=[st["mixed", b]])
            st["normed", b] = n
            st["x1", b] = L.pool.do(nc.gpsimd.tensor_tensor, mixed[:, c0:c0 + CPB, :], mixed[:, c0:c0 + CPB, :],
                                    x[:, b % 3, :, :], ALU.add, after=[n, loads[b]])
            L.x1_saved = L.dma(L.sp, "x1_save", x1_dram[:, c0:c0 + CPB, :], mixed[:, c0:c0 + CPB, :],
                               after=[st["x1", b]])

        def src_stats(b):
            c = slice(b * CPB, (b + 1) * CPB)
            st["src_stats", b] = stats_of(L, lambda i: mixed[:, b * CPB + i, :], stat2[:, b % 2, :, :],
                                          src_mv[:, c, :], src_rstd[:, c], K["power"], CPB, [st["x1", b]],
                                          [st.get(("src_stats", b - 2))])

        def turn(b):
            c0 = b * CPB
            for i in range(CPB):
                g = c0 + i
                n = L.dve.do(nc.vector.tensor_scalar, src[:, b % 2, i, :], mixed[:, g, :],
                             src_mv[:, g, 0:1], src_rstd[:, g:g + 1], ALU.subtract, ALU.mult,
                             after=[st["src_stats", b], st.get(("turned", b - 2))])
            for k in range(KD):
                bank = (b * KD + k) % 3
                for i in range(CPB):
                    t = L.pe.do(nc.tensor.transpose, tbank[bank][:, i * P:(i + 1) * P],
                                src[:, b % 2, i, k * P:(k + 1) * P], K["ident"], after=[n, tevac[bank]])
                st["src_t", b] = tevac[bank] = L.act.do(nc.scalar.copy, srcT[:, k, b * BLK:(b + 1) * BLK],
                                                        tbank[bank][:, :], after=[t])
            st["turned", b] = t

        def values(b):
            for g in range(b * CPB, (b + 1) * CPB, 2):
                bank = g // 2 % 3
                for two in range(2):
                    at = slice((g + two) * P, (g + two + 1) * P)
                    for k in range(KD):
                        m = L.pe.do(nc.tensor.matmul, vbank[bank][:, two * D:(two + 1) * D], srcT[:, k, at],
                                    w_v[:, k, :], start=(k == 0), stop=(k == KD - 1), skip_group_check=True,
                                    after=[st["src_t", b], wl, vevac[bank]])
                for two in range(2):
                    vevac[bank] = L.act.do(nc.scalar.copy, V[:, g + two, :, 0:HD],
                                           heads(vbank[bank][:, two * D:(two + 1) * D], AH, HD), after=[m, one])

        due = {}
        for j, start in enumerate((5, 9)):
            rounds = [0, 0, 1] + [1] * PIECES + [2, 3, 4, 4]
            for wait, (_, step) in zip(rounds, S.split(0, j)):
                due.setdefault(start + wait, []).append(step)
        due.setdefault(14, []).extend(step for _, step in S.stack(0))
        for b in range(max(due) + 1):
            for lag, step in enumerate((load, mixed_stats, residual, src_stats, turn, values)):
                at = b if lag == 0 else b - lag + 1
                if 0 <= at < NBLK:
                    step(at)
            for step in due.get(b, []):
                step()
        L.run()


Q_TERMS = (0, 0, 1, 1, 0, 2)
K_TERMS = (0, 1, 0, 1, 2, 0)
ROWS = len(Q_TERMS) * HD
PIECES = 8
MROWS = 3
HG = 4
NG = AH // HG
KT = SEQ // P
VW = HD + 1


class Stacks:

    def __init__(self, nc, L, io, scope, srcT):
        def sb(name, shape, dt=F32):
            return scope.enter_context(nc.sbuf_tensor(name, shape, dt))[:]

        self.nc, self.L, self.srcT, self.st = nc, L, srcT, {}
        self.qs = sb("q_stack", [ROWS + MROWS, 2, HG, SEQ], BF16)
        self.ks = sb("k_stack", [ROWS + MROWS, 2, HG, SEQ], BF16)
        self.w_qk = sb("w_qk", [P, KD, NG, 3 * HG * HD])
        self.w_sc = sb("w_sc", [P, NG, HG * HD])
        self.raw = sb("qk_raw", [P, 2, BLK])
        self.ez = sb("q_scale", [P, BLK])
        self.parts = sb("qk_parts", [P, 2, 3, BLK], BF16)
        self.qk_dram = nc.dram_tensor("qk_rows", (2, P, 3, SEQ), BF16, kind="Internal").ap()
        L.dma(L.act, "w_qk_load", self.w_qk, io["w_qk"])
        self.loaded = L.dma(L.act, "w_qk_load", self.w_sc, io["w_sc"])
        self.groups = [(b, g) for b in range(BATCH) for g in range(NG)]
        ones = sb("ones_row", [MROWS, P], BF16)
        one = L.dve.do(nc.vector.memset, ones, 1.0)
        flat = self.ks[ROWS:, :, :, :].rearrange("p a h c -> p (a h c)")
        self.one = L.dma(L.act, "ones_fill", heads(flat, flat.shape[1] // P, P),
                         over_mid(ones, flat.shape[1] // P), after=[one])

    def use(self, banks, upper):
        self.upper = upper
        self.banks, self.left, self.turn = banks, [None] * len(banks), 0

    def take(self):
        i = self.turn
        self.turn = (i + 1) % len(self.banks)
        return i, self.banks[i], self.left[i]

    def split(self, n, j):
        nc, L, st = self.nc, self.L, self.st
        b, g = self.groups[n]
        w = HG * HD
        blocks = [(2 * j + i, self.raw[:, i, :], self.parts[:, i, :, :], slice(i * w, (i + 1) * w))
                  for i in range(2)]
        (_, x0, _, q0), (_, x1, _, q1) = blocks
        z = self.ez[:, :]

        def project(i):
            s, x, _, _ = blocks[i]
            cols = slice(b * SEQ + s * BLK, b * SEQ + (s + 1) * BLK)
            t, bank, last = self.take()
            for k in range(KD):
                m = L.pe.do(nc.tensor.matmul, bank[:, :], self.w_qk[:, k, g, i * w:(i + 2) * w], self.srcT[:, k, cols],
                            start=(k == 0), stop=(k == KD - 1), after=[self.loaded, last])
            self.left[t] = st["raw", s] = L.act.do(nc.scalar.copy, x, bank[:, :], after=[m, st.get(("rest2", s % 2))])

        def scale():
            t, bank, last = self.take()
            for s, x, _, q in blocks:
                m = L.pe.do(nc.tensor.matmul, bank[q, :], self.w_sc[q, g, :], x[q, :], start=True, stop=True,
                            skip_group_check=True, after=[st["raw", s], last])
            e = L.act.do(nc.scalar.activation, z, bank[:, :], ACT.Exp, scale=-1.0, after=[m, st.get("scaled")])
            self.left[t] = e
            st["ez"] = L.pool.do(nc.gpsimd.tensor_scalar, z, z, HD ** 0.5 / 2, HD ** 0.5 / 2, ALU.mult,
                                    ALU.add, after=[e])

        def invert(c):
            w = BLK // PIECES
            st["inverse"] = L.dve.do(nc.vector.reciprocal, z[:, c * w:(c + 1) * w], z[:, c * w:(c + 1) * w],
                                     after=[st["ez"]])

        def multiply():
            low = L.pool.do(nc.gpsimd.tensor_tensor, x0[q0, :], x0[q0, :], z[q0, :], ALU.mult, after=[st["inverse"]])
            lane, engine = self.upper
            st["scaled"] = lane.do(engine.tensor_tensor, x1[q1, :], x1[q1, :], z[q1, :], ALU.mult,
                                   after=[st["inverse"], low])

        def high():
            for s, x, p, _ in blocks:
                e = L.act.do(nc.scalar.copy, p[:, 0, :], x, after=[st["scaled"], st.get(("saved", (s + 2) % 4))])
                st["rest", s] = L.pool.do(nc.gpsimd.tensor_tensor, x, x, p[:, 0, :], ALU.subtract, after=[e])

        def low():
            for s, x, p, _ in blocks:
                e = L.act.do(nc.scalar.copy, p[:, 1, :], x, after=[st["rest", s]])
                st["rest2", s % 2] = L.pool.do(nc.gpsimd.tensor_tensor, p[:, 2, :], x, p[:, 1, :], ALU.subtract,
                                           after=[e])

        def save():
            for s, _, p, q in blocks:
                k = slice(w - q.start, 2 * w - q.start)
                for row, of in ((0, q), (w, k)):
                    st["saved", s] = L.dma(L.sp, f"parts_save{s}",
                                           self.qk_dram[n % 2, row:row + w, :, s * BLK:(s + 1) * BLK], p[of, :, :],
                                           after=[st["rest2", s % 2], st.get(("stacked", n - 2))])

        return ((0, lambda: project(0)), (2, lambda: project(1)), (4, scale),
                *((6 + 2 * c, lambda c=c: invert(c)) for c in range(PIECES)),
                (5 + 2 * PIECES, multiply), (7 + 2 * PIECES, high), (8 + 2 * PIECES, low), (8 + 2 * PIECES, save))

    def stack(self, n):
        L, st, slot = self.L, self.st, n % 2

        def bring(t):
            saved = [st["saved", s] for s in range(SEQ // BLK)]
            for dst, base, part in ((self.qs, 0, Q_TERMS[t]), (self.ks, HG * HD, K_TERMS[t])):
                rows = self.qk_dram[slot, base:base + HG * HD, part, :].rearrange("(h r) c -> r h c", h=HG)
                st["stacked", n] = L.dma(L.sp, f"stack{slot}", dst[t * HD:(t + 1) * HD, slot, :, :], rows,
                                         after=saved + [st.get(("scored", n - 2))])

        return tuple((t, lambda t=t: bring(t)) for t in range(len(Q_TERMS)))


def attention(nc, L, K, S, V, attn):
    with ExitStack() as ctx:
        def sb(name, shape, dt=F32):
            return ctx.enter_context(nc.sbuf_tensor(name, shape, dt))

        def ps(name, shape, dt=F32):
            return ctx.enter_context(nc.psum_tensor(name, shape, dt))

        qs, ks, groups, st = S.qs, S.ks, S.groups, S.st
        pt = sb("p_exp", [P, 4, 2, BLK])
        mx = sb("max_part", [P, HG * CPB, CPB])
        neg = sb("max_neg", [P, HG * CPB])
        mparts = sb("max_parts", [P, HG * CPB, MROWS], BF16)
        mrow = sb("max_rows", [HG * MROWS, 2, BLK], BF16)
        pvs = sb("pv_out", [P, BLK])
        rden = sb("rden", [P, CPB * HG])
        ebank = [ps(f"score_psum{i}", [P, 2, BLK]) for i in range(2)]
        pv = ps("pv_psum", [P, BLK])
        rbank = [ps(f"round_psum{i}", [P, BLK]) for i in range(3)]

        zero = L.dve.do(nc.vector.memset, pv[:, :], 0.0)

        units = [(n, q) for n in range(len(groups)) for q in range(SEQ // BLK)]
        S.use(rbank, (L.pool, nc.gpsimd))
        take, left = S.take, S.left

        def max_part(u, i, kb):
            n, q = units[u]
            h, c = i // CPB, i % CPB
            at = q * BLK + c * P
            j, bank, last = take()
            m = L.pe.do(nc.tensor.matmul, bank[:, :], qs[0:ROWS, n % 2, h, at:at + P],
                        ks[0:ROWS, n % 2, h, kb * BLK:(kb + 1) * BLK], start=True, stop=True,
                        after=[st["stacked", n], last])
            left[j] = st["maxed", u] = L.dve.do(nc.vector.tensor_reduce, mx[:, c * HG + h, kb:kb + 1], bank[:, :],
                                                AX_X, ALU.max, after=[m, st.get("negated")])

        def max_rows(u):
            n, q = units[u]

            def negate():
                e = L.dve.do(nc.vector.tensor_reduce, neg[:, :], mx[:, :, :], AX_X, ALU.max, negate=True,
                             after=[st["maxed", u], st.get("mparts")])
                st["negated"] = e
                for i in range(MROWS):
                    c = L.pool.do(nc.gpsimd.tensor_copy, mparts[:, :, i], neg[:, :], after=[e, st.get("mturned")])
                    if i < MROWS - 1:
                        e = L.pool.do(nc.gpsimd.tensor_tensor, neg[:, :], neg[:, :], mparts[:, :, i], ALU.subtract,
                                      after=[c])
                st["mparts"] = c

            def turn_rows():
                j, bank, last = take()
                turned = bank[0:HG * MROWS, 0:BLK // 2].bitcast(BF16)
                for i in range(CPB):
                    t = L.pe.do(nc.tensor.transpose, turned[:, i * P:(i + 1) * P],
                                mparts[:, i * HG:(i + 1) * HG, :].rearrange("p h r -> p (h r)"), K["identb"],
                                after=[st["mparts"], last])
                st["mturned"] = t
                e = L.act.do(nc.scalar.copy, mrow[:, u % 2, :], turned[:, :], after=[t, st.get(("mrows", u - 2))])
                left[j] = e
                for h in range(HG):
                    st["mrows", u] = L.dma(L.sp, f"max_row{u % 2}",
                                           qs[ROWS:ROWS + MROWS, n % 2, h, q * BLK:(q + 1) * BLK],
                                           mrow[h * MROWS:(h + 1) * MROWS, u % 2, :], after=[e])

            return (0, negate), (2, turn_rows)

        def score(u, k, pair):
            n, q = units[u]
            i = k * 2 + pair
            for two in range(2):
                h = pair * 2 + two
                m = L.pe.do(nc.tensor.matmul, ebank[pair][:, two, :], ks[:, n % 2, h, k * P:(k + 1) * P],
                            qs[:, n % 2, h, q * BLK:(q + 1) * BLK], start=True, stop=True,
                            after=[st["mrows", u], S.one, st.get(("efree", pair))])
            st["scored", n] = m
            e = L.act.do(nc.scalar.activation, pt[:, i % 4, :, :], ebank[pair][:, :, :], ACT.Exp,
                         after=[m, st.get(("pfree", i % 4))])
            st["efree", pair] = e
            st["exp", u, k, pair] = e

        def weigh(u, k):
            n, q = units[u]
            b, g = groups[n]
            for h in range(HG):
                i = k * 2 + h // 2
                m = L.pe.do(nc.tensor.matmul, pv[h * 32:h * 32 + VW, :], V[:, b * KT + k, g * HG + h, :],
                            pt[:, i % 4, h % 2, :], start=(k == 0), stop=(k == KT - 1), skip_group_check=True,
                            after=[st["exp", u, k, h // 2], zero, st.get("pvfree")])
                st["pfree", i % 4] = m
            if k == KT - 1:
                st["pvfree"] = L.act.do(nc.scalar.copy, pvs[:, :], pv[:, :], after=[m, st.get("pvturned")])

        def finish(u):
            n, q = units[u]
            b, g = groups[n]
            c0 = b * KT + q * CPB

            def turn_out():
                j, bank, last = take()
                for i in range(CPB):
                    t = L.pe.do(nc.tensor.transpose, bank[:, i * P:(i + 1) * P], pvs[:, i * P:(i + 1) * P],
                                K["ident"], after=[st["pvfree"], last])
                st["pvturned"] = t
                o = bank[:, :].rearrange("p (n w) -> p n w", w=32)
                r = L.dve.do(nc.vector.reciprocal, rden[:, :].unsqueeze(2), o[:, :, HD:HD + 1],
                             after=[t, st.get("divided")])
                for i in range(CPB):
                    e = L.dve.do(nc.vector.tensor_tensor,
                                 heads(attn[:, c0 + i, g * HG * HD:(g + 1) * HG * HD], HG, HD),
                                 o[:, i * HG:(i + 1) * HG, 0:HD], over_last(rden[:, i * HG:(i + 1) * HG], HD),
                                 ALU.mult, after=[r])
                left[j] = st["divided"] = e

            return ((0, turn_out),)

        due = {}

        def plan(t, steps):
            for wait, step in steps:
                due.setdefault(t + wait, []).append(step)

        LEAD = KT + 4
        SPLIT = 25
        total = len(units) * KT
        per_group = total // len(groups)
        done = 3 - LEAD
        for n in range(1, len(groups)):
            first = (n - 1) * per_group + 2
            t0 = max(first - 2 * SPLIT, done)
            for j in range(2):
                plan(t0 + SPLIT * j, S.split(n, j))
            done = t0 + 2 * SPLIT
            plan(max(first, done), S.stack(n))
        for u in range(len(units)):
            plan(u * KT - LEAD + KT - 1, max_rows(u))
            plan(u * KT + KT + 2, finish(u))
        for t in range(-LEAD, total + 4):
            scoring, weighing, ahead = 0 <= t < total, 0 < t <= total, 0 <= t + LEAD < total
            u, k = divmod(t, KT)
            mu, mk = divmod(t + LEAD, KT)
            if scoring:
                score(u, k, 0)
            if ahead:
                max_part(mu, mk, 0)
            if scoring:
                score(u, k, 1)
            if ahead:
                max_part(mu, mk, 1)
            if weighing:
                weigh(*divmod(t - 1, KT))
            if ahead:
                max_part(mu, mk, 2)
            if ahead:
                max_part(mu, mk, 3)
            for step in due.get(t, []):
                step()
        L.run()


TILES = NCH + NE - 1
WROW = KD * FF + FT * D + 2 * FT
BROW = FF + D + 1


def gate_and_route(nc, L, K, io, attn, gT, x1_dram, src_mv, src_rstd, wsum, pos, tile_w, tile_b, to_dram):
    with ExitStack() as ctx:
        def sb(name, shape, dt=F32):
            return ctx.enter_context(nc.sbuf_tensor(name, shape, dt))

        def ps(name, shape, dt=F32):
            return ctx.enter_context(nc.psum_tensor(name, shape, dt))

        w_gate = sb("w_gate", [P, KD, D])
        w_o = sb("w_o", [P, KD, D])
        w_r = sb("w_router", [P, KD, NE])
        gb = sb("gate_b", [P, KD])
        rowsv = sb("rows_n1", [P, 2, D])
        b_r = sb("router_b", [P, NE])
        iota = sb("iotas", [P, NE + TILES + 1])
        oT = sb("attn_t", [P, 2, KD, BLK])
        sig = sb("gate_sig", [P, 2, BLK])
        x1 = sb("x1_block", [P, 3, CPB, D])
        res = sb("attn_res", [P, 3, CPB, D])
        stat = sb("n1_stat", [P, 2, CPB, 6])
        mv = sb("n1_mv", [P, 2, CPB, 2])
        rstd = sb("n1_rstd", [P, 2, CPB])
        xrT = sb("xr_t", [P, 2, 2, KD * P])
        logit = sb("logits", [P, NCH, NE])
        top = sb("top_v", [P, NCH, NE])
        topi = sb("top_i", [P, NCH, NE], U32)
        topf = sb("top_f", [P, NCH, 2])
        sm = sb("route_small", [P, 4, NCH])
        hot = sb("one_hot", [P, NCH, NE])
        rank = sb("rank", [P, NCH, NE])
        cnt = sb("counts", [P, NCH, NE])
        inc = sb("counts_up", [P, NCH, NE])
        exp_ = sb("expert_small", [P, 4, NE])
        tl = sb("tile_small", [P, 2, TILES])
        tbank = [ps(f"o_t{i}", [P, BLK]) for i in range(2)]
        gbank = [ps(f"g_psum{i}", [P, BLK]) for i in range(2)]
        abank = [ps(f"a_psum{i}", [P, BLK]) for i in range(2)]
        lbank = [ps(f"l_psum{i}", [P, NCH, NE]) for i in range(2)]

        wl = None
        for t, n in ((w_gate[:, :, :], "gate_w"), (w_o[:, :, :], "attn_out_w"), (w_r[:, :, :], "router_w"),
                     (gb[:, :], "gate_b"), (rowsv[:, :, :], "n1"), (b_r[:, :], "router_b"), (iota[:, :], "iotas")):
            wl = L.dma(L.act, "gate_load", t, io[n])

        st = {}

        def load(b):
            st["x1", b] = L.dma(L.sp, f"x1_load{b % 3}", x1[:, b % 3, :, :], x1_dram[:, b * CPB:(b + 1) * CPB, :],
                                after=[st.get(("src", b - 3)), L.x1_saved])

        def turn(b):
            for k in range(KD):
                for i in range(CPB):
                    t = L.pe.do(nc.tensor.transpose, tbank[k][:, i * P:(i + 1) * P],
                                attn[:, b * CPB + i, k * P:(k + 1) * P], K["ident"], after=[st.get(("t", k))])
                st["t", k] = st["turned", b, k] = L.act.do(nc.scalar.copy, oT[:, b % 2, k, :], tbank[k][:, :],
                                                           after=[t, st.get(("gated", b - 2))])

        def gate(b):
            for c in range(KD):
                for k in range(KD):
                    m = L.pe.do(nc.tensor.matmul, gbank[c][:, :], w_gate[:, k, c * P:(c + 1) * P], oT[:, b % 2, k, :],
                                start=(k == 0), stop=(k == KD - 1), after=[st["turned", b, k], wl, st.get(("sig", c))])
                st["sig", c] = L.act.do(nc.scalar.activation, sig[:, c, :], gbank[c][:, :], ACT.Sigmoid,
                                        bias=gb[:, c:c + 1], after=[m, st.get(("sigread", c))])
                st["sigread", c] = L.pool.do(nc.gpsimd.tensor_tensor, gT[:, c, b * BLK:(b + 1) * BLK],
                                             oT[:, b % 2, c, :], sig[:, c, :], ALU.mult, after=[st["sig", c]])
            st["gated", b] = st["sigread", c]

        def source(b):
            for i in range(CPB):
                g = b * CPB + i
                st["src", b] = L.dve.do(nc.vector.tensor_scalar, x1[:, b % 3, i, :], x1[:, b % 3, i, :],
                                        src_mv[:, g, 0:1], src_rstd[:, g:g + 1], ALU.subtract, ALU.mult,
                                        after=[st["x1", b]])

        def project(b):
            for half in range(2):
                for i in (2 * half, 2 * half + 1):
                    g = b * CPB + i
                    for k in range(KD):
                        m = L.pe.do(nc.tensor.matmul, abank[half][:, (i % 2) * D:(i % 2 + 1) * D],
                                    gT[:, k, g * P:(g + 1) * P], w_o[:, k, :], start=(k == 0),
                                    stop=(k == KD - 1), skip_group_check=True,
                                    after=[st["gated", b], wl, st.get(("a", half))])
                i = slice(2 * half, 2 * half + 2)
                st["a", half] = L.dve.do(nc.vector.tensor_tensor, res[:, b % 3, i, :], x1[:, b % 3, i, :],
                                         heads(abank[half][:, :], 2, D), ALU.add,
                                         after=[st["src", b], m, st.get(("centered", b - 3))])
            st["src", b] = st["a", half]
            st["stats", b] = stats_of(L, lambda i: res[:, b % 3, i, :], stat[:, b % 2, :, :], mv[:, b % 2, :, :],
                                      rstd[:, b % 2, :], K["power"], CPB, [st["a", half]], [st.get(("xr", b - 2))])

        def norm(b):
            for i in range(CPB):
                c = L.dve.do(nc.vector.scalar_tensor_tensor, res[:, b % 3, i, :], res[:, b % 3, i, :],
                             mv[:, b % 2, i, 0:1], rowsv[:, 0, :], ALU.subtract, ALU.mult, after=[st["stats", b], wl])
                st["xr", b] = L.dve.do(nc.vector.scalar_tensor_tensor, attn[:, b * CPB + i, :], res[:, b % 3, i, :],
                                       rstd[:, b % 2, i:i + 1], rowsv[:, 1, :], ALU.mult, ALU.add,
                                       after=[c, st["turned", b, KD - 1]])
            st["centered", b] = st["xr", b]

        def turn_xr(b):
            for half in range(2):
                for i in range(2):
                    g = b * CPB + 2 * half + i
                    for k in range(KD):
                        t = L.pe.do(nc.tensor.transpose, tbank[half][:, (i * KD + k) * P:(i * KD + k + 1) * P],
                                    attn[:, g, k * P:(k + 1) * P], K["ident"], after=[st["xr", b], st.get(("t", half))])
                st["t", half] = st["xr_t", b, half] = L.act.do(nc.scalar.copy, xrT[:, half, :, :],
                                                               heads(tbank[half][:, :], 2, KD * P),
                                                               after=[t, st.get(("logit", half))])

        def route(b):
            for half in range(2):
                for i in range(2):
                    g = b * CPB + 2 * half + i
                    for k in range(KD):
                        m = L.pe.do(nc.tensor.matmul, lbank[b % 2][:, g, :], xrT[:, half, i, k * P:(k + 1) * P],
                                    w_r[:, k, :], start=(k == 0), stop=(k == KD - 1), skip_group_check=True,
                                    after=[st["xr_t", b, half], st.get(("logits", b - 2)), wl])
                st["logit", half] = m
            c = slice(b * CPB, (b + 1) * CPB)
            v = L.dve.do(nc.vector.tensor_tensor, logit[:, c, :], lbank[b % 2][:, c, :], over_mid(b_r[:, :], CPB),
                         ALU.add, after=[m])
            st["logits", b] = v
            for g in range(b * CPB, (b + 1) * CPB):
                a = L.dve.do(nc.vector.max, top[:, g, :], logit[:, g, :], after=[v])
            for g in range(b * CPB, (b + 1) * CPB):
                a = L.dve.do(nc.vector.max_index, topi[:, g, :], top[:, g, :], logit[:, g, :], after=[a])
            st["top"] = a

        lags = ((load, 0), (turn, 0), (source, 1), (gate, 1), (project, 2), (norm, 3), (route, 5), (turn_xr, 4))
        for b in range(NBLK + 5):
            for step, lag in lags:
                if 0 <= b - lag < NBLK:
                    step(b - lag)
        f = L.dve.do(nc.vector.tensor_copy, topf[:, :, :], topi[:, :, 0:2], after=[st["top"]])
        ch = L.dve.do(nc.vector.tensor_tensor, sm[:, 0, :], topf[:, :, 0], topf[:, :, 1], ALU.max, after=[f])
        df = L.dve.do(nc.vector.tensor_tensor, sm[:, 1, :], top[:, :, 1], top[:, :, 0], ALU.subtract)
        ex = L.act.do(nc.scalar.activation, sm[:, 1, :], sm[:, 1, :], ACT.Exp, after=[df])
        ad = L.dve.do(nc.vector.tensor_scalar_add, sm[:, 2, :], sm[:, 1, :], 1.0, after=[ex])
        rc = L.dve.do(nc.vector.reciprocal, sm[:, 3, :], sm[:, 2, :], after=[ad])
        sc = L.dve.do(nc.vector.tensor_tensor, sm[:, 1, :], sm[:, 1, :], sm[:, 3, :], ALU.mult, after=[rc])
        L.dve.do(nc.vector.tensor_tensor, wsum[:, :], sm[:, 1, :], sm[:, 3, :], ALU.add, after=[sc])
        rbank = gbank[0][:, :].rearrange("p (a g e) -> p a g e", a=2, g=NCH)
        h = L.dve.do(nc.vector.tensor_tensor, hot[:, :, :], over_mid(iota[:, 0:NE], NCH), over_last(sm[:, 0, :], NE),
                     ALU.is_equal, after=[ch, wl])
        hf = hot[:, :, :].rearrange("p g e -> p (g e)")
        L.pe.do(nc.tensor.matmul, rbank[:, 0, :, :].rearrange("p g e -> p (g e)"), K["before"], hf, start=True,
                stop=True, skip_group_check=True, after=[h])
        c = L.pe.do(nc.tensor.matmul, rbank[:, 1, :, :].rearrange("p g e -> p (g e)"), K["ones"], hf, start=True,
                    stop=True, skip_group_check=True)
        cc = L.dve.do(nc.vector.tensor_copy, cnt[:, :, :], rbank[:, 1, :, :], after=[c])
        one = L.dve.do(nc.vector.memset, top[:, :, :], 1.0, after=[sc])
        for e in range(NE):
            i = L.dve.do(nc.vector.tensor_tensor_scan, inc[:, :, e], top[:, :, e], cnt[:, :, e], 0.0, ALU.mult, ALU.add,
                         after=[cc, one])
        rk = L.dve.do(nc.vector.tensor_tensor, rank[:, :, :], rbank[:, 0, :, :], inc[:, :, :], ALU.add, after=[i])
        rk = L.dve.do(nc.vector.tensor_tensor, rank[:, :, :], rank[:, :, :], cnt[:, :, :], ALU.subtract, after=[rk])
        q = L.dve.do(nc.vector.tensor_scalar, exp_[:, 0, :], inc[:, NCH - 1, :], P / 2 - 0.5, 1.0 / P, ALU.add,
                     ALU.mult)
        q = L.dve.do(nc.vector.tensor_scalar_add, exp_[:, 0, :], exp_[:, 0, :], 8388608.0, after=[q])
        q = L.dve.do(nc.vector.tensor_scalar_add, exp_[:, 0, :], exp_[:, 0, :], -8388608.0, after=[q])
        q = L.dve.do(nc.vector.tensor_tensor_scan, exp_[:, 1, :], top[:, 0, :], exp_[:, 0, :], 0.0, ALU.mult, ALU.add,
                     after=[q])
        q1 = L.dve.do(nc.vector.tensor_tensor, exp_[:, 2, :], exp_[:, 1, :], exp_[:, 0, :], ALU.subtract, after=[q])
        q1 = L.dve.do(nc.vector.tensor_scalar_mul, exp_[:, 2, :], exp_[:, 2, :], float(P), after=[q1])
        rk = L.dve.do(nc.vector.tensor_tensor, rank[:, :, :], rank[:, :, :], over_mid(exp_[:, 2, :], NCH), ALU.add,
                      after=[q1, rk])
        rk = L.dve.do(nc.vector.tensor_tensor, rank[:, :, :], rank[:, :, :], hot[:, :, :], ALU.mult, after=[rk])
        rk = L.dve.do(nc.vector.tensor_reduce, sm[:, 0, :], rank[:, :, :], AX_X, ALU.add, after=[rk])
        pp = L.dve.do(nc.vector.tensor_copy, pos[:, :], sm[:, 0, :], after=[rk])
        z = L.dve.do(nc.vector.memset, tl[:, 0, :], 0.0)
        for e in range(NE - 1):
            z = L.dve.do(nc.vector.scalar_tensor_tensor, tl[:, 0, :], iota[:, NE:NE + TILES], exp_[:, 1, e:e + 1],
                         tl[:, 0, :], ALU.is_ge, ALU.add, after=[z])
        L.dve.do(nc.vector.tensor_copy, tile_b[:, :], tl[:, 0, :], after=[z])
        z = L.dve.do(nc.vector.tensor_scalar, tl[:, 1, :], tl[:, 0, :], float(P), iota[:, NE + TILES:], ALU.mult,
                     ALU.add, after=[z])
        L.dve.do(nc.vector.tensor_copy, tile_w[:, :], tl[:, 1, :], after=[z])
        for g in range(NCH):
            L.scattered = L.dma(L.pool, "scatter", to_dram, bass.IndirectOffsetOnAxis(ap=pos[:, g:g + 1], axis=0),
                                after=[pp, L.zeroed], start=lambda o, i, s: nc.gpsimd.indirect_dma_start(o, i, s, None),
                                third=attn[:, g, :])
        L.run()


def experts(nc, L, K, io, tile_w, tile_b, to_dram, from_dram):
    RING = 6
    with ExitStack() as ctx:
        def sb(name, shape, dt=F32):
            return ctx.enter_context(nc.sbuf_tensor(name, shape, dt))

        def ps(name, shape, dt=F32):
            return ctx.enter_context(nc.psum_tensor(name, shape, dt))

        W = sb("expert_w", [P, RING, WROW])
        B = sb("expert_b", [P, RING, BROW])
        xg = sb("expert_x", [P, RING, D])
        xT = sb("expert_xt", [P, 2, KD, P])
        hb = sb("expert_h", [P, 2, FF])
        stat = sb("expert_stat", [P, 6])
        mv = sb("expert_mv", [P, 2, 2])
        var = sb("expert_var", [P, 2])
        rstd = sb("expert_rstd", [P, 2])
        gT = sb("expert_g", [P, 2, FT, P])
        sel = sb("expert_out", [P, 2, D])
        tb = [ps(f"e_t{i}", [P, BLK]) for i in range(2)]
        hp = [ps(f"e_h{i}", [P, BLK]) for i in range(2)]
        gp = [ps(f"e_g{i}", [P, BLK]) for i in range(2)]
        op = [ps(f"e_o{i}", [P, BLK]) for i in range(2)]
        st = {}

        def gather(dst, table, index):
            return dict(out=dst, in_=None, third=table, start=lambda o, i, s: nc.gpsimd.indirect_dma_start(
                o, None, s, bass.IndirectOffsetOnAxis(ap=index, axis=0)))

        def fetch(i):
            s = i % RING
            free = [st.get(("done", i - RING)), st.get(("gelu", i - RING)), st.get(("second", i - RING))]
            st["w", i] = L.dma(L.pool, f"expert_w{s}", after=free, **gather(W[:, s, :], io["expert_w"],
                                                                          tile_w[:, i:i + 1]))
            st["b", i] = L.dma(L.pool, f"expert_b{s}", after=free, **gather(B[:, s, :], io["expert_b"],
                                                                          tile_b[:, i:i + 1]))
            st["x", i] = L.dma(L.sp, f"expert_x{s}", xg[:, s, :], to_dram[i * P:(i + 1) * P, :],
                               after=[L.scattered, *free])

        def first(i):
            s, two = i % RING, i % 2
            for k in range(KD):
                t = L.pe.do(nc.tensor.transpose, tb[two][:, k * P:(k + 1) * P], xg[:, s, k * P:(k + 1) * P], K["ident"],
                            after=[st["x", i], st.get(("xt", i - 2))])
            e = L.act.do(nc.scalar.copy, xT[:, two, :, :], heads(tb[two][:, 0:KD * P], KD, P),
                         after=[t, st.get(("h", i - 2))])
            st["xt", i] = e
            for k in range(KD):
                m = L.pe.do(nc.tensor.matmul, hp[two][:, :], xT[:, two, k, :], W[:, s, k * FF:(k + 1) * FF],
                            start=(k == 0), stop=(k == KD - 1), after=[e, st["w", i], st.get(("hb", i - 2))])
            st["h", i] = m
            v = L.dve.do(nc.vector.tensor_tensor, hb[:, two, :], hp[two][:, :], B[:, s, 0:FF], ALU.add,
                         after=[m, st["b", i], st.get(("g", i - 2))])
            st["hb", i] = v
            v = L.dve.do(nc.vector.bn_stats, stat[:, :], hb[:, two, :], after=[v])
            v = L.dve.do(nc.vector.bn_aggr, mv[:, two, :], stat[:, :], after=[v])
            v = L.dve.do(nc.vector.tensor_scalar_add, var[:, two:two + 1], mv[:, two, 1:2], EPS, after=[v])
            r = L.pool.do(nc.gpsimd.tensor_tensor, rstd[:, two:two + 1], var[:, two:two + 1], K["power"], ALU.pow,
                          after=[v])
            st["n", i] = L.dve.do(nc.vector.tensor_scalar, hb[:, two, :], hb[:, two, :], mv[:, two, 0:1],
                                  rstd[:, two:two + 1], ALU.subtract, ALU.mult, after=[r])

        def second(i):
            s, two = i % RING, i % 2
            for c in range(FT):
                t = L.pe.do(nc.tensor.transpose, gp[two][:, c * P:(c + 1) * P], hb[:, two, c * P:(c + 1) * P],
                            K["ident"], after=[st["n", i], st.get(("gelu", i - 2))])
            st["g", i] = t
            o = KD * FF + FT * D
            for c in range(FT):
                e = L.act.do(nc.scalar.activation, gT[:, two, c, :], gp[two][:, c * P:(c + 1) * P], ACT.Gelu,
                             scale=W[:, s, o + c:o + c + 1], bias=W[:, s, o + FT + c:o + FT + c + 1],
                             after=[t, st["w", i], st.get(("second", i - 2))])
            st["gelu", i] = e

        def third(i):
            s, two = i % RING, i % 2
            o = KD * FF
            for c in range(FT):
                m = L.pe.do(nc.tensor.matmul, op[two][:, 0:D], gT[:, two, c, :], W[:, s, o + c * D:o + (c + 1) * D],
                            start=(c == 0), stop=(c == FT - 1), after=[st["gelu", i], st.get(("ob", i - 2))])
            st["second", i] = m
            v = L.dve.do(nc.vector.tensor_tensor, sel[:, two, :], op[two][:, 0:D], B[:, s, FF:FF + D], ALU.add,
                         after=[m, st.get(("saved", i - 2))])
            st["ob", i] = v
            v = L.dve.do(nc.vector.scalar_tensor_tensor, sel[:, two, :], sel[:, two, :], B[:, s, FF + D:], xg[:, s, :],
                         ALU.mult, ALU.add, after=[v])
            st["done", i] = v
            st["saved", i] = L.dma(L.sp, f"expert_save{two}", from_dram[i * P:(i + 1) * P, :], sel[:, two, :],
                                   after=[v])

        for i in range(RING - 2):
            fetch(i)
        for i in range(TILES + 2):
            if i < TILES:
                first(i)
            if 1 <= i <= TILES:
                second(i - 1)
            if 2 <= i:
                third(i - 2)
            if i + RING - 2 < TILES:
                fetch(i + RING - 2)
        L.saved = [st["saved", TILES - 1], st["saved", TILES - 2]]
        L.run()


def finish_tokens(nc, L, K, io, xr, wsum, pos, from_dram, x1_dram, out):
    with ExitStack() as ctx:
        def sb(name, shape, dt=F32):
            return ctx.enter_context(nc.sbuf_tensor(name, shape, dt))

        x1 = sb("x1_final", [P, NCH, D])
        sel = sb("selected", [P, NCH, D])
        rowsv = sb("rows_n2", [P, 2, D])
        stat = sb("f_stat", [P, 2, 2, CPB, 6])
        mv = sb("f_mv", [P, 2, 2, CPB, 2])
        rstd = sb("f_rstd", [P, 2, 2, CPB])
        shift = sb("f_shift", [P, 2, 2, CPB])
        ov = out.rearrange("b (c p) d -> p (b c) d", p=P)
        wl = L.dma(L.act, "n2_load", rowsv[:, :, :], io["n2"])
        x1l, back = [], []
        for b in range(NBLK):
            c = slice(b * CPB, (b + 1) * CPB)
            x1l.append(L.dma(L.sp, f"x1_final{b}", x1[:, c, :], x1_dram[:, c, :]))
            for g in range(b * CPB, (b + 1) * CPB):
                s = L.dma(L.pool, f"back{b}", sel[:, g, :], None, after=L.saved,
                          start=lambda o, i, s, g=g: nc.gpsimd.indirect_dma_start(
                              o, i, s, bass.IndirectOffsetOnAxis(ap=pos[:, g:g + 1], axis=0)), third=from_dram)
            back.append(s)
        st = {}

        def stats(b, norm, after):
            st["stats", b, norm] = stats_of(L, lambda i: sel[:, b * CPB + i, :], stat[:, b % 2, norm, :, :],
                                            mv[:, b % 2, norm, :, :], rstd[:, b % 2, norm, :], K["power"], CPB,
                                            after, [st.get(("normed", b - 2, norm))])

        def weigh(b):
            for g in range(b * CPB, (b + 1) * CPB):
                v = L.dve.do(nc.vector.scalar_tensor_tensor, sel[:, g, :], sel[:, g, :], wsum[:, g:g + 1], xr[:, g, :],
                             ALU.mult, ALU.add, after=[back[b]])
            stats(b, 0, [v])

        def normed(b, norm):
            m = L.dve.do(nc.vector.scalar_tensor_tensor, shift[:, b % 2, norm, :], mv[:, b % 2, norm, :, 0], -1.0,
                         rstd[:, b % 2, norm, :], ALU.mult, ALU.mult,
                         after=[st["stats", b, norm], st.get(("normed", b - 2, norm))])
            for i in range(CPB):
                row = sel[:, b * CPB + i, :]
                v = L.act.do(nc.scalar.activation, row, row, ACT.Identity, bias=shift[:, b % 2, norm, i:i + 1],
                             scale=rstd[:, b % 2, norm, i:i + 1], after=[m])
            st["normed", b, norm] = v
            return v

        def center(b):
            st["centered", b] = normed(b, 0)

        def norm2(b):
            rows = sel[:, b * CPB:(b + 1) * CPB, :]
            v = L.dve.do(nc.vector.tensor_tensor, rows, rows, over_mid(rowsv[:, 0, :], CPB), ALU.mult,
                         after=[st["centered", b], wl])
            st["norm2", b] = L.pool.do(nc.gpsimd.tensor_tensor, rows, rows, over_mid(rowsv[:, 1, :], CPB), ALU.add,
                                       after=[v])

        def norm2_stats(b):
            stats(b, 1, [st["norm2", b]])

        def last_norm(b):
            st["last", b] = normed(b, 1)

        def residual(b):
            c = slice(b * CPB, (b + 1) * CPB)
            v = L.dve.do(nc.vector.tensor_tensor, sel[:, c, :], sel[:, c, :], x1[:, c, :], ALU.add,
                         after=[st["last", b], x1l[b]])
            st["store"] = L.dma(L.sp, "out_store", ov[:, c, :], sel[:, c, :], after=[v])

        lags = ((weigh, 0), (center, 1), (norm2, 2), (norm2_stats, 3), (last_norm, 4), (residual, 5))
        for b in range(NBLK + 5):
            for step, lag in lags:
                if 0 <= b - lag < NBLK:
                    step(b - lag)
        s = st["store"]
        L.sp.do(nc.sync.wait_ge, s.sem, s.value)
        L.run()


C_PARTS = [("ident", P), ("flip", P), ("upto", P), ("ones", P), ("before", P), ("over_di", 1), ("mask", BLK),
           ("sel", NH * P), ("negsel", NH * P)]
C_BF16 = ("mask", "sel", "negsel")
C_AT, _at = {}, 0
for _n, _w in C_PARTS:
    C_AT[_n] = (_at, _w)
    _at += _w
C_WIDTH = _at


def constants():
    import numpy as np
    t = {n: np.zeros((P, w), np.float32) for n, w in C_PARTS}
    i = np.arange(P)
    t["ident"][i, i] = 1
    t["flip"][i, P - 1 - i] = 1
    t["upto"][:] = i[:, None] <= i[None, :]
    t["ones"][:] = 1
    t["before"][:] = i[:, None] < i[None, :]
    t["over_di"][:] = 1.0 / DI
    t["mask"][:] = np.tile(np.where(i[:, None] <= i[None, :], 0.0, -1e30), (1, CPB))
    for part in range(3):
        for h in range(NH):
            t["sel"][part * NH + h, h * P:(h + 1) * P] = 1
    t["negsel"][:] = -t["sel"]
    return np.concatenate([t[n] for n, _ in C_PARTS], axis=1)


C_WIDE = sum(w for n, w in C_PARTS if n not in C_BF16)


def load_constants(nc, L, ctx, io):
    cf = ctx.enter_context(nc.sbuf_tensor("const_f32", [P, C_WIDE], F32))
    identb = ctx.enter_context(nc.sbuf_tensor("const_ident_bf16", [P, P], BF16))
    K = {n: cf[:, C_AT[n][0]:C_AT[n][0] + C_AT[n][1]] for n, _ in C_PARTS if n not in C_BF16}
    a = L.dma(L.act, "const_load", cf[:, :], io["consts"][:, 0:C_WIDE])
    L.dve.do(nc.vector.tensor_copy, identb[:, :], K["ident"], after=[a])
    power = ctx.enter_context(nc.sbuf_tensor("minus_half", [P, 1], F32))
    L.dve.do(nc.vector.memset, power[:, :], -0.5)
    K["power"] = power[:, :]
    K["identb"] = identb[:, :]
    return K


def load_scan_constants(nc, L, K, io, cb, stage):
    a = L.dma(L.act, "mask_load", stage[:, :], io["consts"][:, C_WIDE:C_WIDTH])
    for n in C_BF16:
        o, w = C_AT[n]
        o -= C_WIDE
        rows = P if n == "mask" else 3 * NH
        K[n] = cb[0:rows, o:o + w]
        L.act.do(nc.scalar.copy, K[n], stage[0:rows, o:o + w], after=[a])


def build(nc, io, out):
    with ExitStack() as ctx:
        L = Lanes(nc, ctx)
        x1_dram = nc.dram_tensor("x1_scratch", (P, NCH, D), F32, kind="Internal").ap()
        to_dram = nc.dram_tensor("expert_rows", (TILES * P, D), F32, kind="Internal").ap()
        from_dram = nc.dram_tensor("expert_results", (TILES * P, D), F32, kind="Internal").ap()

        def sb(scope, name, shape, dt=F32):
            return scope.enter_context(nc.sbuf_tensor(name, shape, dt))

        main = sb(ctx, "tokens", [P, NCH, D])
        turned = sb(ctx, "tokens_t", [P, KD, TOK])
        src_mv = sb(ctx, "src_mv", [P, NCH, 2])
        src_rstd = sb(ctx, "src_rstd", [P, NCH])
        K = load_constants(nc, L, ctx, io)
        zeros = sb(ctx, "zeros", [P, P])
        L.dve.do(nc.vector.memset, zeros[:, :], 0.0)
        with ExitStack() as scan:
            sp = {n: sb(scan, "scan_" + n, [P, 2, NCH * NH]) for n in ("dt", "eto", "etot")}
            sp["cumT"] = sb(scan, "scan_cum_t", [3 * NH, 2 * TOK], BF16)
            cb = sb(scan, "const_bf16", [P, C_WIDTH - C_WIDE], BF16)
            w_in = sb(scan, "w_in", [P, KD, 2 * DI + 2 * NST])
            chan = [sb(scan, f"chan{d}", [P, CX * (TAPS + 1) + 2 * CI]) for d in range(2)]
            with nc.sbuf_tensor("const_stage", [P, C_WIDTH - C_WIDE], F32) as stage:
                load_scan_constants(nc, L, K, io, cb, stage)
                norm_and_steps(nc, L, K, io, turned, sp)
                for d in range(2):
                    chan_loaded = L.dma(L.sp, "chan_load", chan[d][:, :], io[f"chan{d}"])
                w_in_loaded = [L.dma(L.sp, "w_in_load0", w_in[:, :, :], io["w_in0"]), None]
                L.run()
            mamba(nc, L, K, io, zeros, to_dram, turned, sp, w_in, chan, w_in_loaded, chan_loaded, main)
        with ExitStack() as att:
            V = sb(att, "values", [P, NCH, AH, VW])
            S = Stacks(nc, L, io, att, turned)
            residual_and_values(nc, L, K, io, main, turned, S, V, src_mv, src_rstd, x1_dram)
            attention(nc, L, K, S, V, main)
        wsum = sb(ctx, "top_sum", [P, NCH])
        pos = sb(ctx, "token_row", [P, NCH], U32)
        tile_w = sb(ctx, "tile_w_row", [P, TILES], U32)
        tile_b = sb(ctx, "tile_b_row", [P, TILES], U32)
        gate_and_route(nc, L, K, io, main, turned, x1_dram, src_mv, src_rstd, wsum, pos, tile_w, tile_b, to_dram)
        experts(nc, L, K, io, tile_w, tile_b, to_dram, from_dram)
        finish_tokens(nc, L, K, io, main, wsum, pos, from_dram, x1_dram, out)


def layout(a):
    import numpy as np
    a = {n.replace("L0_attn_", "").replace("L0_ffn_", ""): np.asarray(v) for n, v in a.items()}

    def kt(w):
        return np.ascontiguousarray(w.reshape(-1, P, w.shape[1]).transpose(1, 0, 2))

    def rows(v):
        return np.ascontiguousarray(np.broadcast_to(v.reshape(1, -1), (P, v.size)))

    def cols(v):
        return v.reshape(-1, P).T

    o = {"x": a["x"], "consts": constants()}
    proj = DI + CX * P
    o["w_dt"] = kt(np.concatenate([a["f_in_w"][proj:].T, a["b_in_w"][proj:].T], axis=1))
    o["dt_bias"] = rows(np.concatenate([a["f_dt_bias"], a["b_dt_bias"]]))
    o["a_log"] = rows(np.concatenate([a["f_A_log"], a["b_A_log"]]))
    for d, f in enumerate("fb"):
        o[f"w_in{d}"] = kt(a[f + "_in_w"][:proj].T)
        o[f"w_out{d}"] = kt(a[f + "_out_w"].T)
        taps = a[f + "_conv_w"].reshape(CX, P, TAPS).transpose(1, 0, 2).reshape(P, CX * TAPS)
        o[f"chan{d}"] = np.concatenate([taps, cols(a[f + "_conv_b"]), cols(np.repeat(a[f + "_Dp"], HP)),
                                        cols(a[f + "_norm_w"])], axis=1)
    o["v_w"] = kt(a["v_w"])
    q = a["q_w"].reshape(KD, P, NG, HG * HD)
    k = a["k_w"].reshape(KD, P, NG, HG * HD)
    o["w_qk"] = np.concatenate([q, k, q], axis=3).transpose(1, 0, 2, 3)
    sc = np.zeros((NG, HG, HD, HG, HD), np.float32)
    for h in range(HG):
        sc[:, h, :, h, :] = a["scale_w"].reshape(NG, HG, HD)[:, h, :, None]
    sc = sc.reshape(NG, HG * HD, HG * HD).transpose(1, 0, 2)
    o["w_sc"] = np.concatenate([sc, sc], axis=0)
    o["gate_w"], o["attn_out_w"], o["router_w"] = kt(a["gate_w"]), kt(a["out_w"]), kt(a["moe_gate_w"])
    o["gate_b"] = cols(a["gate_b"])
    o["n1"] = rows(np.stack([a["n1_g"], a["n1_b"]])).reshape(P, 2, D)
    o["n2"] = rows(np.stack([a["n2_g"], a["n2_b"]])).reshape(P, 2, D)
    o["router_b"] = rows(a["moe_gate_b"])
    o["iotas"] = np.concatenate([np.tile(np.concatenate([np.arange(NE), np.arange(TILES)]), (P, 1)),
                                 np.arange(P)[:, None]], axis=1).astype(np.float32)
    part = lambda w: w.reshape(NE, -1, P, w.shape[-1]).transpose(0, 2, 1, 3).reshape(NE, P, -1)
    o["expert_w"] = np.concatenate([part(a["w1"]), part(a["w2"]), a["ln_g"].reshape(NE, FT, P).transpose(0, 2, 1),
                                    a["ln_b"].reshape(NE, FT, P).transpose(0, 2, 1)], axis=2).reshape(NE * P, WROW)
    o["expert_b"] = np.concatenate([a["b1"], a["b2"], a["res_scale"][:, None]], axis=1)
    return {k: np.ascontiguousarray(v) for k, v in o.items()}


def kernel(**inputs):
    import concourse.bacc as bacc
    from concourse.bass_utils import run_bass_kernel_spmd

    nc = bacc.Bacc("TRN2", target_bir_lowering=False, num_devices=1)
    arrays = layout(inputs)
    io = {n: nc.dram_tensor("in_" + n, v.shape, mybir.dt.from_np(v.dtype), kind="ExternalInput").ap()
          for n, v in arrays.items()}
    out = nc.dram_tensor("out", (BATCH, SEQ, D), F32, kind="ExternalOutput").ap()
    build(nc, io, out)
    r = run_bass_kernel_spmd(nc, [{"in_" + n: v for n, v in arrays.items()}], core_ids=[0])
    return r.results[0]["out"]
```
